# Optimizing a Trainium2 kernel written in Bass

```python
import numpy as np
import jax
import jax.numpy as jnp

def _softmax(x, axis=-1):
    return jax.nn.softmax(x, axis=axis)

def _gelu(x):
    return jax.nn.gelu(x, approximate=True)

def _silu(x):
    return jax.nn.silu(x)

def _sigmoid(x):
    return jax.nn.sigmoid(x)

def _layernorm(x, axis=-1, eps=1e-05):
    m = jnp.mean(x, axis=axis, keepdims=True)
    v = jnp.var(x, axis=axis, keepdims=True)
    return (x - m) / jnp.sqrt(v + eps)

def _scatter_add(tgt, idx, src, axis=0):
    return tgt.at[idx].add(src)

def _segment_sum(src, seg, n):
    return jax.ops.segment_sum(src, seg, n)
kernel_name = 'mk_decoder_preln_d1_seqx_r8_042cc9'

def setup_inputs(seed: int=0):
    np.random.seed(seed)
    _w = jnp.asarray

    def _rec_inputs():
        import jax
        import jax.numpy as jnp
        _rk = jax.random.key(seed)
        x = 7.22e-05 + 1 * jax.random.normal(jax.random.fold_in(_rk, 1), (64, 64, 256), jnp.float32)
        _lenS = 64 - jax.random.randint(jax.random.fold_in(_rk, 7), (64,), 0, max(1, 64 // 4) + 1, jnp.int32)
        _lenS2 = 64 - jax.random.randint(jax.random.fold_in(_rk, 8), (64,), 0, max(1, 64 // 4) + 1, jnp.int32)
        _ctx_2048P = jax.random.normal(jax.random.fold_in(_rk, 11), (64, 16, 256), jnp.float32)
        _ctx_2048c = jax.random.dirichlet(jax.random.fold_in(_rk, 511), 0.3 * jnp.ones((16,), jnp.float32), (64, 64))
        _ctx_2048t = jnp.einsum('bsk,bkd->bsd', _ctx_2048c, _ctx_2048P)
        _ctx_2048t = _ctx_2048t * jax.lax.rsqrt(jnp.mean(jnp.square(_ctx_2048t)) + 1e-12) * 0.953939
        ctx_2048 = 4.13588e-05 + 0.999923 * (_ctx_2048t + 0.3 * jax.random.normal(jax.random.fold_in(_rk, 611), (64, 64, 256), jnp.float32))
        return (x, ctx_2048)
    x, ctx_2048 = _rec_inputs()

    def _L0_attn_setup():
        import jax, jax.numpy as jnp
        import numpy as np
        import math
        HIDDEN = 256
        HEADS = 16
        HEAD_DIM = HIDDEN // HEADS
        SEQ = 256
        BATCH = 1
        THRESH = 0.7
        key = jax.random.key(seed)
        ks = jax.random.split(key, 9)
        init = lambda k, shape: jax.random.normal(k, shape, dtype=jnp.float32) * 0.02
        return {'hidden_states': jax.random.normal(ks[0], (BATCH, SEQ, HIDDEN), dtype=jnp.float32), 'Wq': init(ks[1], (HIDDEN, HIDDEN)), 'bq': jnp.zeros((HIDDEN,), jnp.float32), 'Wk': init(ks[2], (HIDDEN, HIDDEN)), 'bk': jnp.zeros((HIDDEN,), jnp.float32), 'Wv': init(ks[3], (HIDDEN, HIDDEN)), 'bv': jnp.zeros((HIDDEN,), jnp.float32), 'Wo': init(ks[4], (HIDDEN, HIDDEN)), 'bo': jnp.zeros((HIDDEN,), jnp.float32), 'truth_gate': jnp.full((1,), THRESH, jnp.float32), 'balance_gate': jnp.full((1,), THRESH, jnp.float32), 'order_gate': jnp.full((1,), THRESH, jnp.float32), 'justice_gate': jnp.full((1,), THRESH, jnp.float32), 'harmony_gate': jnp.full((1,), THRESH, jnp.float32)}
    _L0_attn_all = _L0_attn_setup()
    _L0_attn_in = {k: v for k, v in _L0_attn_all.items() if k in ('Wq', 'bq', 'Wk', 'bk', 'Wv', 'bv', 'Wo', 'bo', 'truth_gate', 'balance_gate', 'order_gate', 'justice_gate', 'harmony_gate')}
    del _L0_attn_all

    def _L0_xattn_setup():
        import jax, jax.numpy as jnp
        import numpy as np
        N_HEAD = 8
        key = jax.random.key(seed)
        k1, k2, k3 = jax.random.split(key, 3)
        B, D, L = (4, 128, 256)
        q = jax.random.normal(k1, (B, D, L), dtype=jnp.float32)
        k = jax.random.normal(k2, (B, D, L), dtype=jnp.float32)
        v = jax.random.normal(k3, (B, D, L), dtype=jnp.float32)
        gamma = jnp.ones((), dtype=jnp.float32)
        return {'q': q, 'k': k, 'v': v, 'gamma': gamma}
    _L0_xattn_all = _L0_xattn_setup()
    _L0_xattn_in = {k: v for k, v in _L0_xattn_all.items() if k in ('gamma',)}
    del _L0_xattn_all

    def _L0_ffn_setup():
        import jax, jax.numpy as jnp
        import numpy as np
        N_EXPERTS = 8
        TOP_K = 2
        D_MODEL = 256
        D_FF = 128
        BATCH, SEQ = (2, 256)

        def _trunc_normal(key, shape, fan_in):
            std = jnp.sqrt(1.0 / 3.0) / jnp.sqrt(float(fan_in))
            return jax.random.truncated_normal(key, -2.0, 2.0, shape, dtype=jnp.float32) * std
        key = jax.random.key(seed)
        kx, kr, k1, k2, k3 = jax.random.split(key, 5)
        x = jax.random.normal(kx, (BATCH, SEQ, D_MODEL), dtype=jnp.float32)
        router_w = jax.random.uniform(kr, (N_EXPERTS, D_MODEL), dtype=jnp.float32, minval=-1.0, maxval=1.0) / jnp.sqrt(float(D_MODEL))
        w1 = _trunc_normal(k1, (N_EXPERTS, D_MODEL, D_FF), D_MODEL)
        w2 = _trunc_normal(k2, (N_EXPERTS, D_MODEL, D_FF), D_MODEL)
        w3 = _trunc_normal(k3, (N_EXPERTS, D_FF, D_MODEL), D_FF)
        return {'x': x, 'router_w': router_w, 'w1': w1, 'w2': w2, 'w3': w3}
    _L0_ffn_all = _L0_ffn_setup()
    _L0_ffn_in = {k: v for k, v in _L0_ffn_all.items() if k in ('router_w', 'w1', 'w2', 'w3')}
    del _L0_ffn_all
    return {'x': x, 'ctx_2048': ctx_2048, 'L0_attn_Wq': _L0_attn_in['Wq'], 'L0_attn_bq': _L0_attn_in['bq'], 'L0_attn_Wk': _L0_attn_in['Wk'], 'L0_attn_bk': _L0_attn_in['bk'], 'L0_attn_Wv': _L0_attn_in['Wv'], 'L0_attn_bv': _L0_attn_in['bv'], 'L0_attn_Wo': _L0_attn_in['Wo'], 'L0_attn_bo': _L0_attn_in['bo'], 'L0_attn_truth_gate': _L0_attn_in['truth_gate'], 'L0_attn_balance_gate': _L0_attn_in['balance_gate'], 'L0_attn_order_gate': _L0_attn_in['order_gate'], 'L0_attn_justice_gate': _L0_attn_in['justice_gate'], 'L0_attn_harmony_gate': _L0_attn_in['harmony_gate'], 'L0_xattn_gamma': _L0_xattn_in['gamma'], 'L0_ffn_router_w': _L0_ffn_in['router_w'], 'L0_ffn_w1': _L0_ffn_in['w1'], 'L0_ffn_w2': _L0_ffn_in['w2'], 'L0_ffn_w3': _L0_ffn_in['w3']}

def reference(x, ctx_2048, L0_attn_Wq, L0_attn_bq, L0_attn_Wk, L0_attn_bk, L0_attn_Wv, L0_attn_bv, L0_attn_Wo, L0_attn_bo, L0_attn_truth_gate, L0_attn_balance_gate, L0_attn_order_gate, L0_attn_justice_gate, L0_attn_harmony_gate, L0_xattn_gamma, L0_ffn_router_w, L0_ffn_w1, L0_ffn_w2, L0_ffn_w3):
    import jax
    import jax.numpy as jnp

    def _L0_attn_ref(hidden_states, Wq, bq, Wk, bk, Wv, bv, Wo, bo, truth_gate, balance_gate, order_gate, justice_gate, harmony_gate):
        import jax, jax.numpy as jnp
        import numpy as np
        import math
        HIDDEN = 256
        HEADS = 16
        HEAD_DIM = HIDDEN // HEADS
        SEQ = 256
        BATCH = 1
        THRESH = 0.7
        B, S, D = hidden_states.shape
        H, hd = (HEADS, HEAD_DIM)

        def proj(W, b):
            return (hidden_states @ W.T + b).reshape(B, S, H, hd).transpose(0, 2, 1, 3)
        q, k, v = (proj(Wq, bq), proj(Wk, bk), proj(Wv, bv))
        scores = jnp.einsum('bhqd,bhkd->bhqk', q, k) / math.sqrt(hd)
        truth_penalty = jax.nn.sigmoid(truth_gate) * (jnp.linalg.norm(k, axis=-1, keepdims=True) * 0.01)
        logp = jax.nn.log_softmax(scores, axis=-1)
        entropy = -jnp.sum(jnp.exp(logp) * logp, axis=-1, keepdims=True)
        balance_adjustment = jax.nn.sigmoid(balance_gate) * (entropy / math.log(S) * 0.1)
        position_bias = jnp.arange(S, dtype=jnp.float32) / S
        order_bonus = jax.nn.sigmoid(order_gate) * (position_bias * 0.05)
        mean_score = scores.mean(axis=-1, keepdims=True)
        justice_adjustment = jax.nn.sigmoid(justice_gate) * ((mean_score - scores) * 0.1)
        smoothness = -jnp.abs(scores[..., 1:] - scores[..., :-1]).mean(axis=-1, keepdims=True)
        harmony_smooth = jax.nn.sigmoid(harmony_gate) * (smoothness * 0.1)
        scores = scores - truth_penalty + balance_adjustment + order_bonus + justice_adjustment + harmony_smooth
        attn = jax.nn.softmax(scores, axis=-1)
        out = jnp.einsum('bhqk,bhkd->bhqd', attn, v)
        out = out.transpose(0, 2, 1, 3).reshape(B, S, D)
        return out @ Wo.T + bo

    def _L0_xattn_ref(q, k, v, gamma):
        import jax, jax.numpy as jnp
        import numpy as np
        N_HEAD = 8
        B, Dq, Lq = q.shape
        Dv, Lk = (v.shape[-2], v.shape[-1])
        h = N_HEAD
        dq = Dq // h
        dv = Dv // h
        qh = q.reshape(B, h, dq, Lq)
        kh = k.reshape(B, h, dq, Lk)
        vh = v.reshape(B, h, dv, Lk)
        scale = 1.0 / jnp.sqrt(jnp.asarray(dq, dtype=q.dtype))
        qk = jnp.einsum('bhdq,bhdl->bhql', qh, kh) * scale
        sm = jax.nn.softmax(qk, axis=-1)
        ret = jnp.einsum('bhql,bhdl->bhdq', sm, vh)
        ret = ret.reshape(B, Dv, Lq)
        return gamma * ret

    def _L0_ffn_ref(x, router_w, w1, w2, w3):
        import jax, jax.numpy as jnp
        import numpy as np
        N_EXPERTS = 8
        TOP_K = 2
        D_MODEL = 256
        D_FF = 128
        BATCH, SEQ = (2, 256)

        def _trunc_normal(key, shape, fan_in):
            std = jnp.sqrt(1.0 / 3.0) / jnp.sqrt(float(fan_in))
            return jax.random.truncated_normal(key, -2.0, 2.0, shape, dtype=jnp.float32) * std
        B, S, D = x.shape
        xf = x.reshape(-1, D)
        n_tokens = xf.shape[0]
        logits = xf @ router_w.T
        topk_vals, topk_idx = jax.lax.top_k(logits, TOP_K)
        topk_weights = jax.nn.softmax(topk_vals, axis=-1)
        gate = jax.nn.silu(jnp.einsum('nd,edf->enf', xf, w1))
        value = jnp.einsum('nd,edf->enf', xf, w2)
        expert_out = jnp.einsum('enf,efd->end', gate * value, w3)
        tok = jnp.arange(n_tokens)[:, None]
        selected = expert_out[topk_idx, tok]
        out = jnp.sum(selected * topk_weights[..., None], axis=1)
        return out.reshape(B, S, D)
    x = x + _L0_attn_ref(_layernorm(x, axis=-1), L0_attn_Wq, L0_attn_bq, L0_attn_Wk, L0_attn_bk, L0_attn_Wv, L0_attn_bv, L0_attn_Wo, L0_attn_bo, L0_attn_truth_gate, L0_attn_balance_gate, L0_attn_order_gate, L0_attn_justice_gate, L0_attn_harmony_gate)
    x = x + _L0_xattn_ref(_layernorm(x, axis=-1), ctx_2048, ctx_2048, L0_xattn_gamma)
    x = x + _L0_ffn_ref(_layernorm(x, axis=-1), L0_ffn_router_w, L0_ffn_w1, L0_ffn_w2, L0_ffn_w3)
    return x

_drawn_inputs = setup_inputs


def setup_inputs(seed=0):
    import zlib

    import numpy as np

    out = dict(_drawn_inputs(seed))
    spreads = {'L0_attn_bq': (0.0, 0.8),
     'L0_attn_bk': (0.0, 0.8),
     'L0_attn_bv': (0.0, 0.1),
     'L0_attn_bo': (0.0, 0.1)}
    factors = {'L0_attn_Wq': 8.0, 'L0_attn_Wk': 8.0, 'L0_attn_Wv': 3.031}
    for name, (base, spread) in spreads.items():
        noise = np.random.default_rng([zlib.crc32(name.encode()), seed]).standard_normal(out[name].shape)
        drawn = base * np.exp(spread * noise) if base else spread * noise
        out[name] = jnp.asarray(drawn.astype(out[name].dtype))
    for name, factor in factors.items():
        out[name] = (out[name] * factor).astype(out[name].dtype)
    return out
```

```python
import math
from contextlib import ExitStack

import concourse.bass as bass
from concourse import mybir

F32 = mybir.dt.float32
BF16 = mybir.dt.bfloat16
U32 = mybir.dt.uint32
ALU = mybir.AluOpType
ACT = mybir.ActivationFunctionType
AX_X = mybir.AxisListType.X

P = 128
EPS = 1e-5


class Link:

    def __init__(self, eng, sem):
        self.eng, self.sem, self.base, self.n = eng, sem, 0, 0

    def __call__(self, ins):
        ins.then_inc(self.sem, 1)
        self.n += 1
        self.eng.wait_ge(self.sem, self.base + self.n)

    def enter_loop(self):
        self.before = self.n
        self.n = 0

    def at(self, i, per):
        self.base = self.before + i * per

    def leave_loop(self, trips, per):
        assert self.n == per, (self.n, per)
        self.base, self.n = 0, self.before + trips * per


def run_steps(eng, step, first, steady, end, unroll, link=None, per=0):
    lo, hi = steady
    for t in range(first, lo):
        step(t, t % unroll, False, lambda n, off=0, t=t: (t + off) // n)
    trips = (hi - lo) // unroll
    assert lo + trips * unroll == hi
    if link:
        link.enter_loop()
    with eng.Fori(0, trips) as i:
        if link:
            link.at(i, per)
        for s in range(unroll):
            step(i * unroll + (lo + s), (lo + s) % unroll, True,
                 lambda n, off=0, s=s: i * (unroll // n) + (lo + s + off) // n)
    if link:
        link.leave_loop(trips, per)
    for t in range(hi, end):
        step(t, t % unroll, False, lambda n, off=0, t=t: (t + off) // n)


def decoder_kernel(nc, t):
    B, S, D = t["x"].shape
    H, HD = 16, D // 16
    TILES = B * S // P
    ctx = ExitStack()

    def sbt(stack, name, shape, dt=F32):
        return stack.enter_context(nc.sbuf_tensor(name, shape, dt))

    def pst(stack, name, shape, dt=F32):
        return stack.enter_context(nc.psum_tensor(name, shape, dt))

    def sem(stack, name):
        return stack.enter_context(nc.semaphore(name))

    x1_dram = nc.dram_tensor("x1_scratch", [B * S, D], F32, kind="Internal").ap()
    x2_dram = nc.dram_tensor("x2_scratch", [B * S, D], F32, kind="Internal").ap()
    qp_dram = nc.dram_tensor("q_parts", [B, 3, 8, 8, D], BF16, kind="Internal").ap()
    kp_dram = nc.dram_tensor("k_parts", [B, 3, 8, 8, D], BF16, kind="Internal").ap()
    x_in = t["x"].rearrange("b s d -> (b s) d")
    c_in = t["ctx"].rearrange("b s d -> (b s) d")
    out = t["out"].rearrange("b s d -> (b s) d")

    with ctx:
        ident = sbt(ctx, "ident", [P, P])
        ident16 = sbt(ctx, "ident16", [P, P], BF16)
        gamma = sbt(ctx, "gamma", [P, 1])
        w1 = sbt(ctx, "w1", [P, 8, 2, P])
        w2 = sbt(ctx, "w2", [P, 8, 2, P])
        w3 = sbt(ctx, "w3", [P, 8, D])
        rw = sbt(ctx, "rw", [P, 2, 8])
        iota8 = sbt(ctx, "iota8", [P, 8])
        weights_in = sem(ctx, "weights_in")
        ffn_in = sem(ctx, "ffn_in")

        with ExitStack() as st:
            phase1(nc, t, st, sbt, pst, sem, locals())
        with ExitStack() as st:
            phase2(nc, t, st, sbt, pst, sem, locals())
        with ExitStack() as st:
            phase3(nc, t, st, sbt, pst, sem, locals())


def layernorm_scale(nc, link, var, v, rs, tmp, ready, done, count):
    pass


def phase1(nc, t, st, sbt, pst, sem, g):
    TILES, D = g["TILES"], g["D"]
    ident, ident16, gamma = g["ident"], g["ident16"], g["gamma"]
    x_in, c_in, x1_dram, qp_dram, kp_dram = (g[k] for k in ("x_in", "c_in", "x1_dram", "qp_dram", "kp_dram"))
    weights_in, ffn_in = g["weights_in"], g["ffn_in"]

    def sb(name, shape, dt=F32):
        return sbt(st, name, shape, dt)

    def sm(name):
        return sem(st, name)

    wq, wk, wv, wo = (sb(n, [P, 2, D]) for n in ("wq", "wk", "wv", "wo"))
    bq, bk = sb("bq", [P, 2]), sb("bk", [P, 2])
    bv, bo = sb("bv", [P, D]), sb("bo", [P, D])
    gates = sb("gates", [P, 5])
    cst = sb("cst", [P, 11])
    sig = sb("sig", [P, 5])
    coef = sb("coef", [P, 6])
    bkm = sb("bkm", [P, 2, 2])
    x = sb("x_tile", [P, 4, D])
    c = sb("c_tile", [P, 2, D])
    stats = sb("stats", [P, 2, 8])
    ln_s = sb("ln_s", [P, 2, 4])
    xhat = sb("xhat", [P, 2, D])
    hT = sb("hT", [P, 2, 2, 2, 2, 64])
    qT = sb("qT", [P, 2, 2, P])
    kT = sb("kT", [P, 2, 2, 2, 2, 64])
    ksq = sb("ksq", [P, 2, 2, P])
    vblk = sb("vblk", [P, 2, 2, 8, 2, 17])
    s_sb = sb("s_sb", [P, 16, 64])
    dif = sb("dif", [P, 16, 63])
    dd = sb("dd", [P, 16, 64])
    e1 = sb("e1", [P, 16, 64])
    ed = sb("ed", [P, 16, 64])
    e2 = sb("e2", [P, 8, P])
    pT = sb("pT", [P, 8, P])
    rows = sb("rows", [P, 2, 12, 16])
    MX, SUM, ABS, Z, SED, LNZ, KN2, KN, C, W, TA, TB = range(12)
    att = sb("att", [P, D])
    recw = sb("recw", [P, 2, 16])
    aT = sb("aT", [P, 2, P])
    x1 = sb("x1_tile", [P, 2, D])
    stats2 = sb("stats2", [P, 2, 8])
    ln2 = sb("ln2", [P, 2, 4])
    q = sb("q_tile", [P, D])
    r = sb("q_rest", [P, 2, D])
    qp = sb("q_part", [P, 2, 3, D], BF16)
    cr = sb("c_rest", [P, 2, D])
    cp = sb("c_part", [P, 2, 3, D], BF16)

    ps_x = pst(st, "ps_x", [P, 512])
    ps_qk = pst(st, "ps_qk", [P, 4, P])
    ps_v = pst(st, "ps_v", [P, 2, D])
    ps_s = pst(st, "ps_s", [P, 4, 512])
    ps_o = pst(st, "ps_o", [P, 512])

    x_loaded = [sm(f"x_loaded{i}") for i in range(4)]
    c_loaded = [sm(f"c_loaded{i}") for i in range(2)]
    small_in = sm("small_in")
    id_ready, setup_done, sig_done = sm("id_ready"), sm("setup_done"), sm("sig_done")
    zeros_done = sm("zeros_done")
    waits_met = sm("waits_met")
    dve_own, act_own = sm("dve_own"), sm("act_own")
    var1_ready, rs1_ready, var2_ready, rs2_ready = sm("var1_ready"), sm("rs1_ready"), sm("var2_ready"), sm("rs2_ready")
    xhat_ready, xT_done, hT_ready = sm("xhat_ready"), sm("xT_done"), sm("hT_ready")
    qk_done, v_done, qk_ready, v_ready = sm("qk_done"), sm("v_done"), sm("qk_ready"), sm("v_ready")
    kn_done, kn_read = sm("kn_done"), sm("kn_read")
    s_done, s_ready, max_ready, sum_done = sm("s_done"), sm("s_ready"), sm("max_ready"), sm("sum_done")
    dif_ready, d_ready, e1_ready, e2_ready, ed_ready = sm("dif_ready"), sm("d_ready"), sm("e1_ready"), sm("e2_ready"), sm("ed_ready")
    abs_done, z_ready, sed_done = sm("abs_done"), sm("z_ready"), sm("sed_done")
    logs_ready, w_arg, w_ready = sm("logs_ready"), sm("w_arg"), sm("w_ready")
    pT_done, pT_ready, o_done, att_ready = sm("pT_done"), sm("pT_ready"), sm("o_done"), sm("att_ready")
    aT_done, aT_ready, y_done, x1_ready = sm("aT_done"), sm("aT_ready"), sm("y_done"), sm("x1_ready")
    qp_ready = sm("qp_ready")
    c_copied, c_rest, cp_ready = sm("c_copied"), sm("c_rest_ready"), sm("cp_ready")
    x1_stored = [sm(f"x1_stored{i}") for i in range(2)]
    qp_stored = [sm(f"qp_stored{i}") for i in range(2)]
    cp_stored = [sm(f"cp_stored{i}") for i in range(2)]
    N_STEADY = (3, TILES - 1)

    def bc(col, n):
        return col.unsqueeze(2).to_broadcast([P, 16, n])

    block = st.enter_context(nc.Block())

    @block.sync
    def _(sp):
        def load(u, s4, s2):
            row = u * P
            sp.dma_start(x[:, s4, :], x_in[bass.ds(row, P), :]).then_inc(x_loaded[s4], 16)

        sp.dma_start(x[:, 0, :], x_in[0:P, :]).then_inc(x_loaded[0], 16)
        for tile, name in ((ident, "ident"), (cst, "cst")):
            sp.dma_start(tile[:], t[name]).then_inc(small_in, 16)
        for tile, name in ((wq, "wqT"), (wk, "wkT"), (wv, "wvT"), (wo, "woT")):
            sp.dma_start(tile[:], t[name].rearrange("(c p) o -> p c o", p=P)).then_inc(weights_in, 16)
        for tile, name in ((bq, "bq"), (bk, "bk")):
            sp.dma_start(tile[:], t[name].rearrange("(c p) -> p c", p=P), allow_slow_non_contiguous=True).then_inc(small_in, 16)
        for tile, name in ((bv, "bv"), (bo, "bo")):
            a = t[name]
            sp.dma_start(tile[:], bass.AP(a.tensor, a.offset, [[0, P]] + list(a.ap))).then_inc(small_in, 16)
        for i, name in enumerate(("truth", "balance", "order", "justice", "harmony")):
            a = t[name]
            sp.dma_start(gates[:, i:i + 1], bass.AP(a.tensor, a.offset, [[0, P]] + list(a.ap))).then_inc(small_in, 16)
        a = t["gamma"]
        sp.dma_start(gamma[:], bass.AP(a.tensor, a.offset, [[0, P]] + list(a.ap))).then_inc(small_in, 16)
        load(1, 1, 1)
        load(2, 2, 0)
        sp.dma_start(g["iota8"][:], t["iota8"]).then_inc(ffn_in, 16)
        sp.dma_start(g["w1"][:], t["w1"].rearrange("e (c p) f -> p e c f", p=P)).then_inc(ffn_in, 16)
        sp.dma_start(g["w2"][:], t["w2"].rearrange("e (c p) f -> p e c f", p=P)).then_inc(ffn_in, 16)
        sp.dma_start(g["w3"][:], t["w3"].rearrange("e f d -> f e d")).then_inc(ffn_in, 16)
        sp.dma_start(g["rw"][:], t["rwT"].rearrange("(c p) e -> p c e", p=P)).then_inc(ffn_in, 16)

        def step(u, s, steady, over):
            s2 = s % 2
            if steady or 0 <= u < TILES:
                if steady or u >= 2:
                    sp.wait_ge(cp_ready, u - 1)
                sp.dma_start(c[:, s2, :], c_in[bass.ds(u * P, P), :]).then_inc(c_loaded[s2], 16)
            if steady or 0 <= u + 3 < TILES and u >= 0:
                if steady or u >= 1:
                    sp.wait_ge(x1_ready, u)
                load(u + 3, (s + 3) % 4, (s + 1) % 2)
            if steady or 1 <= u <= TILES:
                v, sv = u - 1, (s - 1) % 2
                sp.wait_ge(x1_ready, v + 1)
                sp.dma_start(x1_dram[bass.ds(v * P, P), :], x1[:, sv, :]).then_inc(x1_stored[sv], 16)
                sp.wait_ge(cp_ready, v + 1)
                for bb in range(2):
                    for i in range(3):
                        sp.dma_start(kp_dram[v * 2 + bb, i].rearrange("d h c -> h d c"),
                                     cp[64 * bb:64 * bb + 64, sv, i, :]).then_inc(cp_stored[sv], 16)
                sp.wait_ge(qp_ready, v + 1)
                for bb in range(2):
                    for i in range(3):
                        sp.dma_start(qp_dram[v * 2 + bb, i].rearrange("d h c -> h d c"),
                                     qp[64 * bb:64 * bb + 64, sv, i, :]).then_inc(qp_stored[sv], 16)

        run_steps(sp, step, 0, (4, TILES - 4), TILES + 1, 4)
        for i in range(2):
            sp.wait_ge(x1_stored[i], 16 * (TILES // 2))
            sp.wait_ge(qp_stored[i], 96 * (TILES // 2))
            sp.wait_ge(cp_stored[i], 96 * (TILES // 2))

    @block.tensor
    def _(pe):
        def project(u, s2, steady):
            pe.wait_ge(xhat_ready, u + 1)
            if steady or u >= 1:
                pe.wait_ge(hT_ready, u)
                pe.wait_ge(kn_read, u)
            for kc in range(2):
                last = nc.tensor.transpose(ps_x[:, kc * P:(kc + 1) * P], xhat[:, s2, kc * P:(kc + 1) * P], ident[:])
            last.then_inc(xT_done, 1)
            pe.wait_ge(hT_ready, u + 1)
            if steady or u >= 1:
                pe.wait_ge(qk_ready, u)
            for n, w in enumerate((wq, wk)):
                for m in range(2):
                    for kc in range(2):
                        last = nc.tensor.matmul(ps_qk[:, 2 * n + m, :], w[:, kc, m * P:(m + 1) * P],
                                                hT[:, s2, kc, :, 0, :], start=kc == 0, stop=kc == 1)
            last.then_inc(qk_done, 1)
            if steady or u >= 1:
                pe.wait_ge(v_ready, u)
            for b in range(2):
                for kc in range(2):
                    last = nc.tensor.matmul(ps_v[:, b, :], hT[:, s2, kc, b, :, :], wv[:, kc, :],
                                            start=kc == 0, stop=kc == 1)
            last.then_inc(v_done, 1)

        def finish(u):
            pe.wait_ge(att_ready, u + 1)
            for kc in range(2):
                last = nc.tensor.transpose(ps_o[:, kc * P:(kc + 1) * P], att[:, kc * P:(kc + 1) * P], ident[:])
            last.then_inc(aT_done, 1)
            pe.wait_ge(aT_ready, u + 1)
            for kc in range(2):
                last = nc.tensor.matmul(ps_o[:, 0:D], aT[:, kc, :], wo[:, kc, :], start=kc == 0, stop=kc == 1)
            last.then_inc(y_done, 1)

        def weights(u):
            pe.wait_ge(e2_ready, u + 1)
            for n in range(8):
                last = nc.tensor.transpose(ps_s[:, n // 4, (n % 4) * P:(n % 4 + 1) * P], e2[:, n, :], ident[:])
            last.then_inc(pT_done, 1)

        def times_v(u, s2, steady):
            pe.wait_ge(v_ready, u + 1)
            pe.wait_ge(pT_ready, u + 1)
            if steady or u >= 1:
                pe.wait_ge(x1_ready, u)
            for n in range(8):
                for b in range(2):
                    last = nc.tensor.matmul(ps_o[64 * b:64 * b + 64, n * 34:(n + 1) * 34],
                                            pT[:, n, 64 * b:64 * b + 64], vblk[:, s2, b, n, :, :],
                                            start=True, stop=True)
            last.then_inc(o_done, 1)

        def scores(u, s2, steady):
            pe.wait_ge(qk_ready, u + 1)
            for m in range(2):
                last = nc.tensor.matmul(ps_x[:, 256 + 8 * m:264 + 8 * m], ksq[:, s2, m, :], cst[:, 2:10],
                                        start=True, stop=True)
            last.then_inc(kn_done, 1)
            if steady or u >= 1:
                pe.wait_ge(pT_ready, u)
            for m in range(2):
                for b in range(2):
                    for j in range(4):
                        last = nc.tensor.matmul(ps_s[64 * b:64 * b + 64, j, m * P:(m + 1) * P],
                                                qT[32 * j:32 * j + 32, s2, m, 64 * b:64 * b + 64],
                                                kT[32 * j:32 * j + 32, s2, m, b, :, :], start=True, stop=True)
            last.then_inc(s_done, 1)

        def step(u, s, steady, over):
            if steady or u + 1 < TILES:
                project(u + 1, (s + 1) % 2, steady)
            if steady or 1 <= u <= TILES:
                finish(u - 1)
            if steady or 0 <= u < TILES:
                weights(u)
            if steady or u + 1 < TILES:
                scores(u + 1, (s + 1) % 2, steady)
            if steady or 0 <= u < TILES:
                times_v(u, s % 2, steady)

        pe.wait_ge(small_in, 12 * 16)
        pe.wait_ge(weights_in, 4 * 16)
        run_steps(pe, step, -1, N_STEADY, TILES + 1, 4)

    @block.scalar
    def _(act):
        link = Link(act, act_own)
        act.preload_act_table_set("natural_log_exp_and_others")
        act.wait_ge(small_in, 12 * 16)
        nc.scalar.activation(sig[:], gates[:], ACT.Exp, scale=-1.0).then_inc(sig_done, 1)
        act.wait_ge(setup_done, 1)
        nc.scalar.activation(coef[:, 5:6], coef[:, 5:6], ACT.Exp).then_inc(sig_done, 1)
        act.wait_ge(sig_done, 2)

        def rsqrt(v, ready, u, done):
            act.wait_ge(ready, u + 1)
            link(nc.scalar.activation(v[:, 1:2], v[:, 0:1], ACT.Ln))
            nc.scalar.activation(v[:, 2:3], v[:, 1:2], ACT.Exp, scale=-0.5).then_inc(done, 1)

        def step(u, s, steady, over):
            s2, n2 = s % 2, (s + 1) % 2
            here, ahead, behind = (steady or 0 <= u < TILES), (steady or u + 1 < TILES), (steady or 1 <= u <= TILES)
            if here:
                act.wait_ge(s_done, u + 1)
                if steady or u >= 1:
                    act.wait_ge(dif_ready, u)
                    act.wait_ge(d_ready, u)
                    act.wait_ge(sum_done, u)
                nc.scalar.activation(s_sb[:].rearrange("p (j h) k -> p j (h k)", j=4), ps_s[:, :, 0:256], ACT.Copy,
                                     scale=1.0 / math.sqrt(16)).then_inc(s_ready, 1)
            if behind:
                act.wait_ge(w_arg, u)
                nc.scalar.activation(rows[:, n2, W, :], rows[:, n2, TB, :], ACT.Exp).then_inc(w_ready, 1)
            if ahead:
                rsqrt(ln_s[:, n2, :], var1_ready, u + 1, rs1_ready)
                act.wait_ge(xT_done, u + 2)
                if steady or u >= 1:
                    act.wait_ge(v_done, u)
                for i in range(2):
                    ins = nc.scalar.activation(hT[:, n2, :, :, i, :],
                                               ps_x[:, 0:256].rearrange("p (c b t) -> p c b t", c=2, b=2), ACT.Copy)
                ins.then_inc(hT_ready, 1)
            if here:
                act.wait_ge(d_ready, u + 1)
                if steady or u >= 1:
                    act.wait_ge(ed_ready, u)
                    act.wait_ge(z_ready, u)
                nc.scalar.activation(e1[:], dd[:], ACT.Exp).then_inc(e1_ready, 1)
                if steady or u >= 1:
                    act.wait_ge(pT_done, u)
                nc.scalar.activation(e2[:].rearrange("p n k -> p (n k)"), dd[:].rearrange("p h k -> p (h k)"), ACT.Exp,
                                     scale=coef[:, 4:5]).then_inc(e2_ready, 1)
            if ahead:
                act.wait_ge(qk_done, u + 2)
                if steady or u >= 1:
                    act.wait_ge(s_done, u)
                for m in range(2):
                    nc.scalar.activation(qT[:, n2, m, :], ps_qk[:, m, :], ACT.Identity, bias=bq[:, m:m + 1])
                    for par in range(2):
                        nc.scalar.activation(kT[:, n2, m, :, par, :],
                                             ps_qk[:, 2 + m, :].rearrange("p (b k) -> p b k", b=2), ACT.Identity,
                                             bias=bkm[:, m, par:par + 1], scale=cst[:, par:par + 1])
                    ins = nc.scalar.activation(ksq[:, n2, m, :], ps_qk[:, 2 + m, :], ACT.Square, bias=bk[:, m:m + 1])
                ins.then_inc(qk_ready, 1)
            if behind:
                act.wait_ge(aT_done, u)
                if steady or u >= 2:
                    act.wait_ge(y_done, u - 1)
                nc.scalar.activation(aT[:], ps_o[:, 0:256].rearrange("p (c t) -> p c t", c=2), ACT.Copy).then_inc(aT_ready, 1)
            if here:
                act.wait_ge(pT_done, u + 1)
                if steady or u >= 1:
                    act.wait_ge(o_done, u)
                nc.scalar.activation(pT[:], ps_s[:, 0:2, :].rearrange("p a (n k) -> p (a n) k", k=P), ACT.Copy,
                                     scale=coef[:, 5:6]).then_inc(pT_ready, 1)
                act.wait_ge(c_loaded[s2], (u // 2 + 1) * 16 if not steady else (u - s2) * 8 + 16)
                if steady or u >= 2:
                    act.wait_ge(cp_stored[s2], (u // 2) * 96 if not steady else (u - s2) * 48)
                nc.scalar.activation(cp[:, s2, 0, :], c[:, s2, :], ACT.Copy).then_inc(c_copied, 1)
                act.wait_ge(z_ready, u + 1)
                link(nc.scalar.activation(rows[:, s2, LNZ, :], rows[:, s2, Z, :], ACT.Ln))
                act.wait_ge(kn_read, u + 1)
                link(nc.scalar.activation(rows[:, s2, KN, :], rows[:, s2, KN2, :], ACT.Ln))
                nc.scalar.activation(rows[:, s2, KN, :], rows[:, s2, KN, :], ACT.Exp, scale=0.5).then_inc(logs_ready, 1)
                act.wait_ge(c_rest, 2 * u + 1)
                nc.scalar.activation(cp[:, s2, 1, :], cr[:, 0, :], ACT.Copy).then_inc(c_copied, 1)
            if behind:
                rsqrt(ln2[:, n2, :], var2_ready, u - 1, rs2_ready)
            if here:
                act.wait_ge(c_rest, 2 * u + 2)
                nc.scalar.activation(cp[:, s2, 2, :], cr[:, 1, :], ACT.Copy).then_inc(cp_ready, 1)

        run_steps(act, step, -1, N_STEADY, TILES + 1, 4, link, 4 * 4)

    @block.gpsimd
    def _(pool):
        def step(u, s, steady, over):
            s2 = s % 2
            pool.wait_ge(s_ready, u + 1)
            if steady or u >= 1:
                pool.wait_ge(abs_done, u)
            nc.gpsimd.tensor_tensor(dif[:], s_sb[:, :, 1:64], s_sb[:, :, 0:63], ALU.subtract).then_inc(dif_ready, 1)
            pool.wait_ge(max_ready, u + 1)
            if steady or u >= 1:
                pool.wait_ge(e2_ready, u)
                pool.wait_ge(ed_ready, u)
            nc.gpsimd.tensor_tensor(dd[:], s_sb[:], bc(rows[:, s2, MX, :], 64), ALU.subtract).then_inc(d_ready, 1)
            pool.wait_ge(e1_ready, u + 1)
            pool.wait_ge(d_ready, u + 1)
            if steady or u >= 1:
                pool.wait_ge(sed_done, u)
            nc.gpsimd.tensor_tensor(ed[:], e1[:], dd[:], ALU.mult).then_inc(ed_ready, 1)

        run_steps(pool, step, 0, (4, TILES - 4), TILES, 4)

    @block.vector
    def _(dve):
        link = Link(dve, dve_own)
        link(nc.vector.memset(vblk[:], 0.0))
        nc.vector.memset(vblk[0:64, :, :, :, 0, 16:17], 1.0).then_inc(zeros_done, 1)
        nc.vector.memset(vblk[64:128, :, :, :, 1, 16:17], 1.0).then_inc(zeros_done, 1)
        dve.wait_ge(zeros_done, 2)
        dve.wait_ge(small_in, 12 * 16)
        link(nc.vector.tensor_copy(ident16[:], ident[:]))
        dve.wait_ge(sig_done, 1)
        link(nc.vector.tensor_scalar(sig[:], sig[:], 1.0, None, ALU.add))
        link(nc.vector.reciprocal(sig[:], sig[:]))
        for i, (gate, f) in enumerate(((0, -0.01), (1, 0.1 / math.log(64)), (3, 0.1 / 64), (4, -0.1 / 63))):
            link(nc.vector.tensor_scalar(coef[:, i:i + 1], sig[:, gate:gate + 1], f, None, ALU.mult))
        link(nc.vector.tensor_scalar(coef[:, 4:5], sig[:, 3:4], -0.1, 1.0, ALU.mult, ALU.add))
        link(nc.vector.tensor_scalar(coef[:, 5:6], cst[:, 10:11], sig[:, 2:3], 0.05, ALU.mult, ALU.mult))
        for par in range(2):
            link(nc.vector.tensor_scalar(bkm[:, :, par], bk[:], cst[:, par:par + 1], None, ALU.mult))
        nc.vector.tensor_scalar(bkm[:, :, 0], bk[:], cst[:, 0:1], None, ALU.mult).then_inc(setup_done, 1)
        dve.wait_ge(setup_done, 1)

        def ln_stats(src, stt, v, ready):
            link(nc.vector.bn_stats(stt[:, 0:6], src))
            dve.sem_inc(waits_met, 1)
            link(nc.vector.bn_aggr(stt[:, 6:8], stt[:, 0:6]))
            nc.vector.tensor_scalar(v[:, 0:1], stt[:, 7:8], EPS, None, ALU.add).then_inc(ready, 1)

        def ln_apply(dst, src, stt, v):
            link(nc.vector.scalar_tensor_tensor(out=v[:, 3:4], in0=v[:, 2:3], scalar=v[:, 2:3], in1=v[:, 0:1],
                                                op0=ALU.mult, op1=ALU.mult))
            link(nc.vector.tensor_scalar(v[:, 3:4], v[:, 3:4], -0.5, 1.5, ALU.mult, ALU.add))
            link(nc.vector.tensor_tensor(v[:, 3:4], v[:, 3:4], v[:, 2:3], ALU.mult))
            return nc.vector.tensor_scalar(dst, src, stt[:, 6:7], v[:, 3:4], ALU.subtract, ALU.mult)

        def step(u, s, steady, over):
            s2, n2 = s % 2, (s + 1) % 2
            here, ahead, behind = (steady or 0 <= u < TILES), (steady or u + 1 < TILES), (steady or 1 <= u <= TILES)
            R = rows[:, s2]
            if ahead:
                s4 = (s + 1) % 4
                dve.wait_ge(x_loaded[s4], ((u + 1) // 4 + 1) * 16 if not steady else (u + 1 - s4) * 4 + 16)
                if steady or u >= 1:
                    dve.wait_ge(rs1_ready, u)
                ln_stats(x[:, s4, :], stats[:, n2, :], ln_s[:, n2, :], var1_ready)
            if here:
                dve.wait_ge(s_ready, u + 1)
                nc.vector.tensor_reduce(R[:, MX, :], s_sb[:], AX_X, ALU.max).then_inc(max_ready, 1)
            if ahead:
                dve.wait_ge(rs1_ready, u + 2)
                dve.wait_ge(var1_ready, u + 2)
                if steady or u >= 1:
                    dve.wait_ge(xT_done, u)
                ln_apply(xhat[:, n2, :], x[:, s4, :], stats[:, n2, :], ln_s[:, n2, :]).then_inc(xhat_ready, 1)
            if here:
                nc.vector.tensor_reduce(R[:, SUM, :], s_sb[:], AX_X, ALU.add).then_inc(sum_done, 1)
                dve.wait_ge(dif_ready, u + 1)
                nc.vector.tensor_reduce(R[:, ABS, :], dif[:], AX_X, ALU.add, apply_absolute_value=True).then_inc(abs_done, 1)
            if behind:
                dve.wait_ge(o_done, u)
                dve.wait_ge(w_ready, u)
                Rb = rows[:, n2]
                o = ps_o[:, 0:272].rearrange("p (h e) -> p h e", e=17)
                link(nc.vector.tensor_tensor(recw[:, 0, :], o[:, :, 16], Rb[:, W, :], ALU.mult))
                link(nc.vector.reciprocal(recw[:, 1, :], recw[:, 0, :]))
                link(nc.vector.tensor_tensor(recw[:, 1, :], recw[:, 1, :], Rb[:, W, :], ALU.mult))
                for m in range(2):
                    om = o.rearrange("p (j m r) e -> p m j r e", j=4, m=2)[:, m, :, :, 0:16]
                    rm = recw[:, 1, :].rearrange("p (j m r) -> p m j r", j=4, m=2)[:, m].unsqueeze(3).to_broadcast([P, 4, 2, 16])
                    am = att[:, m * P:(m + 1) * P].rearrange("p (j r e) -> p j r e", j=4, r=2)
                    ins = nc.vector.tensor_tensor(am, om, rm, ALU.mult)
                    if m == 0:
                        link(ins)
                ins.then_inc(att_ready, 1)
            if here:
                dve.wait_ge(e1_ready, u + 1)
                nc.vector.tensor_reduce(R[:, Z, :], e1[:], AX_X, ALU.add).then_inc(z_ready, 1)
            if ahead:
                dve.wait_ge(v_done, u + 2)
                if steady or u >= 1:
                    dve.wait_ge(o_done, u)
                for par in range(2):
                    rr = slice(64 * par, 64 * par + 64)
                    for b in range(2):
                        o = vblk[rr, n2, b, :, par, 0:16].rearrange("p (j m) e -> p m j e", m=2)
                        i0 = ps_v[rr, b, :].rearrange("p (m j r e) -> p m j r e", m=2, j=4, r=2)[:, :, :, par]
                        i1 = bv[rr, :].rearrange("p (m j r e) -> p m j r e", m=2, j=4, r=2)[:, :, :, par]
                        ins = nc.vector.tensor_tensor(o, i0, i1, ALU.add)
                        if (par, b) != (1, 1):
                            link(ins)
                ins.then_inc(v_ready, 1)
            if here:
                dve.wait_ge(c_copied, 2 * u + 1)
                nc.vector.tensor_tensor(cr[:, 0, :], c[:, s2, :], cp[:, s2, 0, :], ALU.subtract).then_inc(c_rest, 1)
                dve.wait_ge(ed_ready, u + 1)
                nc.vector.tensor_reduce(R[:, SED, :], ed[:], AX_X, ALU.add).then_inc(sed_done, 1)
            if behind:
                sx = (s - 1) % 4
                dve.wait_ge(y_done, u)
                if steady or u >= 3:
                    dve.wait_ge(x1_stored[n2], ((u - 1) // 2) * 16 if not steady else (u - 1 - n2) * 8)
                link(nc.vector.tensor_tensor(x1[:, n2, :], ps_o[:, 0:D], x[:, sx, :], ALU.add))
                link(nc.vector.tensor_tensor(x1[:, n2, :], x1[:, n2, :], bo[:], ALU.add))
                nc.vector.bn_stats(stats2[:, n2, 0:6], x1[:, n2, :]).then_inc(x1_ready, 1)
                dve.wait_ge(x1_ready, u)
                dve.sem_inc(waits_met, 1)
                link(nc.vector.bn_aggr(stats2[:, n2, 6:8], stats2[:, n2, 0:6]))
                nc.vector.tensor_scalar(ln2[:, n2, 0:1], stats2[:, n2, 7:8], EPS, None, ALU.add).then_inc(var2_ready, 1)
            if here:
                dve.wait_ge(c_copied, 2 * u + 2)
                dve.wait_ge(c_rest, 2 * u + 1)
                nc.vector.tensor_tensor(cr[:, 1, :], cr[:, 0, :], cp[:, s2, 1, :], ALU.subtract).then_inc(c_rest, 1)
                dve.wait_ge(logs_ready, u + 1)
                dve.wait_ge(sed_done, u + 1)
                link(nc.vector.reciprocal(R[:, TA, :], R[:, Z, :]))
                link(nc.vector.tensor_tensor(R[:, TA, :], R[:, TA, :], R[:, SED, :], ALU.mult))
                link(nc.vector.tensor_tensor(R[:, TA, :], R[:, LNZ, :], R[:, TA, :], ALU.subtract))
                link(nc.vector.tensor_scalar(R[:, C, :], R[:, KN, :], coef[:, 0:1], None, ALU.mult))
                for i, n in ((1, TA), (2, SUM), (3, ABS)):
                    link(nc.vector.scalar_tensor_tensor(out=R[:, C, :], in0=R[:, n, :], scalar=coef[:, i:i + 1],
                                                        in1=R[:, C, :], op0=ALU.mult, op1=ALU.add))
                link(nc.vector.scalar_tensor_tensor(out=R[:, TA, :], in0=R[:, MX, :], scalar=coef[:, 4:5],
                                                    in1=R[:, C, :], op0=ALU.mult, op1=ALU.add))
                link(nc.vector.tensor_tensor(R[:, TB, :], R[:, C, :], R[:, TA, :], ALU.subtract))
                nc.vector.scalar_tensor_tensor(out=R[:, TB, :], in0=R[:, MX, :], scalar=coef[:, 4:5],
                                               in1=R[:, TB, :], op0=ALU.mult, op1=ALU.add).then_inc(w_arg, 1)
            if behind:
                dve.wait_ge(rs2_ready, u)
                dve.wait_ge(var2_ready, u)
                link(ln_apply(q[:], x1[:, n2, :], stats2[:, n2, :], ln2[:, n2, :]))
                if steady or u >= 3:
                    dve.wait_ge(qp_stored[n2], ((u - 1) // 2) * 96 if not steady else (u - 1 - n2) * 48)
                link(nc.vector.tensor_copy(qp[:, n2, 0, :], q[:]))
                link(nc.vector.tensor_tensor(r[:, 0, :], q[:], qp[:, n2, 0, :], ALU.subtract))
                link(nc.vector.tensor_copy(qp[:, n2, 1, :], r[:, 0, :]))
                link(nc.vector.tensor_tensor(r[:, 1, :], r[:, 0, :], qp[:, n2, 1, :], ALU.subtract))
                nc.vector.tensor_copy(qp[:, n2, 2, :], r[:, 1, :]).then_inc(qp_ready, 1)
            if ahead:
                dve.wait_ge(kn_done, u + 2)
                if steady or u >= 1:
                    dve.wait_ge(logs_ready, u)
                nc.vector.tensor_scalar(rows[:, n2, KN2, :].rearrange("p (j m r) -> p m j r", j=4, m=2),
                                        ps_x[:, 256:272].rearrange("p (m j r) -> p m j r", m=2, j=4), 1e-18, None,
                                        ALU.max).then_inc(kn_read, 1)

        PER = 2 + 3 + 4 + 3 + 3 + 9 + 3 + 5
        run_steps(dve, step, -1, N_STEADY, TILES + 1, 4, link, 4 * PER)


def phase2(nc, t, st, sbt, pst, sem, g):
    B, S, D = g["B"], g["S"], g["D"]
    HX = 8
    ident16, gamma = g["ident16"], g["gamma"]
    x1_dram, x2_dram, qp_dram, kp_dram = (g[k] for k in ("x1_dram", "x2_dram", "qp_dram", "kp_dram"))
    SCALE = 1.0 / math.sqrt(S // HX)
    PAIRS = B // 2

    def sb(name, shape, dt=F32):
        return sbt(st, name, shape, dt)

    def sm(name):
        return sem(st, name)

    ks = sb("ks", [P, 4, HX, D], BF16)
    qs = sb("qs", [P, 4, HX, D], BF16)
    vT = sb("vT", [P, 4, 2, 64])
    vaug = sb("vaug", [P, 4, 2, HX, 32])
    mx = sb("mx", [P, 2, 16])
    mp = sb("mp", [P, 2, 48], BF16)
    mr = sb("mr", [P, 2, 16])
    mT = sb("mT", [48, 2, P], BF16)
    pr = sb("pr", [P, 2, 4, 2, D])
    o_sb = sb("o_sb", [P, 2, 2, D])
    num = sb("num", [P, 2, D])
    den = sb("den", [P, 2, D])
    rd = sb("rd", [P, D])
    x1 = sb("x1_in", [P, 2, D])
    x2 = sb("x2_tile", [P, 2, D])

    ps_s = pst(st, "ps2_s", [P, 2, 2, D])
    ps_t = pst(st, "ps2_t", [P, 2, 2, 2, D])
    ps_o = pst(st, "ps2_o", [P, 2, D])
    ps_m = pst(st, "ps2_m", [P, P * 4], BF16)

    zero_done, ones_done = sm("zero_done"), sm("ones_done")
    dve_own = sm("dve2_own")
    waits_met, pool_waits_met = sm("waits2_met"), sm("pool_waits_met")
    kq_loaded = [sm(f"kq_loaded{i}") for i in range(4)]
    v_loaded = [sm(f"v_loaded{i}") for i in range(4)]
    m_loaded = [sm(f"m_loaded{i}") for i in range(4)]
    x1_loaded = [sm(f"x1_loaded{i}") for i in range(2)]
    o_moved = [sm(f"o_moved{i}") for i in range(2)]
    x2_stored = [sm(f"x2_stored{i}") for i in range(2)]
    s_ready, max_done, mp_ready, mT_done, mT_ready = sm("s2_ready"), sm("max2_done"), sm("mp_ready"), sm("mT_done"), sm("mT_ready")
    st_ready, exp_done, pv_done, o_ready = sm("st_ready"), sm("exp_done"), sm("pv_done"), sm("o_ready")
    vaug_ready, x2_ready = sm("vaug_ready"), sm("x2_ready")
    STEADY = (7, B - 5)

    def slot_value(b, slot, slots, steady, each):
        return (b // slots + 1) * each if not steady else (b - slot) * (each // slots) + each

    block = st.enter_context(nc.Block())

    @block.sync
    def _(sp):
        def load(b, s, steady):
            for i in range(3):
                kp, qp = kp_dram[b, i], qp_dram[b]
                k2 = kp.rearrange("d h c -> d (h c)")
                sp.dma_start(ks[24 * i:24 * i + 24, s, :, :].rearrange("p h c -> p (h c)"),
                             bass.AP(k2.tensor, k2.offset, [[0, 3]] + list(k2.ap))).then_inc(kq_loaded[s], 16)
                sp.dma_start(qs[24 * i:24 * i + 24, s, :, :].rearrange("p h c -> p (h c)"),
                             qp.rearrange("i d h c -> (i d) (h c)")).then_inc(kq_loaded[s], 16)
            if steady or b >= 4:
                sp.wait_ge(vaug_ready, b - 3)
            sp.dma_start(vT[:, s, :, :], t["ctxT"][b].rearrange("(c l) r -> l c r", c=2)).then_inc(v_loaded[s], 16)

        def step(b, s, steady, over):
            if steady or 0 <= b < B - 3:
                if steady or b >= 1:
                    sp.wait_ge(st_ready, b * 4)
                load(b + 3, (s + 3) % 4, steady)
            if s % 2 == 1 and (steady or 0 <= b < B):
                p = (s // 2) % 2
                if steady or b >= 5:
                    sp.wait_ge(x2_ready, over(2, -3))
                row = (b - 1) * S
                sp.dma_start(x1[:, p, :], x1_dram[bass.ds(row, P), :]).then_inc(x1_loaded[p], 16)
            if steady or 0 <= b + 1 < B:
                n = (s + 1) % 4
                sp.wait_ge(mT_ready, b + 2)
                sp.dma_start(qs[96:99, n, :, :].rearrange("p h (c q) -> p (h c) q", c=2),
                             mT[:, n % 2, :]).then_inc(m_loaded[n], 16)
            if steady or 1 <= b <= B:
                v, sv = b - 1, (s - 1) % 2
                pp = (((s - 1) % 4) // 2) % 2
                sp.wait_ge(o_ready, v + 1)
                for h in range(HX):
                    half_, j = h // 4, h % 4
                    rows = slice(64 * sv + 8 * h, 64 * sv + 8 * h + 8)
                    sp.dma_start(num[rows, pp, :], o_sb[32 * j:32 * j + 8, sv, half_, :]).then_inc(o_moved[sv], 16)
                    sp.dma_start(den[rows, pp, :], o_sb[32 * j + 8:32 * j + 16, sv, half_, :]).then_inc(o_moved[sv], 16)
            if s % 2 == 1 and (steady or 3 <= b < B + 2):
                p = (((s - 3) % 4) // 2) % 2
                sp.wait_ge(x2_ready, over(2, -1))
                sp.dma_start(x2_dram[bass.ds((b - 3) * S, P), :], x2[:, p, :]).then_inc(x2_stored[p], 16)

        sp.wait_ge(ones_done, 2)
        for b in range(3):
            load(b, b, False)
        run_steps(sp, step, -1, STEADY, B + 2, 4)
        for i in range(2):
            sp.wait_ge(x2_stored[i], 16 * (PAIRS // 2))

    @block.tensor
    def _(pe):
        def weigh(b, s, hf, steady):
            n = 2 * b + hf
            pe.wait_ge(exp_done, 2 * n + 2)
            if hf == 0:
                pe.wait_ge(vaug_ready, b + 1)
                if steady or b >= 1:
                    pe.wait_ge(o_ready, b)
            for lc in range(2):
                for j in range(4):
                    last = nc.tensor.matmul(ps_o[32 * j:32 * j + 32, hf, :], vaug[:, s, lc, 4 * hf + j, :],
                                            pr[:, hf, j, lc, :], start=lc == 0, stop=lc == 1)
            last.then_inc(pv_done, 1)

        def step(b, s, steady, over):
            here, ahead = (steady or 0 <= b < B), (steady or b + 2 < B)
            if steady or 0 <= b + 1 < B:
                n = (s + 1) % 2
                pe.wait_ge(mp_ready, b + 2)
                if steady or b >= 0:
                    pe.wait_ge(mT_ready, b + 1)
                pe.sem_inc(waits_met, 1)
                nc.tensor.transpose(ps_m[0:48, 0:P], mp[:, n, :], ident16[:]).then_inc(mT_done, 1)
            if here:
                pe.wait_ge(m_loaded[s], slot_value(b, s, 4, steady, 16))
            if ahead:
                sa = (s + 2) % 4
                pe.wait_ge(kq_loaded[sa], slot_value(b + 2, sa, 4, steady, 96))
            for p in range(4):
                if here:
                    u = 4 * b + p
                    if steady or u >= 2:
                        pe.wait_ge(exp_done, u - 1)
                    for h in (2 * p, 2 * p + 1):
                        for lc in range(2):
                            last = nc.tensor.matmul(ps_t[:, p % 2, h % 2, lc, :], ks[:, s, h, lc * P:(lc + 1) * P],
                                                    qs[:, s, h, :], start=True, stop=True)
                    last.then_inc(st_ready, 1)
                if ahead:
                    for h in (2 * p, 2 * p + 1):
                        v = 8 * (b + 2) + h
                        if steady or v >= 2:
                            pe.wait_ge(max_done, v - 1)
                        for c in range(2):
                            last = nc.tensor.matmul(ps_s[:, h % 2, c, :], qs[0:96, sa, h, c * P:(c + 1) * P],
                                                    ks[0:96, sa, h, :], start=True, stop=True)
                        last.then_inc(s_ready, 1)
                if p == 0 and (steady or 1 <= b <= B):
                    weigh(b - 1, (s - 1) % 4, 1, steady)
                if p == 2 and here:
                    weigh(b, s, 0, steady)

        run_steps(pe, step, -2, STEADY, B + 1, 4)

    @block.scalar
    def _(act):
        def step(b, s, steady, over):
            here = steady or 0 <= b < B
            for p in range(4):
                if here:
                    u = 4 * b + p
                    act.wait_ge(st_ready, u + 1)
                    if steady or 2 * b + p // 2 >= 2:
                        act.wait_ge(pv_done, 2 * b + p // 2 - 1)
                    nc.scalar.activation(pr[:, p // 2, 2 * (p % 2):2 * (p % 2) + 2, :, :], ps_t[:, p % 2, :, :, :],
                                         ACT.Exp, scale=SCALE).then_inc(exp_done, 1)
                if p == 0 and (steady or 0 <= b + 1 < B):
                    n = (s + 1) % 2
                    act.wait_ge(mT_done, b + 2)
                    if steady or b >= 1:
                        m = (s - 1) % 4
                        act.wait_ge(m_loaded[m], slot_value(b - 1, m, 4, steady, 16))
                    nc.scalar.activation(mT[:, n, :], ps_m[0:48, 0:P], ACT.Copy).then_inc(mT_ready, 1)
                if p == 1 and (steady or 1 <= b <= B):
                    v, sv = b - 1, (s - 1) % 2
                    act.wait_ge(pv_done, 2 * v + 2)
                    if steady or v >= 2:
                        act.wait_ge(o_moved[sv], slot_value(v - 2, sv, 2, steady, 256))
                    nc.scalar.activation(o_sb[:, sv, :, :], ps_o[:], ACT.Copy).then_inc(o_ready, 1)

        run_steps(act, step, -1, STEADY, B + 1, 4)

    @block.gpsimd
    def _(pool):
        nc.gpsimd.memset(vaug[:], 0.0).then_inc(zero_done, 1)
        pool.wait_ge(zero_done, 1)
        nc.gpsimd.memset(vaug[:, :, :, :, 8:16], 1.0).then_inc(zero_done, 1)
        pool.wait_ge(zero_done, 2)

        def step(b, s, steady, over):
            pool.wait_ge(v_loaded[s], slot_value(b, s, 4, steady, 16))
            if steady or b >= 4:
                pool.wait_ge(pv_done, 2 * (b - 4) + 2)
            pool.sem_inc(pool_waits_met, 1)
            nc.gpsimd.tensor_copy(vaug[:, s, :, :, 0:8], vT[:, s, :, :].rearrange("p c (h d) -> p c h d", h=HX))\
                .then_inc(vaug_ready, 1)

        run_steps(pool, step, 0, (4, B), B, 4)

    @block.vector
    def _(dve):
        link = Link(dve, dve_own)
        link(nc.vector.memset(ks[:], 0.0))
        link(nc.vector.memset(qs[:], 0.0))
        nc.vector.memset(ks[96:99, :, :, :], 1.0).then_inc(ones_done, 2)
        dve.wait_ge(ones_done, 2)

        def step(b, s, steady, over):
            if steady or b + 2 < B:
                n = (s + 2) % 2
                for h in range(HX):
                    dve.wait_ge(s_ready, 8 * (b + 2) + h + 1)
                    nc.vector.tensor_reduce(mx[:, n, 2 * h:2 * h + 2], ps_s[:, h % 2, :, :], AX_X, ALU.max).then_inc(max_done, 1)
                dve.wait_ge(max_done, 8 * (b + 2) + 8)
                if steady or b >= 0:
                    dve.wait_ge(mT_done, b + 1)
                part = [mp[:, n, 16 * i:16 * i + 16] for i in range(3)]
                link(nc.vector.tensor_scalar(part[0], mx[:, n, :], -1.0, None, ALU.mult))
                link(nc.vector.scalar_tensor_tensor(out=mr[:, 0, :], in0=mx[:, n, :], scalar=-1.0, in1=part[0],
                                                    op0=ALU.mult, op1=ALU.subtract))
                link(nc.vector.tensor_copy(part[1], mr[:, 0, :]))
                link(nc.vector.tensor_tensor(mr[:, 1, :], mr[:, 0, :], part[1], ALU.subtract))
                nc.vector.tensor_copy(part[2], mr[:, 1, :]).then_inc(mp_ready, 1)
            if s % 2 == 1 and (steady or 3 <= b < B + 2):
                p = (((s - 3) % 4) // 2) % 2
                for bb in range(2):
                    dve.wait_ge(o_moved[bb], over(2, -1) * 256)
                dve.wait_ge(x1_loaded[p], over(4, 1) * 16)
                link(nc.vector.reciprocal(rd[:], den[:, p, :]))
                link(nc.vector.tensor_tensor(rd[:], rd[:], num[:, p, :], ALU.mult))
                if steady or b >= 7:
                    dve.wait_ge(x2_stored[p], over(4, -3) * 16)
                nc.vector.scalar_tensor_tensor(out=x2[:, p, :], in0=rd[:], scalar=gamma[:, 0:1], in1=x1[:, p, :],
                                               op0=ALU.mult, op1=ALU.add).then_inc(x2_ready, 1)

        run_steps(dve, step, -2, STEADY, B + 2, 4, link, 4 * 4 + 2 * 2)


def phase3(nc, t, st, sbt, pst, sem, g):
    D = g["D"]
    E, TOK, BL = 8, 512, 4
    T = g["B"] * g["S"] // TOK
    ident, w1, w2, w3, rw, iota8 = (g[k] for k in ("ident", "w1", "w2", "w3", "rw", "iota8"))
    x2_dram, out, ffn_in = g["x2_dram"], g["out"], g["ffn_in"]

    def sb(name, shape, dt=F32):
        return sbt(st, name, shape, dt)

    def sm(name):
        return sem(st, name)

    x = sb("x2_in", [P, 2, BL, D])
    xn = sb("xn", [P, BL, D])
    xnT = sb("xnT", [P, 2, 2, TOK])
    stats = sb("stats3", [P, BL, 6])
    mv = sb("mv3", [P, BL, 2])
    v3 = sb("v3", [P, 4, BL])
    lg = sb("logits", [P, BL, E])
    top = sb("top", [P, BL, 8])
    idx = sb("idx", [P, BL, 8], U32)
    idf = sb("idf", [P, BL, 8])
    dl = sb("dl", [P, 3, BL])
    wt = sb("wt", [P, 2, BL, E])
    wtb = sb("wtb", [P, BL, E])
    sg = sb("sg", [P, 2, TOK])
    hh = sb("hh", [P, 2, TOK])
    acc = sb("acc", [P, 2, BL, D])

    ps_g = pst(st, "ps_g", [P, 2, TOK])
    ps_v = pst(st, "ps3_v", [P, 2, TOK])
    ps_y = pst(st, "ps_y", [P, BL, D])
    ps_x = pst(st, "ps3_x", [P, TOK])
    ps_l = pst(st, "ps_l", [P, 512])

    x_loaded = [sm(f"x2_loaded{i}") for i in range(2)]
    stored = [sm(f"out_stored{i}") for i in range(2)]
    own = sm("dve3_own")
    waits_met = sm("waits3_met")
    act_own = sm("act3_own")
    var_ready, rs_ready, xn_ready = sm("var3_ready"), sm("rs3_ready"), sm("xn_ready")
    xT_done, xT_ready, lg_done, dl_ready, tw_ready, wt_ready = (sm(n) for n in (
        "xT3_done", "xT3_ready", "lg_done", "dl_ready", "tw_ready", "wt_ready"))
    gv_done, sg_ready, hh_ready, y_done, acc_done = (sm(n) for n in ("gv_done", "sg_ready", "hh_ready", "y3_done", "acc_done"))
    STEADY = (1, T - 1)

    block = st.enter_context(nc.Block())

    @block.sync
    def _(sp):
        def rows(ap, k):
            return ap[bass.ds(k * TOK, TOK), :].rearrange("(n p) d -> p n d", p=P)

        def step(k, s, steady, over):
            if steady or k + 1 < T:
                n = (s + 1) % 2
                if steady or k >= 1:
                    sp.wait_ge(acc_done, 8 * (k - 1) + 1)
                sp.dma_start(x[:, n, :, :], rows(x2_dram, k + 1)).then_inc(x_loaded[n], 16)
            if steady or k >= 1:
                sp.wait_ge(acc_done, 8 * k)
                sp.dma_start(rows(out, k - 1), acc[:, (s - 1) % 2, :, :]).then_inc(stored[(s - 1) % 2], 16)

        run_steps(sp, step, -1, STEADY, T + 1, 2)
        for i in range(2):
            sp.wait_ge(stored[i], 16 * (T // 2))

    @block.tensor
    def _(pe):
        def prep(k, s):
            pe.wait_ge(xn_ready, k + 1)
            for kc in range(2):
                if kc == 1:
                    pe.wait_ge(xT_ready, 2 * k + 1)
                for n in range(BL):
                    last = nc.tensor.transpose(ps_x[:, n * P:(n + 1) * P], xn[:, n, kc * P:(kc + 1) * P], ident[:])
                last.then_inc(xT_done, 1)

        def logits(k, s, steady):
            pe.wait_ge(xT_ready, 2 * k + 2)
            for n in range(BL):
                for kc in range(2):
                    last = nc.tensor.matmul(ps_l[:, n * E:(n + 1) * E], xnT[:, s, kc, n * P:(n + 1) * P], rw[:, kc, :],
                                            start=kc == 0, stop=kc == 1)
            last.then_inc(lg_done, 1)

        def expert_out(k, e, steady):
            n = 8 * k + e
            pe.wait_ge(hh_ready, n + 1)
            if steady or n >= 1:
                pe.wait_ge(acc_done, n)
            for bl in range(BL):
                last = nc.tensor.matmul(ps_y[:, bl, :], hh[:, e % 2, bl * P:(bl + 1) * P], w3[:, e, :],
                                        start=True, stop=True)
            last.then_inc(y_done, 1)

        def step(k, s, steady, over):
            here, ahead = (steady or 0 <= k < T), (steady or k + 1 < T)
            for e in range(E):
                if here:
                    n = 8 * k + e
                    if steady or n >= 2:
                        pe.wait_ge(hh_ready, n - 1)
                    if e == 0:
                        pe.wait_ge(xT_ready, 2 * k + 2)
                    for ps, w in ((ps_g, w1), (ps_v, w2)):
                        for kc in range(2):
                            last = nc.tensor.matmul(ps[:, e % 2, :], w[:, e, kc, :], xnT[:, s, kc, :],
                                                    start=kc == 0, stop=kc == 1)
                    last.then_inc(gv_done, 1)
                if e == 0 and (steady or k >= 1):
                    expert_out(k - 1, E - 1, steady)
                if here and e >= 1:
                    expert_out(k, e - 1, steady)
                if ahead and e == 4:
                    prep(k + 1, (s + 1) % 2)
                if ahead and e == 6:
                    logits(k + 1, (s + 1) % 2, steady)

        pe.wait_ge(ffn_in, 5 * 16)
        run_steps(pe, step, -1, STEADY, T + 1, 2)

    @block.scalar
    def _(act):
        link = Link(act, act_own)

        def step(k, s, steady, over):
            here, ahead = (steady or 0 <= k < T), (steady or k + 1 < T)
            n2 = (s + 1) % 2
            for e in range(E):
                if here:
                    n = 8 * k + e
                    act.wait_ge(gv_done, n + 1)
                    if steady or n >= 2:
                        act.wait_ge(hh_ready, n - 1)
                    nc.scalar.activation(sg[:, e % 2, :], ps_g[:, e % 2, :], ACT.Sigmoid).then_inc(sg_ready, 1)
                if ahead and e == 2:
                    act.preload_act_table_set("natural_log_exp_and_others")
                    act.wait_ge(var_ready, k + 2)
                    link(nc.scalar.activation(v3[:, 1, :], v3[:, 0, :], ACT.Ln))
                    nc.scalar.activation(v3[:, 2, :], v3[:, 1, :], ACT.Exp, scale=-0.5).then_inc(rs_ready, 1)
                if ahead and e == 4:
                    for kc in range(2):
                        act.wait_ge(xT_done, 2 * (k + 1) + kc + 1)
                        if kc == 0 and (steady or k >= 1):
                            act.wait_ge(gv_done, 8 * k)
                        nc.scalar.activation(xnT[:, n2, kc, :], ps_x[:], ACT.Copy).then_inc(xT_ready, 1)
                if ahead and e == 6:
                    act.wait_ge(dl_ready, k + 2)
                    nc.scalar.activation(dl[:, 1, :], dl[:, 0, :], ACT.Sigmoid).then_inc(tw_ready, 1)
                    nc.scalar.activation(dl[:, 2, :], dl[:, 0, :], ACT.Sigmoid, scale=-1.0).then_inc(tw_ready, 1)

        run_steps(act, step, -1, STEADY, T, 2, link, 2)

    @block.vector
    def _(dve):
        link = Link(dve, own)

        def add_expert(k, s, e, steady):
            n = 8 * k + e
            dve.wait_ge(y_done, n + 1)
            if e == 0:
                dve.wait_ge(wt_ready, k + 1)
                if steady or k >= 2:
                    dve.wait_ge(stored[s], (k // 2) * 16)
            else:
                dve.wait_ge(acc_done, n)
            for bl in range(BL):
                before = x[:, s, bl, :] if e == 0 else acc[:, s, bl, :]
                ins = nc.vector.scalar_tensor_tensor(out=acc[:, s, bl, :], in0=ps_y[:, bl, :],
                                                     scalar=wt[:, s, bl, e:e + 1], in1=before,
                                                     op0=ALU.mult, op1=ALU.add)
                if bl < BL - 1:
                    link(ins)
            ins.then_inc(acc_done, 1)

        def step(k, s, steady, over):
            here, ahead = (steady or 0 <= k < T), (steady or k + 1 < T)
            n2 = (s + 1) % 2
            for e in range(E):
                if here:
                    n = 8 * k + e
                    dve.wait_ge(sg_ready, n + 1)
                    if steady or n >= 2:
                        dve.wait_ge(y_done, n - 1)
                    link(nc.vector.tensor_tensor(hh[:, e % 2, :], sg[:, e % 2, :], ps_g[:, e % 2, :], ALU.mult))
                    nc.vector.tensor_tensor(hh[:, e % 2, :], hh[:, e % 2, :], ps_v[:, e % 2, :], ALU.mult).then_inc(hh_ready, 1)
                if e == 0 and (steady or k >= 1):
                    add_expert(k - 1, (s - 1) % 2, E - 1, steady)
                if here and e >= 1:
                    add_expert(k, s, e - 1, steady)
                if ahead and e == 1:
                    dve.wait_ge(x_loaded[n2], ((k + 1) // 2 + 1) * 16 if not steady else (k + 1 - n2) * 8 + 16)
                    for n in range(BL):
                        link(nc.vector.bn_stats(stats[:, n, :], x[:, n2, n, :]))
                    for n in range(BL):
                        dve.sem_inc(waits_met, 1)
                        link(nc.vector.bn_aggr(mv[:, n, :], stats[:, n, :]))
                    nc.vector.tensor_scalar(v3[:, 0, :], mv[:, :, 1], EPS, None, ALU.add).then_inc(var_ready, 1)
                if ahead and e == 3:
                    dve.wait_ge(rs_ready, k + 2)
                    dve.wait_ge(var_ready, k + 2)
                    link(nc.vector.tensor_tensor(v3[:, 3, :], v3[:, 2, :], v3[:, 2, :], ALU.mult))
                    link(nc.vector.tensor_tensor(v3[:, 3, :], v3[:, 3, :], v3[:, 0, :], ALU.mult))
                    link(nc.vector.tensor_scalar(v3[:, 3, :], v3[:, 3, :], -0.5, 1.5, ALU.mult, ALU.add))
                    link(nc.vector.tensor_tensor(v3[:, 3, :], v3[:, 3, :], v3[:, 2, :], ALU.mult))
                    if steady or k >= 0:
                        dve.wait_ge(xT_done, 2 * k + 2)
                    for n in range(BL):
                        ins = nc.vector.tensor_scalar(xn[:, n, :], x[:, n2, n, :], mv[:, n, 0:1], v3[:, 3, n:n + 1],
                                                      ALU.subtract, ALU.mult)
                        if n < BL - 1:
                            link(ins)
                    ins.then_inc(xn_ready, 1)
                if ahead and e == 6:
                    dve.wait_ge(lg_done, k + 2)
                    link(nc.vector.tensor_copy(lg[:], ps_l[:, 0:BL * E].rearrange("p (n e) -> p n e", n=BL)))
                    for n in range(BL):
                        dve.sem_inc(waits_met, 1)
                        link(nc.vector.max(top[:, n, :], lg[:, n, :]))
                    for n in range(BL):
                        dve.sem_inc(waits_met, 1)
                        link(nc.vector.max_index(idx[:, n, :], top[:, n, :], lg[:, n, :]))
                    nc.vector.tensor_tensor(dl[:, 0, :], top[:, :, 0], top[:, :, 1], ALU.subtract).then_inc(dl_ready, 1)
                    link(nc.vector.tensor_copy(idf[:], idx[:]))
                if ahead and e == 7:
                    dve.wait_ge(tw_ready, 2 * (k + 2))
                    for n in range(BL):
                        for j, dst in ((0, wt[:, n2, n, :]), (1, wtb[:, n, :])):
                            link(nc.vector.tensor_scalar(dst, iota8[:], idf[:, n, j:j + 1], dl[:, 1 + j, n:n + 1],
                                                         ALU.is_equal, ALU.mult))
                    nc.vector.tensor_tensor(wt[:, n2, :, :], wt[:, n2, :, :], wtb[:], ALU.add).then_inc(wt_ready, 1)

        dve.wait_ge(ffn_in, 5 * 16)
        run_steps(dve, step, -1, STEADY, T + 1, 2, link, 2 * (8 * 4 + 8 + 4 + 3 + 1 + 8 + 1 + 8))


def kernel(**inputs):
    import numpy as np
    import concourse.bacc as bacc
    from concourse.bass_utils import run_bass_kernel_spmd

    a = {k: np.asarray(v) for k, v in inputs.items()}
    B, S, D = a["x"].shape
    cst = np.zeros((P, 11), np.float32)
    lane = np.arange(P)
    cst[:, 0] = (lane // 16) % 2 == 0
    cst[:, 1] = (lane // 16) % 2 == 1
    for h in range(8):
        cst[:, 2 + h] = lane // 16 == h
    cst[:, 10] = (lane % S) / S
    arrays = {
        "x": a["x"], "ctx": a["ctx_2048"], "ctxT": a["ctx_2048"].transpose(0, 2, 1),
        "wqT": a["L0_attn_Wq"].T, "wkT": a["L0_attn_Wk"].T, "wvT": a["L0_attn_Wv"].T, "woT": a["L0_attn_Wo"].T,
        "bq": a["L0_attn_bq"], "bk": a["L0_attn_bk"], "bv": a["L0_attn_bv"], "bo": a["L0_attn_bo"],
        "truth": a["L0_attn_truth_gate"], "balance": a["L0_attn_balance_gate"], "order": a["L0_attn_order_gate"],
        "justice": a["L0_attn_justice_gate"], "harmony": a["L0_attn_harmony_gate"],
        "gamma": a["L0_xattn_gamma"].reshape(1), "rwT": a["L0_ffn_router_w"].T,
        "w1": a["L0_ffn_w1"], "w2": a["L0_ffn_w2"], "w3": a["L0_ffn_w3"],
        "ident": np.eye(P, dtype=np.float32), "cst": cst,
        "iota8": np.tile(np.arange(8, dtype=np.float32), (P, 1)),
    }
    nc = bacc.Bacc("TRN2", target_bir_lowering=False, num_devices=1)
    feeds, t = {}, {}
    for name, v in arrays.items():
        v = np.ascontiguousarray(v)
        feeds["in_" + name] = v
        t[name] = nc.dram_tensor("in_" + name, v.shape, mybir.dt.from_np(v.dtype), kind="ExternalInput").ap()
    t["out"] = nc.dram_tensor("out_x", (B, S, D), F32, kind="ExternalOutput").ap()
    decoder_kernel(nc, t)
    r = run_bass_kernel_spmd(nc, [feeds], core_ids=[0])
    return r.results[0]["out_x"]
```

```python
import math
from contextlib import ExitStack

import concourse.bass as bass
from concourse import mybir

F32 = mybir.dt.float32
BF16 = mybir.dt.bfloat16
U32 = mybir.dt.uint32
ALU = mybir.AluOpType
ACT = mybir.ActivationFunctionType
AX_X = mybir.AxisListType.X

P = 128
EPS = 1e-5


class Link:

    def __init__(self, eng, sem):
        self.eng, self.sem, self.base, self.n = eng, sem, 0, 0

    def __call__(self, ins):
        ins.then_inc(self.sem, 1)
        self.n += 1
        self.eng.wait_ge(self.sem, self.base + self.n)

    def enter_loop(self):
        self.before = self.n
        self.n = 0

    def at(self, i, per):
        self.base = self.before + i * per

    def leave_loop(self, trips, per):
        assert self.n == per, (self.n, per)
        self.base, self.n = 0, self.before + trips * per


def run_steps(eng, step, first, steady, end, unroll, link=None, per=0):
    lo, hi = steady
    for t in range(first, lo):
        step(t, t % unroll, False, lambda n, off=0, t=t: (t + off) // n)
    trips = (hi - lo) // unroll
    assert lo + trips * unroll == hi
    if link:
        link.enter_loop()
    with eng.Fori(0, trips) as i:
        if link:
            link.at(i, per)
        for s in range(unroll):
            step(i * unroll + (lo + s), (lo + s) % unroll, True,
                 lambda n, off=0, s=s: i * (unroll // n) + (lo + s + off) // n)
    if link:
        link.leave_loop(trips, per)
    for t in range(hi, end):
        step(t, t % unroll, False, lambda n, off=0, t=t: (t + off) // n)


def decoder_kernel(nc, t):
    B, S, D = t["x"].shape
    H, HD = 16, D // 16
    TILES = B * S // P
    ctx = ExitStack()

    def sbt(stack, name, shape, dt=F32):
        return stack.enter_context(nc.sbuf_tensor(name, shape, dt))

    def pst(stack, name, shape, dt=F32):
        return stack.enter_context(nc.psum_tensor(name, shape, dt))

    def sem(stack, name):
        return stack.enter_context(nc.semaphore(name))

    x1_dram = nc.dram_tensor("x1_scratch", [B * S, D], F32, kind="Internal").ap()
    x2_dram = nc.dram_tensor("x2_scratch", [B * S, D], F32, kind="Internal").ap()
    qp_dram = nc.dram_tensor("q_parts", [B, 8, 3, 8, D], BF16, kind="Internal").ap()
    o_dram = nc.dram_tensor("o_scratch", [B, 2, P, D], F32, kind="Internal").ap()
    kp_dram = nc.dram_tensor("k_parts", [B, 3, 8, 8, D], BF16, kind="Internal").ap()
    x_in = t["x"].rearrange("b s d -> (b s) d")
    c_in = t["ctx"].rearrange("b s d -> (b s) d")
    out = t["out"].rearrange("b s d -> (b s) d")

    with ctx:
        ident = sbt(ctx, "ident", [P, P])
        ident16 = sbt(ctx, "ident16", [P, P], BF16)
        gamma = sbt(ctx, "gamma", [P, 1])
        w1 = sbt(ctx, "w1", [P, 8, 2, P])
        w2 = sbt(ctx, "w2", [P, 8, 2, P])
        w3 = sbt(ctx, "w3", [P, 8, D])
        rw = sbt(ctx, "rw", [P, 2, 8])
        iota8 = sbt(ctx, "iota8", [P, 8])
        weights_in = sem(ctx, "weights_in")
        ffn_in = sem(ctx, "ffn_in")

        with ExitStack() as st:
            phase1(nc, t, st, sbt, pst, sem, locals())
        with ExitStack() as st:
            phase2(nc, t, st, sbt, pst, sem, locals())
        with ExitStack() as st:
            phase3(nc, t, st, sbt, pst, sem, locals())


def phase1(nc, t, st, sbt, pst, sem, g):
    TILES, D = g["TILES"], g["D"]
    ident, ident16, gamma = g["ident"], g["ident16"], g["gamma"]
    x_in, c_in, x1_dram, qp_dram, kp_dram = (g[k] for k in ("x_in", "c_in", "x1_dram", "qp_dram", "kp_dram"))
    weights_in, ffn_in = g["weights_in"], g["ffn_in"]

    def sb(name, shape, dt=F32):
        return sbt(st, name, shape, dt)

    def sm(name):
        return sem(st, name)

    wq, wk, wv, wo = (sb(n, [P, 2, D]) for n in ("wq", "wk", "wv", "wo"))
    bq, bk = sb("bq", [P, 2]), sb("bk", [P, 2])
    bv, bo = sb("bv", [P, D]), sb("bo", [P, D])
    gates = sb("gates", [P, 5])
    cst = sb("cst", [P, 11])
    sig = sb("sig", [P, 5])
    coef = sb("coef", [P, 6])
    cf = sb("cf", [P, 5, 16])
    bkm = sb("bkm", [P, 2, 2])
    x = sb("x_tile", [P, 4, D])
    c = sb("c_tile", [P, 2, D])
    stats = sb("stats", [P, 2, 8])
    ln_s = sb("ln_s", [P, 2, 4])
    xhat = sb("xhat", [P, 2, D])
    hT = sb("hT", [P, 2, 2, 2, 2, 64])
    qT = sb("qT", [P, 2, 2, P])
    kT = sb("kT", [P, 2, 2, 2, 2, 64])
    ksq = sb("ksq", [P, 2, 2, P])
    vblk = sb("vblk", [P, 2, 2, 8, 2, 17])
    s_sb = sb("s_sb", [P, 16, 64])
    dif = sb("dif", [P, 16, 63])
    dd = sb("dd", [P, 16, 64])
    e1 = sb("e1", [P, 16, 64])
    ed = sb("ed", [P, 16, 64])
    e2 = sb("e2", [P, 8, P])
    pT = sb("pT", [P, 8, P])
    rows = sb("rows", [P, 2, 13, 16])
    MX, SUM, ABS, Z, RZ, SED, LNZ, KN2, KN, C, W, TA, TB = range(13)
    att = sb("att", [P, D])
    recw = sb("recw", [P, 2, 16])
    aT = sb("aT", [P, 2, P])
    x1 = sb("x1_tile", [P, 2, D])
    stats2 = sb("stats2", [P, 2, 8])
    ln2 = sb("ln2", [P, 2, 4])
    q = sb("q_tile", [P, D])
    r = sb("q_rest", [P, 2, D])
    qp = sb("q_part", [P, 2, 3, D], BF16)
    cr = sb("c_rest", [P, 2, D])
    cp = sb("c_part", [P, 2, 3, D], BF16)

    ps_x = pst(st, "ps_x", [P, 512])
    ps_qk = pst(st, "ps_qk", [P, 4, P])
    ps_v = pst(st, "ps_v", [P, 2, D])
    ps_s = pst(st, "ps_s", [P, 4, 512])
    ps_o = pst(st, "ps_o", [P, 512])

    x_loaded = [sm(f"x_loaded{i}") for i in range(4)]
    c_loaded = [sm(f"c_loaded{i}") for i in range(2)]
    small_in = sm("small_in")
    id_ready, setup_done, sig_done = sm("id_ready"), sm("setup_done"), sm("sig_done")
    zeros_done = sm("zeros_done")
    waits_met = sm("waits_met")
    dve_own, act_own = sm("dve_own"), sm("act_own")
    var1_ready, rs1_ready, var2_ready, rs2_ready = sm("var1_ready"), sm("rs1_ready"), sm("var2_ready"), sm("rs2_ready")
    xhat_ready, xT_done, hT_ready = sm("xhat_ready"), sm("xT_done"), sm("hT_ready")
    qk_done, v_done, qk_ready, v_ready = sm("qk_done"), sm("v_done"), sm("qk_ready"), sm("v_ready")
    kn_done, kn_read = sm("kn_done"), sm("kn_read")
    s_done, s_ready, max_ready, sum_done = sm("s_done"), sm("s_ready"), sm("max_ready"), sm("sum_done")
    dif_ready, d_ready, e1_ready, e2_ready, ed_ready = sm("dif_ready"), sm("d_ready"), sm("e1_ready"), sm("e2_ready"), sm("ed_ready")
    abs_done, z_ready, sed_done = sm("abs_done"), sm("z_ready"), sm("sed_done")
    logs_ready, w_arg, w_ready = sm("logs_ready"), sm("w_arg"), sm("w_ready")
    pT_done, pT_ready, o_done, att_ready = sm("pT_done"), sm("pT_ready"), sm("o_done"), sm("att_ready")
    aT_done, aT_ready, y_done, x1_ready = sm("aT_done"), sm("aT_ready"), sm("y_done"), sm("x1_ready")
    qp_ready = sm("qp_ready")
    rz_ready, xb_ready, pool_own = sm("rz_ready"), sm("xb_ready"), sm("pool_own")
    c_copied, c_rest, cp_ready = sm("c_copied"), sm("c_rest_ready"), sm("cp_ready")
    x1_stored = [sm(f"x1_stored{i}") for i in range(2)]
    qp_stored = [sm(f"qp_stored{i}") for i in range(2)]
    cp_stored = [sm(f"cp_stored{i}") for i in range(2)]
    N_STEADY = (3, TILES - 5)

    def bc(col, n):
        return col.unsqueeze(2).to_broadcast([P, 16, n])

    block = st.enter_context(nc.Block())

    @block.sync
    def _(sp):
        def load(u, s4, s2):
            row = u * P
            sp.dma_start(x[:, s4, :], x_in[bass.ds(row, P), :]).then_inc(x_loaded[s4], 16)

        sp.dma_start(x[:, 0, :], x_in[0:P, :]).then_inc(x_loaded[0], 16)
        for tile, name in ((ident, "ident"), (cst, "cst")):
            sp.dma_start(tile[:], t[name]).then_inc(small_in, 16)
        for tile, name in ((wq, "wqT"), (wk, "wkT"), (wv, "wvT"), (wo, "woT")):
            sp.dma_start(tile[:], t[name].rearrange("(c p) o -> p c o", p=P)).then_inc(weights_in, 16)
        for tile, name in ((bq, "bq"), (bk, "bk")):
            sp.dma_start(tile[:], t[name].rearrange("(c p) -> p c", p=P), allow_slow_non_contiguous=True).then_inc(small_in, 16)
        for tile, name in ((bv, "bv"), (bo, "bo")):
            a = t[name]
            sp.dma_start(tile[:], bass.AP(a.tensor, a.offset, [[0, P]] + list(a.ap))).then_inc(small_in, 16)
        for i, name in enumerate(("truth", "balance", "order", "justice", "harmony")):
            a = t[name]
            sp.dma_start(gates[:, i:i + 1], bass.AP(a.tensor, a.offset, [[0, P]] + list(a.ap))).then_inc(small_in, 16)
        a = t["gamma"]
        sp.dma_start(gamma[:], bass.AP(a.tensor, a.offset, [[0, P]] + list(a.ap))).then_inc(small_in, 16)
        load(1, 1, 1)
        load(2, 2, 0)
        sp.dma_start(g["iota8"][:], t["iota8"]).then_inc(ffn_in, 16)
        sp.dma_start(g["w1"][:], t["w1"].rearrange("e (c p) f -> p e c f", p=P)).then_inc(ffn_in, 16)
        sp.dma_start(g["w2"][:], t["w2"].rearrange("e (c p) f -> p e c f", p=P)).then_inc(ffn_in, 16)
        sp.dma_start(g["w3"][:], t["w3"].rearrange("e f d -> f e d")).then_inc(ffn_in, 16)
        sp.dma_start(g["rw"][:], t["rwT"].rearrange("(c p) e -> p c e", p=P)).then_inc(ffn_in, 16)

        def step(u, s, steady, over):
            s2 = s % 2
            if steady or 0 <= u < TILES:
                if steady or u >= 2:
                    sp.wait_ge(cp_ready, u - 1)
                sp.dma_start(c[:, s2, :], c_in[bass.ds(u * P, P), :]).then_inc(c_loaded[s2], 16)
            if steady or 0 <= u + 3 < TILES and u >= 0:
                if steady or u >= 1:
                    sp.wait_ge(x1_ready, u)
                load(u + 3, (s + 3) % 4, (s + 1) % 2)
            if steady or 1 <= u <= TILES:
                v, sv = u - 1, (s - 1) % 2
                sp.wait_ge(x1_ready, v + 1)
                sp.dma_start(x1_dram[bass.ds(v * P, P), :], x1[:, sv, :]).then_inc(x1_stored[sv], 16)
                sp.wait_ge(cp_ready, v + 1)
                for bb in range(2):
                    for i in range(3):
                        sp.dma_start(kp_dram[v * 2 + bb, i].rearrange("d h c -> h d c"),
                                     cp[64 * bb:64 * bb + 64, sv, i, :]).then_inc(cp_stored[sv], 16)
                sp.wait_ge(qp_ready, v + 1)
                for bb in range(2):
                    for i in range(3):
                        sp.dma_start(qp_dram[v * 2 + bb, :, i].rearrange("d h c -> h d c"),
                                     qp[64 * bb:64 * bb + 64, sv, i, :]).then_inc(qp_stored[sv], 16)

        run_steps(sp, step, 0, (4, TILES - 4), TILES + 1, 4)
        for i in range(2):
            sp.wait_ge(x1_stored[i], 16 * (TILES // 2))
            sp.wait_ge(qp_stored[i], 96 * (TILES // 2))
            sp.wait_ge(cp_stored[i], 96 * (TILES // 2))

    @block.tensor
    def _(pe):
        def project(u, s2, steady):
            pe.wait_ge(xhat_ready, u + 1)
            if steady or u >= 1:
                pe.wait_ge(hT_ready, u)
                pe.wait_ge(kn_read, u)
            for kc in range(2):
                last = nc.tensor.transpose(ps_x[:, kc * P:(kc + 1) * P], xhat[:, s2, kc * P:(kc + 1) * P], ident[:])
            last.then_inc(xT_done, 1)
            pe.wait_ge(hT_ready, u + 1)
            if steady or u >= 1:
                pe.wait_ge(qk_ready, u)
            for n, w in enumerate((wq, wk)):
                for m in range(2):
                    for kc in range(2):
                        last = nc.tensor.matmul(ps_qk[:, 2 * n + m, :], w[:, kc, m * P:(m + 1) * P],
                                                hT[:, s2, kc, :, 0, :], start=kc == 0, stop=kc == 1)
            last.then_inc(qk_done, 1)
            if steady or u >= 1:
                pe.wait_ge(v_ready, u)
            for b in range(2):
                for kc in range(2):
                    last = nc.tensor.matmul(ps_v[:, b, :], hT[:, s2, kc, b, :, :], wv[:, kc, :],
                                            start=kc == 0, stop=kc == 1)
            last.then_inc(v_done, 1)

        def finish(u):
            pe.wait_ge(att_ready, u + 1)
            for kc in range(2):
                last = nc.tensor.transpose(ps_o[:, kc * P:(kc + 1) * P], att[:, kc * P:(kc + 1) * P], ident[:])
            last.then_inc(aT_done, 1)
            pe.wait_ge(aT_ready, u + 1)
            for kc in range(2):
                last = nc.tensor.matmul(ps_o[:, 0:D], aT[:, kc, :], wo[:, kc, :], start=kc == 0, stop=kc == 1)
            last.then_inc(y_done, 1)

        def weights(u):
            pe.wait_ge(e2_ready, u + 1)
            for n in range(8):
                last = nc.tensor.transpose(ps_s[:, n // 4, (n % 4) * P:(n % 4 + 1) * P], e2[:, n, :], ident[:])
            last.then_inc(pT_done, 1)

        def times_v(u, s2, steady):
            pe.wait_ge(v_ready, u + 1)
            pe.wait_ge(pT_ready, u + 1)
            if steady or u >= 1:
                pe.wait_ge(x1_ready, u)
            for n in range(8):
                for b in range(2):
                    last = nc.tensor.matmul(ps_o[64 * b:64 * b + 64, n * 34:(n + 1) * 34],
                                            pT[:, n, 64 * b:64 * b + 64], vblk[:, s2, b, n, :, :],
                                            start=True, stop=True)
            last.then_inc(o_done, 1)

        def scores(u, s2, steady):
            pe.wait_ge(qk_ready, u + 1)
            for m in range(2):
                last = nc.tensor.matmul(ps_x[:, 256 + 8 * m:264 + 8 * m], ksq[:, s2, m, :], cst[:, 2:10],
                                        start=True, stop=True)
            last.then_inc(kn_done, 1)
            if steady or u >= 1:
                pe.wait_ge(pT_ready, u)
            for m in range(2):
                for b in range(2):
                    for j in range(4):
                        last = nc.tensor.matmul(ps_s[64 * b:64 * b + 64, j, m * P:(m + 1) * P],
                                                qT[32 * j:32 * j + 32, s2, m, 64 * b:64 * b + 64],
                                                kT[32 * j:32 * j + 32, s2, m, b, :, :], start=True, stop=True)
            last.then_inc(s_done, 1)

        def step(u, s, steady, over):
            if steady or u + 1 < TILES:
                project(u + 1, (s + 1) % 2, steady)
            if steady or 0 <= u < TILES:
                weights(u)
            if steady or 1 <= u <= TILES:
                finish(u - 1)
            if steady or u + 1 < TILES:
                scores(u + 1, (s + 1) % 2, steady)
            if steady or 0 <= u < TILES:
                times_v(u, s % 2, steady)

        pe.wait_ge(small_in, 12 * 16)
        pe.wait_ge(weights_in, 4 * 16)
        run_steps(pe, step, -1, N_STEADY, TILES + 1, 4)

    @block.scalar
    def _(act):
        link = Link(act, act_own)
        act.preload_act_table_set("natural_log_exp_and_others")
        act.wait_ge(small_in, 12 * 16)
        nc.scalar.activation(sig[:], gates[:], ACT.Exp, scale=-1.0).then_inc(sig_done, 1)
        act.wait_ge(setup_done, 1)
        nc.scalar.activation(coef[:, 5:6], coef[:, 5:6], ACT.Exp).then_inc(sig_done, 1)
        act.wait_ge(sig_done, 2)

        def rsqrt(v, ready, u, done):
            act.wait_ge(ready, u + 1)
            link(nc.scalar.activation(v[:, 1:2], v[:, 0:1], ACT.Ln))
            nc.scalar.activation(v[:, 2:3], v[:, 1:2], ACT.Exp, scale=-0.5).then_inc(done, 1)

        def step(u, s, steady, over):
            s2, n2 = s % 2, (s + 1) % 2
            here, ahead, behind = (steady or 0 <= u < TILES), (steady or -1 <= u < TILES - 1), (steady or 1 <= u <= TILES)
            if here:
                act.wait_ge(s_done, u + 1)
                if steady or u >= 1:
                    act.wait_ge(dif_ready, u)
                    act.wait_ge(d_ready, u)
                    act.wait_ge(sum_done, u)
                nc.scalar.activation(s_sb[:].rearrange("p (j h) k -> p j (h k)", j=4), ps_s[:, :, 0:256], ACT.Copy,
                                     scale=1.0 / math.sqrt(16)).then_inc(s_ready, 1)
            if ahead:
                act.wait_ge(xT_done, u + 2)
                if steady or u >= 1:
                    act.wait_ge(v_done, u)
                for i in range(2):
                    ins = nc.scalar.activation(hT[:, n2, :, :, i, :],
                                               ps_x[:, 0:256].rearrange("p (c b t) -> p c b t", c=2, b=2), ACT.Copy)
                ins.then_inc(hT_ready, 1)
            if behind:
                act.wait_ge(w_arg, u)
                nc.scalar.activation(rows[:, n2, W, :], rows[:, n2, TB, :], ACT.Exp).then_inc(w_ready, 1)
            if here:
                act.wait_ge(d_ready, u + 1)
                if steady or u >= 1:
                    act.wait_ge(pT_done, u)
                    act.wait_ge(ed_ready, u)
                    act.wait_ge(z_ready, u)
                nc.scalar.activation(e2[:].rearrange("p n k -> p (n k)"), dd[:].rearrange("p h k -> p (h k)"), ACT.Exp,
                                     scale=coef[:, 4:5]).then_inc(e2_ready, 1)
                nc.scalar.activation(e1[:], dd[:], ACT.Exp).then_inc(e1_ready, 1)
                act.wait_ge(c_loaded[s2], over(2) * 16 + 16)
                if steady or u >= 2:
                    act.wait_ge(cp_stored[s2], over(2) * 96)
                nc.scalar.activation(cp[:, s2, 0, :], c[:, s2, :], ACT.Copy).then_inc(c_copied, 1)
            if ahead:
                act.wait_ge(qk_done, u + 2)
                if steady or u >= 1:
                    act.wait_ge(s_done, u)
                for m in range(2):
                    nc.scalar.activation(qT[:, n2, m, :], ps_qk[:, m, :], ACT.Identity, bias=bq[:, m:m + 1])
                    for par in range(2):
                        nc.scalar.activation(kT[:, n2, m, :, par, :],
                                             ps_qk[:, 2 + m, :].rearrange("p (b k) -> p b k", b=2), ACT.Identity,
                                             bias=bkm[:, m, par:par + 1], scale=cst[:, par:par + 1])
                    ins = nc.scalar.activation(ksq[:, n2, m, :], ps_qk[:, 2 + m, :], ACT.Square, bias=bk[:, m:m + 1])
                ins.then_inc(qk_ready, 1)
            if steady or u + 2 < TILES:
                rsqrt(ln_s[:, s2, :], var1_ready, u + 2, rs1_ready)
            if here:
                act.wait_ge(pT_done, u + 1)
                if steady or u >= 1:
                    act.wait_ge(o_done, u)
                nc.scalar.activation(pT[:], ps_s[:, 0:2, :].rearrange("p a (n k) -> p (a n) k", k=P), ACT.Copy,
                                     scale=coef[:, 5:6]).then_inc(pT_ready, 1)
            if behind:
                act.wait_ge(aT_done, u)
                if steady or u >= 2:
                    act.wait_ge(y_done, u - 1)
                nc.scalar.activation(aT[:], ps_o[:, 0:256].rearrange("p (c t) -> p c t", c=2), ACT.Copy).then_inc(aT_ready, 1)
            if here:
                act.wait_ge(c_rest, 2 * u + 1)
                nc.scalar.activation(cp[:, s2, 1, :], cr[:, 0, :], ACT.Copy).then_inc(c_copied, 1)
                act.wait_ge(z_ready, u + 1)
                link(nc.scalar.activation(rows[:, s2, LNZ, :], rows[:, s2, Z, :], ACT.Ln))
                act.wait_ge(kn_read, u + 1)
                link(nc.scalar.activation(rows[:, s2, KN, :], rows[:, s2, KN2, :], ACT.Ln))
                nc.scalar.activation(rows[:, s2, KN, :], rows[:, s2, KN, :], ACT.Exp, scale=0.5).then_inc(logs_ready, 1)
            if behind:
                rsqrt(ln2[:, n2, :], var2_ready, u - 1, rs2_ready)
            if here:
                act.wait_ge(c_rest, 2 * u + 2)
                nc.scalar.activation(cp[:, s2, 2, :], cr[:, 1, :], ACT.Copy).then_inc(cp_ready, 1)

        run_steps(act, step, -2, N_STEADY, TILES + 1, 4, link, 4 * 4)

    @block.gpsimd
    def _(pool):
        link = Link(pool, pool_own)
        tt = nc.gpsimd.tensor_tensor

        def step(u, s, steady, over):
            s2, s4 = s % 2, s % 4
            R = rows[:, s2]
            pool.wait_ge(s_ready, u + 1)
            pool.wait_ge(max_ready, u + 1)
            if steady or u >= 1:
                pool.wait_ge(e1_ready, u)
            tt(dd[:], s_sb[:], bc(R[:, MX, :], 64), ALU.subtract).then_inc(d_ready, 1)
            if steady or u >= 1:
                pool.wait_ge(abs_done, u)
            tt(dif[:], s_sb[:, :, 1:64], s_sb[:, :, 0:63], ALU.subtract).then_inc(dif_ready, 1)
            pool.wait_ge(e1_ready, u + 1)
            pool.wait_ge(d_ready, u + 1)
            if steady or u >= 1:
                pool.wait_ge(sed_done, u)
            tt(ed[:], e1[:], dd[:], ALU.mult).then_inc(ed_ready, 1)
            pool.wait_ge(c_copied, 2 * u + 1)
            tt(cr[:, 0, :], c[:, s2, :], cp[:, s2, 0, :], ALU.subtract).then_inc(c_rest, 1)
            pool.wait_ge(xhat_ready, u + 1)
            tt(x[:, s4, :], x[:, s4, :], bo[:], ALU.add).then_inc(xb_ready, 1)
            pool.wait_ge(c_copied, 2 * u + 2)
            pool.wait_ge(c_rest, 2 * u + 1)
            tt(cr[:, 1, :], cr[:, 0, :], cp[:, s2, 1, :], ALU.subtract).then_inc(c_rest, 1)
            pool.wait_ge(rz_ready, u + 1)
            pool.wait_ge(sed_done, u + 1)
            pool.wait_ge(logs_ready, u + 1)
            link(tt(R[:, TA, :], R[:, RZ, :], R[:, SED, :], ALU.mult))
            link(tt(R[:, TA, :], R[:, LNZ, :], R[:, TA, :], ALU.subtract))
            link(tt(R[:, TA, :], R[:, TA, :], cf[:, 1, :], ALU.mult))
            link(tt(R[:, C, :], R[:, KN, :], cf[:, 0, :], ALU.mult))
            link(tt(R[:, C, :], R[:, C, :], R[:, TA, :], ALU.add))
            for i, n in ((2, SUM), (3, ABS)):
                link(tt(R[:, TA, :], R[:, n, :], cf[:, i, :], ALU.mult))
                link(tt(R[:, C, :], R[:, C, :], R[:, TA, :], ALU.add))
            link(tt(R[:, TB, :], R[:, MX, :], cf[:, 4, :], ALU.mult))
            link(tt(R[:, TA, :], R[:, TB, :], R[:, C, :], ALU.add))
            link(tt(R[:, C, :], R[:, C, :], R[:, TA, :], ALU.subtract))
            tt(R[:, TB, :], R[:, C, :], R[:, TB, :], ALU.add).then_inc(w_arg, 1)

        pool.wait_ge(small_in, 12 * 16)
        pool.wait_ge(setup_done, 1)
        run_steps(pool, step, 0, (4, TILES - 4), TILES, 4, link, 4 * 12)

    @block.vector
    def _(dve):
        link = Link(dve, dve_own)
        link(nc.vector.memset(vblk[:], 0.0))
        nc.vector.memset(vblk[0:64, :, :, :, 0, 16:17], 1.0).then_inc(zeros_done, 1)
        nc.vector.memset(vblk[64:128, :, :, :, 1, 16:17], 1.0).then_inc(zeros_done, 1)
        dve.wait_ge(zeros_done, 2)
        dve.wait_ge(small_in, 12 * 16)
        link(nc.vector.tensor_copy(ident16[:], ident[:]))
        dve.wait_ge(sig_done, 1)
        link(nc.vector.tensor_scalar(sig[:], sig[:], 1.0, None, ALU.add))
        link(nc.vector.reciprocal(sig[:], sig[:]))
        for i, (gate, f) in enumerate(((0, -0.01), (1, 0.1 / math.log(64)), (3, 0.1 / 64), (4, -0.1 / 63))):
            link(nc.vector.tensor_scalar(coef[:, i:i + 1], sig[:, gate:gate + 1], f, None, ALU.mult))
        link(nc.vector.tensor_scalar(coef[:, 4:5], sig[:, 3:4], -0.1, 1.0, ALU.mult, ALU.add))
        for i in range(5):
            link(nc.vector.tensor_copy(cf[:, i, :], coef[:, i:i + 1].to_broadcast([P, 16])))
        link(nc.vector.tensor_scalar(coef[:, 5:6], cst[:, 10:11], sig[:, 2:3], 0.05, ALU.mult, ALU.mult))
        for par in range(2):
            link(nc.vector.tensor_scalar(bkm[:, :, par], bk[:], cst[:, par:par + 1], None, ALU.mult))
        nc.vector.tensor_scalar(bkm[:, :, 0], bk[:], cst[:, 0:1], None, ALU.mult).then_inc(setup_done, 1)
        dve.wait_ge(setup_done, 1)

        def ln_stats(src, stt, v, ready):
            link(nc.vector.bn_stats(stt[:, 0:6], src))
            dve.sem_inc(waits_met, 1)
            link(nc.vector.bn_aggr(stt[:, 6:8], stt[:, 0:6]))
            nc.vector.tensor_scalar(v[:, 0:1], stt[:, 7:8], EPS, None, ALU.add).then_inc(ready, 1)

        def ln_apply(dst, src, stt, v):
            link(nc.vector.scalar_tensor_tensor(out=v[:, 3:4], in0=v[:, 2:3], scalar=v[:, 2:3], in1=v[:, 0:1],
                                                op0=ALU.mult, op1=ALU.mult))
            link(nc.vector.tensor_scalar(v[:, 3:4], v[:, 3:4], -0.5, 1.5, ALU.mult, ALU.add))
            link(nc.vector.tensor_tensor(v[:, 3:4], v[:, 3:4], v[:, 2:3], ALU.mult))
            return nc.vector.tensor_scalar(dst, src, stt[:, 6:7], v[:, 3:4], ALU.subtract, ALU.mult)

        def step(u, s, steady, over):
            s2, n2 = s % 2, (s + 1) % 2
            here, ahead, behind = (steady or 0 <= u < TILES), (steady or -1 <= u < TILES - 1), (steady or 1 <= u <= TILES)
            ahead2 = steady or u + 2 < TILES
            R = rows[:, s2]
            if here:
                dve.wait_ge(s_ready, u + 1)
                nc.vector.tensor_reduce(R[:, MX, :], s_sb[:], AX_X, ALU.max).then_inc(max_ready, 1)
                nc.vector.tensor_reduce(R[:, SUM, :], s_sb[:], AX_X, ALU.add).then_inc(sum_done, 1)
            if behind:
                dve.wait_ge(o_done, u)
                dve.wait_ge(w_ready, u)
                Rb = rows[:, n2]
                o = ps_o[:, 0:272].rearrange("p (h e) -> p h e", e=17)
                link(nc.vector.tensor_tensor(recw[:, 0, :], o[:, :, 16], Rb[:, W, :], ALU.mult))
                link(nc.vector.reciprocal(recw[:, 1, :], recw[:, 0, :]))
                link(nc.vector.tensor_tensor(recw[:, 1, :], recw[:, 1, :], Rb[:, W, :], ALU.mult))
                for m in range(2):
                    om = o.rearrange("p (j m r) e -> p m j r e", j=4, m=2)[:, m, :, :, 0:16]
                    rm = recw[:, 1, :].rearrange("p (j m r) -> p m j r", j=4, m=2)[:, m].unsqueeze(3).to_broadcast([P, 4, 2, 16])
                    am = att[:, m * P:(m + 1) * P].rearrange("p (j r e) -> p j r e", j=4, r=2)
                    ins = nc.vector.tensor_tensor(am, om, rm, ALU.mult)
                    if m == 0:
                        link(ins)
                ins.then_inc(att_ready, 1)
            if ahead2:
                s4 = (s + 2) % 4
                dve.wait_ge(x_loaded[s4], over(4, 2) * 16 + 16)
                if steady or u >= 0:
                    dve.wait_ge(rs1_ready, u + 1)
                ln_stats(x[:, s4, :], stats[:, s2, :], ln_s[:, s2, :], var1_ready)
            if here:
                dve.wait_ge(dif_ready, u + 1)
                nc.vector.tensor_reduce(R[:, ABS, :], dif[:], AX_X, ALU.add, apply_absolute_value=True).then_inc(abs_done, 1)
                dve.wait_ge(e1_ready, u + 1)
                nc.vector.tensor_reduce(R[:, Z, :], e1[:], AX_X, ALU.add).then_inc(z_ready, 1)
            if ahead:
                dve.wait_ge(v_done, u + 2)
                if steady or u >= 1:
                    dve.wait_ge(o_done, u)
                for par in range(2):
                    rr = slice(64 * par, 64 * par + 64)
                    for b in range(2):
                        o = vblk[rr, n2, b, :, par, 0:16].rearrange("p (j m) e -> p m j e", m=2)
                        i0 = ps_v[rr, b, :].rearrange("p (m j r e) -> p m j r e", m=2, j=4, r=2)[:, :, :, par]
                        i1 = bv[rr, :].rearrange("p (m j r e) -> p m j r e", m=2, j=4, r=2)[:, :, :, par]
                        ins = nc.vector.tensor_tensor(o, i0, i1, ALU.add)
                        if (par, b) != (1, 1):
                            link(ins)
                ins.then_inc(v_ready, 1)
            if here:
                dve.wait_ge(z_ready, u + 1)
                nc.vector.reciprocal(R[:, RZ, :], R[:, Z, :]).then_inc(rz_ready, 1)
                dve.wait_ge(ed_ready, u + 1)
                nc.vector.tensor_reduce(R[:, SED, :], ed[:], AX_X, ALU.add).then_inc(sed_done, 1)
            if ahead2:
                dve.wait_ge(rs1_ready, u + 3)
                dve.wait_ge(var1_ready, u + 3)
                if steady or u >= 0:
                    dve.wait_ge(xT_done, u + 1)
                ln_apply(xhat[:, s2, :], x[:, s4, :], stats[:, s2, :], ln_s[:, s2, :]).then_inc(xhat_ready, 1)
            if behind:
                sx = (s - 1) % 4
                dve.wait_ge(y_done, u)
                dve.wait_ge(xb_ready, u)
                if steady or u >= 3:
                    dve.wait_ge(x1_stored[n2], over(2, -1) * 16)
                link(nc.vector.tensor_tensor(x1[:, n2, :], ps_o[:, 0:D], x[:, sx, :], ALU.add))
                nc.vector.bn_stats(stats2[:, n2, 0:6], x1[:, n2, :]).then_inc(x1_ready, 1)
                dve.wait_ge(x1_ready, u)
                dve.sem_inc(waits_met, 1)
                link(nc.vector.bn_aggr(stats2[:, n2, 6:8], stats2[:, n2, 0:6]))
                nc.vector.tensor_scalar(ln2[:, n2, 0:1], stats2[:, n2, 7:8], EPS, None, ALU.add).then_inc(var2_ready, 1)
            if ahead:
                dve.wait_ge(kn_done, u + 2)
                if steady or u >= 1:
                    dve.wait_ge(logs_ready, u)
                nc.vector.tensor_scalar(rows[:, n2, KN2, :].rearrange("p (j m r) -> p m j r", j=4, m=2),
                                        ps_x[:, 256:272].rearrange("p (m j r) -> p m j r", m=2, j=4), 1e-18, None,
                                        ALU.max).then_inc(kn_read, 1)
            if behind:
                dve.wait_ge(rs2_ready, u)
                dve.wait_ge(var2_ready, u)
                link(ln_apply(q[:], x1[:, n2, :], stats2[:, n2, :], ln2[:, n2, :]))
                if steady or u >= 3:
                    dve.wait_ge(qp_stored[n2], over(2, -1) * 96)
                link(nc.vector.tensor_copy(qp[:, n2, 0, :], q[:]))
                link(nc.vector.tensor_tensor(r[:, 0, :], q[:], qp[:, n2, 0, :], ALU.subtract))
                link(nc.vector.tensor_copy(qp[:, n2, 1, :], r[:, 0, :]))
                link(nc.vector.tensor_tensor(r[:, 1, :], r[:, 0, :], qp[:, n2, 1, :], ALU.subtract))
                nc.vector.tensor_copy(qp[:, n2, 2, :], r[:, 1, :]).then_inc(qp_ready, 1)

        PER = 4 + 2 + 3 + 3 + 2 + 4 + 4
        run_steps(dve, step, -2, N_STEADY, TILES + 1, 4, link, 4 * PER)


def phase2(nc, t, st, sbt, pst, sem, g):
    B, S, D = g["B"], g["S"], g["D"]
    HX = 8
    ident16, gamma = g["ident16"], g["gamma"]
    x1_dram, x2_dram, qp_dram, kp_dram, o_dram = (g[k] for k in ("x1_dram", "x2_dram", "qp_dram", "kp_dram", "o_dram"))
    SCALE = 1.0 / math.sqrt(S // HX)
    PAIRS = B // 2

    def sb(name, shape, dt=F32):
        return sbt(st, name, shape, dt)

    def sm(name):
        return sem(st, name)

    ks = sb("ks", [P, 4, HX, D], BF16)
    qs = sb("qs", [P, 4, HX, D], BF16)
    vT = sb("vT", [P, 4, 2, 64])
    vaug = sb("vaug", [P, 4, 2, HX, 32])
    mx = sb("mx", [P, 2, 16])
    mp = sb("mp", [P, 2, 48], BF16)
    mr = sb("mr", [P, 2, 16])
    mT = sb("mT", [48, 2, P], BF16)
    pr = sb("pr", [P, 2, 4, 2, D])
    o_sb = sb("o_sb", [P, 2, 2, D])
    num = sb("num", [P, 2, D])
    den = sb("den", [P, 2, D])
    r0 = sb("r0", [P, D])
    ra = sb("ra", [P, D])
    lnd = sb("lnd", [P, D])
    ones, twos, minus, gammas = sb("ones", [P, D]), sb("twos", [P, D]), sb("minus", [P, 16]), sb("gammas", [P, D])
    x1 = sb("x1_in", [P, 2, D])
    x2 = sb("x2_tile", [P, 2, D])

    ps_s = pst(st, "ps2_s", [P, 2, 2, D])
    ps_t = pst(st, "ps2_t", [P, 2, 2, 2, D])
    ps_o = pst(st, "ps2_o", [P, 2, D])
    ps_m = pst(st, "ps2_m", [P, P * 4], BF16)

    zero_done, ones_done = sm("zero_done"), sm("ones_done")
    act_own, pool_own, r0_ready = sm("act2_own"), sm("pool2_own"), sm("r0_ready")
    dve_own = sm("dve2_own")
    waits_met, sp_waits_met = sm("waits2_met"), sm("sp_waits_met")
    kq_loaded = [sm(f"kq_loaded{i}") for i in range(4)]
    v_loaded = [sm(f"v_loaded{i}") for i in range(2)]
    m_loaded = [sm(f"m_loaded{i}") for i in range(4)]
    x1_loaded = [sm(f"x1_loaded{i}") for i in range(2)]
    o_moved = [sm(f"o_moved{i}") for i in range(4)]
    o_stored = [sm(f"o_stored{i}") for i in range(2)]
    x2_stored = [sm(f"x2_stored{i}") for i in range(2)]
    s_ready, max_done, mp_ready, mT_done, mT_ready = sm("s2_ready"), sm("max2_done"), sm("mp_ready"), sm("mT_done"), sm("mT_ready")
    st_ready, exp_done, pv_done, o_ready = sm("st_ready"), sm("exp_done"), sm("pv_done"), sm("o_ready")
    vaug_ready, x2_ready = sm("vaug_ready"), sm("x2_ready")
    STEADY = (7, B - 5)

    def slot_value(b, slot, slots, steady, each):
        return (b // slots + 1) * each if not steady else (b - slot) * (each // slots) + each

    block = st.enter_context(nc.Block())

    @block.sync
    def _(sp):
        def load(b, s):
            k, q = kp_dram[b].rearrange("i d h c -> (i d) (h c)"), qp_dram[b].rearrange("d i h c -> (d i) (h c)")
            ki = list(k.ap)
            sp.dma_start(ks[0:72, s, :, :].rearrange("p h c -> p (h c)"),
                         bass.AP(k.tensor, k.offset, [ki[0], [0, 3], ki[1]])).then_inc(kq_loaded[s], 16)
            sp.dma_start(qs[0:72, s, :, :].rearrange("p h c -> p (h c)"),
                         bass.AP(q.tensor, q.offset, [[0, 3]] + list(q.ap))).then_inc(kq_loaded[s], 16)

        def load_v(b, p):
            for i in range(2):
                sp.dma_start(vT[:, 2 * p + i, :, :], t["ctxT"][b + i].rearrange("(c l) r -> l c r", c=2))\
                    .then_inc(v_loaded[p], 16)

        def step(b, s, steady, over):
            if steady or 0 <= b < B - 3:
                if steady or b >= 1:
                    sp.wait_ge(st_ready, b * 4)
                load(b + 3, (s + 3) % 4)
            if s % 2 == 1 and (steady or 1 <= b < B - 4):
                sp.wait_ge(vaug_ready, b + 1)
                load_v(b + 3, ((s + 3) // 2) % 2)
            if s % 2 == 1 and (steady or 0 <= b < B):
                p = (s // 2) % 2
                if steady or b >= 5:
                    sp.wait_ge(x2_ready, over(2, -3))
                sp.dma_start(x1[:, p, :], x1_dram[bass.ds((b - 1) * S, P), :]).then_inc(x1_loaded[p], 16)
            if steady or 2 <= b < B + 2:
                v, sv = b - 2, s % 2
                pp = (((s - 2) % 4) // 2) % 2
                sp.wait_ge(o_stored[sv], over(2) * 16)
                if steady or b >= 6:
                    sp.sem_inc(sp_waits_met, 1)
                    sp.wait_ge(x2_ready, over(2, -4))
                src = o_dram[v].rearrange("f p c -> (f p) c").rearrange("(j w r) c -> w j r c", j=8, w=4)
                sp.dma_start(num[64 * sv:64 * sv + 64, pp, :], src[0]).then_inc(o_moved[2 * pp + sv], 16)
                sp.dma_start(den[64 * sv:64 * sv + 64, pp, :], src[1]).then_inc(o_moved[2 * pp + sv], 16)
            if steady or 0 <= b + 1 < B:
                n = (s + 1) % 4
                sp.wait_ge(mT_ready, b + 2)
                sp.dma_start(qs[96:99, n, :, :].rearrange("p h (c q) -> p (h c) q", c=2),
                             mT[:, n % 2, :]).then_inc(m_loaded[n], 16)
            if s % 2 == 1 and (steady or 3 <= b < B + 2):
                store(b - 2, over(2, -3), (((s - 5) % 4) // 2) % 2) if (steady or b >= 5) else None

        def store(b, count, p):
            sp.wait_ge(x2_ready, count)
            sp.dma_start(x2_dram[bass.ds((b - 3) * S, P), :], x2[:, p, :]).then_inc(x2_stored[p], 16)

        sp.wait_ge(ones_done, 3)
        for b in range(3):
            load(b, b)
        load_v(0, 0)
        load_v(2, 1)
        run_steps(sp, step, -1, STEADY, B + 2, 4)
        store(B + 1, PAIRS, (PAIRS - 1) % 2)
        for i in range(2):
            sp.wait_ge(x2_stored[i], 16 * (PAIRS // 2))

    @block.tensor
    def _(pe):
        def weigh(b, s, hf, steady):
            n = 2 * b + hf
            pe.wait_ge(exp_done, 2 * n + 2)
            if hf == 0:
                pe.wait_ge(vaug_ready, b + 1)
                if steady or b >= 1:
                    pe.wait_ge(o_ready, b)
            for lc in range(2):
                for j in range(4):
                    last = nc.tensor.matmul(ps_o[32 * j:32 * j + 32, hf, :], vaug[:, s, lc, 4 * hf + j, :],
                                            pr[:, hf, j, lc, :], start=lc == 0, stop=lc == 1)
            last.then_inc(pv_done, 1)

        def step(b, s, steady, over):
            here, ahead = (steady or 0 <= b < B), (steady or b + 2 < B)
            if here:
                pe.wait_ge(m_loaded[s], slot_value(b, s, 4, steady, 16))
            if ahead:
                sa = (s + 2) % 4
                pe.wait_ge(kq_loaded[sa], slot_value(b + 2, sa, 4, steady, 32))
            for p in range(4):
                if here:
                    u = 4 * b + p
                    if steady or u >= 2:
                        pe.wait_ge(exp_done, u - 1)
                    for h in (2 * p, 2 * p + 1):
                        for lc in range(2):
                            last = nc.tensor.matmul(ps_t[:, p % 2, h % 2, lc, :], ks[:, s, h, lc * P:(lc + 1) * P],
                                                    qs[:, s, h, :], start=True, stop=True)
                    last.then_inc(st_ready, 1)
                if ahead:
                    for h in (2 * p, 2 * p + 1):
                        v = 8 * (b + 2) + h
                        if steady or v >= 2:
                            pe.wait_ge(max_done, v - 1)
                        for c in range(2):
                            last = nc.tensor.matmul(ps_s[:, h % 2, c, :], qs[0:96, sa, h, c * P:(c + 1) * P],
                                                    ks[0:96, sa, h, :], start=True, stop=True)
                        last.then_inc(s_ready, 1)
                if p == 0 and (steady or 1 <= b <= B):
                    weigh(b - 1, (s - 1) % 4, 1, steady)
                if p == 1 and (steady or 0 <= b + 1 < B):
                    n = (s + 1) % 2
                    pe.wait_ge(mp_ready, b + 2)
                    if steady or b >= 0:
                        pe.wait_ge(mT_ready, b + 1)
                    pe.sem_inc(waits_met, 1)
                    nc.tensor.transpose(ps_m[0:48, 0:P], mp[:, n, :], ident16[:]).then_inc(mT_done, 1)
                if p == 2 and here:
                    weigh(b, s, 0, steady)

        run_steps(pe, step, -2, STEADY, B + 1, 4)

    @block.scalar
    def _(act):
        link = Link(act, act_own)
        act.preload_act_table_set("natural_log_exp_and_others")

        def step(b, s, steady, over):
            here = steady or 0 <= b < B
            for p in range(4):
                if here:
                    u = 4 * b + p
                    act.wait_ge(st_ready, u + 1)
                    if steady or 2 * b + p // 2 >= 2:
                        act.wait_ge(pv_done, 2 * b + p // 2 - 1)
                    nc.scalar.activation(pr[:, p // 2, 2 * (p % 2):2 * (p % 2) + 2, :, :], ps_t[:, p % 2, :, :, :],
                                         ACT.Exp, scale=SCALE).then_inc(exp_done, 1)
                if p == 1 and (steady or 0 <= b + 1 < B):
                    n = (s + 1) % 2
                    act.wait_ge(mT_done, b + 2)
                    if steady or b >= 1:
                        m = (s - 1) % 4
                        act.wait_ge(m_loaded[m], slot_value(b - 1, m, 4, steady, 16))
                    nc.scalar.activation(mT[:, n, :], ps_m[0:48, 0:P], ACT.Copy).then_inc(mT_ready, 1)
                if p == 1 and (steady or 1 <= b <= B):
                    v, sv = b - 1, (s - 1) % 2
                    act.wait_ge(pv_done, 2 * v + 2)
                    if steady or v >= 2:
                        act.wait_ge(o_stored[sv], over(2, -1) * 16)
                    nc.scalar.activation(o_sb[:, sv, :, :], ps_o[:], ACT.Copy).then_inc(o_ready, 1)
                    act.wait_ge(o_ready, v + 1)
                    act.dma_start(o_dram[v].rearrange("f p c -> p f c"), o_sb[:, sv, :, :]).then_inc(o_stored[sv], 16)
            if s % 2 == 1 and (steady or 3 <= b < B + 2):
                p = (((s - 3) % 4) // 2) % 2
                for bb in range(2):
                    act.wait_ge(o_moved[2 * p + bb], over(4, 1) * 32)
                link(nc.scalar.activation(lnd[:], den[:, p, :], ACT.Ln))
                if steady or b >= 5:
                    act.wait_ge(x2_ready, over(2, -3))
                nc.scalar.activation(r0[:], lnd[:], ACT.Exp, scale=-1.0).then_inc(r0_ready, 1)
                act.wait_ge(r0_ready, over(2, -1))

        run_steps(act, step, -1, STEADY, B + 2, 4, link, 2)

    @block.gpsimd
    def _(pool):
        nc.gpsimd.memset(vaug[:], 0.0).then_inc(zero_done, 1)
        pool.wait_ge(zero_done, 1)
        nc.gpsimd.memset(vaug[:, :, :, :, 8:16], 1.0).then_inc(zero_done, 1)
        for tile, v in ((ones, 1.0), (minus, -1.0), (twos, 2.0)):
            nc.gpsimd.memset(tile[:], v).then_inc(zero_done, 1)
        nc.gpsimd.tensor_copy(gammas[:], gamma[:, 0:1].to_broadcast([P, D])).then_inc(zero_done, 1)
        pool.wait_ge(zero_done, 6)

        link = Link(pool, pool_own)
        tt = nc.gpsimd.tensor_tensor

        def step(b, s, steady, over):
            if steady or 0 <= b + 1 < B:
                a = (s + 1) % 4
                pool.wait_ge(v_loaded[a // 2], over(4, 1) * 32 + 32)
                if steady or b >= 3:
                    pool.wait_ge(pv_done, 2 * (b - 3) + 2)
                tt(vaug[:, a, :, :, 0:8], vT[:, a, :, :].rearrange("p c (h d) -> p c h d", h=HX),
                   ones[:, 0:128].rearrange("p (c h d) -> p c h d", c=2, h=HX), ALU.mult).then_inc(vaug_ready, 1)
            if s % 2 == 1 and (steady or 3 <= b < B + 2):
                p = (((s - 3) % 4) // 2) % 2
                pool.wait_ge(r0_ready, over(2, -1))
                pool.wait_ge(x1_loaded[p], over(4, 1) * 16)
                link(tt(ra[:], den[:, p, :], r0[:], ALU.mult))
                link(tt(ra[:], twos[:], ra[:], ALU.subtract))
                link(tt(ra[:], ra[:], r0[:], ALU.mult))
                link(tt(ra[:], ra[:], num[:, p, :], ALU.mult))
                link(tt(ra[:], ra[:], gammas[:], ALU.mult))
                if steady or b >= 7:
                    pool.wait_ge(x2_stored[p], over(4, -3) * 16)
                tt(x2[:, p, :], ra[:], x1[:, p, :], ALU.add).then_inc(x2_ready, 1)
                pool.wait_ge(x2_ready, over(2, -1))

        run_steps(pool, step, -2, STEADY, B + 2, 4, link, 2 * 5)

    @block.vector
    def _(dve):
        link = Link(dve, dve_own)
        nc.vector.memset(ks[:], 0.0).then_inc(ones_done, 1)
        nc.vector.memset(qs[:], 0.0).then_inc(ones_done, 1)
        dve.wait_ge(ones_done, 2)
        nc.vector.memset(ks[96:99, :, :, :], 1.0).then_inc(ones_done, 1)

        def step(b, s, steady, over):
            if steady or b + 2 < B:
                n = (s + 2) % 2
                for h in range(HX):
                    dve.wait_ge(s_ready, 8 * (b + 2) + h + 1)
                    nc.vector.tensor_reduce(mx[:, n, 2 * h:2 * h + 2], ps_s[:, h % 2, :, :], AX_X, ALU.max).then_inc(max_done, 1)
                dve.wait_ge(max_done, 8 * (b + 2) + 8)
                if steady or b >= 0:
                    dve.wait_ge(mT_done, b + 1)
                part = [mp[:, n, 16 * i:16 * i + 16] for i in range(3)]
                link(nc.vector.tensor_scalar(part[0], mx[:, n, :], -1.0, None, ALU.mult))
                link(nc.vector.scalar_tensor_tensor(out=mr[:, 0, :], in0=mx[:, n, :], scalar=-1.0, in1=part[0],
                                                    op0=ALU.mult, op1=ALU.subtract))
                link(nc.vector.tensor_copy(part[1], mr[:, 0, :]))
                link(nc.vector.tensor_tensor(mr[:, 1, :], mr[:, 0, :], part[1], ALU.subtract))
                nc.vector.tensor_copy(part[2], mr[:, 1, :]).then_inc(mp_ready, 1)

        run_steps(dve, step, -2, STEADY, B - 2, 4, link, 4 * 4)


def phase3(nc, t, st, sbt, pst, sem, g):
    D = g["D"]
    E, TOK, BL = 8, 512, 4
    T = g["B"] * g["S"] // TOK
    ident, w1, w2, w3, rw, iota8 = (g[k] for k in ("ident", "w1", "w2", "w3", "rw", "iota8"))
    x2_dram, out, ffn_in = g["x2_dram"], g["out"], g["ffn_in"]

    def sb(name, shape, dt=F32):
        return sbt(st, name, shape, dt)

    def sm(name):
        return sem(st, name)

    x = sb("x2_in", [P, 2, BL, D])
    xn = sb("xn", [P, BL, D])
    xnT = sb("xnT", [P, 2, 2, TOK])
    stats = sb("stats3", [P, BL, 6])
    mv = sb("mv3", [P, BL, 2])
    v3 = sb("v3", [P, 4, BL])
    lg = sb("logits", [P, BL, E])
    top = sb("top", [P, BL, 8])
    idx = sb("idx", [P, BL, 8], U32)
    idf = sb("idf", [P, BL, 8])
    dl = sb("dl", [P, 3, BL])
    wt = sb("wt", [P, 2, BL, E])
    wtb = sb("wtb", [P, BL, E])
    sg = sb("sg", [P, 2, TOK])
    hh = sb("hh", [P, 2, TOK])
    acc = sb("acc", [P, 2, BL, D])

    ps_g = pst(st, "ps_g", [P, 2, TOK])
    ps_v = pst(st, "ps3_v", [P, 2, TOK])
    ps_y = pst(st, "ps_y", [P, BL, D])
    ps_x = pst(st, "ps3_x", [P, TOK])
    ps_l = pst(st, "ps_l", [P, 512])

    x_loaded = [sm(f"x2_loaded{i}") for i in range(2)]
    stored = [sm(f"out_stored{i}") for i in range(2)]
    own = sm("dve3_own")
    waits_met = sm("waits3_met")
    act_own = sm("act3_own")
    var_ready, rs_ready, xn_ready = sm("var3_ready"), sm("rs3_ready"), sm("xn_ready")
    xT_done, xT_ready, lg_done, dl_ready, tw_ready, wt_ready = (sm(n) for n in (
        "xT3_done", "xT3_ready", "lg_done", "dl_ready", "tw_ready", "wt_ready"))
    gv_done, sg_ready, hh_ready, y_done, acc_done = (sm(n) for n in ("gv_done", "sg_ready", "hh_ready", "y3_done", "acc_done"))
    STEADY = (1, T - 1)

    block = st.enter_context(nc.Block())

    @block.sync
    def _(sp):
        def rows(ap, k):
            return ap[bass.ds(k * TOK, TOK), :].rearrange("(n p) d -> p n d", p=P)

        def step(k, s, steady, over):
            if steady or k + 1 < T:
                n = (s + 1) % 2
                if steady or k >= 1:
                    sp.wait_ge(acc_done, 8 * (k - 1) + 1)
                sp.dma_start(x[:, n, :, :], rows(x2_dram, k + 1)).then_inc(x_loaded[n], 16)
            if steady or k >= 1:
                sp.wait_ge(acc_done, 8 * k)
                sp.dma_start(rows(out, k - 1), acc[:, (s - 1) % 2, :, :]).then_inc(stored[(s - 1) % 2], 16)

        run_steps(sp, step, -1, STEADY, T + 1, 2)
        for i in range(2):
            sp.wait_ge(stored[i], 16 * (T // 2))

    @block.tensor
    def _(pe):
        def prep(k, s):
            pe.wait_ge(xn_ready, k + 1)
            for kc in range(2):
                if kc == 1:
                    pe.wait_ge(xT_ready, 2 * k + 1)
                for n in range(BL):
                    last = nc.tensor.transpose(ps_x[:, n * P:(n + 1) * P], xn[:, n, kc * P:(kc + 1) * P], ident[:])
                last.then_inc(xT_done, 1)

        def logits(k, s, steady):
            pe.wait_ge(xT_ready, 2 * k + 2)
            for n in range(BL):
                for kc in range(2):
                    last = nc.tensor.matmul(ps_l[:, n * E:(n + 1) * E], xnT[:, s, kc, n * P:(n + 1) * P], rw[:, kc, :],
                                            start=kc == 0, stop=kc == 1)
            last.then_inc(lg_done, 1)

        def expert_out(k, e, steady):
            n = 8 * k + e
            pe.wait_ge(hh_ready, n + 1)
            if steady or n >= 1:
                pe.wait_ge(acc_done, n)
            for bl in range(BL):
                last = nc.tensor.matmul(ps_y[:, bl, :], hh[:, e % 2, bl * P:(bl + 1) * P], w3[:, e, :],
                                        start=True, stop=True)
            last.then_inc(y_done, 1)

        def step(k, s, steady, over):
            here, ahead = (steady or 0 <= k < T), (steady or k + 1 < T)
            for e in range(E):
                if here:
                    n = 8 * k + e
                    if steady or n >= 2:
                        pe.wait_ge(hh_ready, n - 1)
                    if e == 0:
                        pe.wait_ge(xT_ready, 2 * k + 2)
                    for ps, w in ((ps_g, w1), (ps_v, w2)):
                        for kc in range(2):
                            last = nc.tensor.matmul(ps[:, e % 2, :], w[:, e, kc, :], xnT[:, s, kc, :],
                                                    start=kc == 0, stop=kc == 1)
                    last.then_inc(gv_done, 1)
                if e == 0 and (steady or k >= 1):
                    expert_out(k - 1, E - 1, steady)
                if here and e >= 1:
                    expert_out(k, e - 1, steady)
                if ahead and e == 4:
                    prep(k + 1, (s + 1) % 2)
                if ahead and e == 6:
                    logits(k + 1, (s + 1) % 2, steady)

        pe.wait_ge(ffn_in, 5 * 16)
        run_steps(pe, step, -1, STEADY, T + 1, 2)

    @block.scalar
    def _(act):
        link = Link(act, act_own)

        def step(k, s, steady, over):
            here, ahead = (steady or 0 <= k < T), (steady or k + 1 < T)
            n2 = (s + 1) % 2
            for e in range(E):
                if here:
                    n = 8 * k + e
                    act.wait_ge(gv_done, n + 1)
                    if steady or n >= 2:
                        act.wait_ge(hh_ready, n - 1)
                    nc.scalar.activation(sg[:, e % 2, :], ps_g[:, e % 2, :], ACT.Sigmoid).then_inc(sg_ready, 1)
                if ahead and e == 2:
                    act.preload_act_table_set("natural_log_exp_and_others")
                    act.wait_ge(var_ready, k + 2)
                    link(nc.scalar.activation(v3[:, 1, :], v3[:, 0, :], ACT.Ln))
                    nc.scalar.activation(v3[:, 2, :], v3[:, 1, :], ACT.Exp, scale=-0.5).then_inc(rs_ready, 1)
                if ahead and e == 4:
                    for kc in range(2):
                        act.wait_ge(xT_done, 2 * (k + 1) + kc + 1)
                        if kc == 0 and (steady or k >= 1):
                            act.wait_ge(gv_done, 8 * k)
                        nc.scalar.activation(xnT[:, n2, kc, :], ps_x[:], ACT.Copy).then_inc(xT_ready, 1)
                if ahead and e == 6:
                    act.wait_ge(dl_ready, k + 2)
                    nc.scalar.activation(dl[:, 1, :], dl[:, 0, :], ACT.Sigmoid).then_inc(tw_ready, 1)
                    nc.scalar.activation(dl[:, 2, :], dl[:, 0, :], ACT.Sigmoid, scale=-1.0).then_inc(tw_ready, 1)

        run_steps(act, step, -1, STEADY, T, 2, link, 2)

    @block.vector
    def _(dve):
        link = Link(dve, own)

        def add_expert(k, s, e, steady):
            n = 8 * k + e
            dve.wait_ge(y_done, n + 1)
            if e == 0:
                dve.wait_ge(wt_ready, k + 1)
                if steady or k >= 2:
                    dve.wait_ge(stored[s], (k // 2) * 16)
            else:
                dve.wait_ge(acc_done, n)
            for bl in range(BL):
                before = x[:, s, bl, :] if e == 0 else acc[:, s, bl, :]
                ins = nc.vector.scalar_tensor_tensor(out=acc[:, s, bl, :], in0=ps_y[:, bl, :],
                                                     scalar=wt[:, s, bl, e:e + 1], in1=before,
                                                     op0=ALU.mult, op1=ALU.add)
                if bl < BL - 1:
                    link(ins)
            ins.then_inc(acc_done, 1)

        def step(k, s, steady, over):
            here, ahead = (steady or 0 <= k < T), (steady or k + 1 < T)
            n2 = (s + 1) % 2
            for e in range(E):
                if here:
                    n = 8 * k + e
                    dve.wait_ge(sg_ready, n + 1)
                    if steady or n >= 2:
                        dve.wait_ge(y_done, n - 1)
                    link(nc.vector.tensor_tensor(hh[:, e % 2, :], sg[:, e % 2, :], ps_g[:, e % 2, :], ALU.mult))
                    nc.vector.tensor_tensor(hh[:, e % 2, :], hh[:, e % 2, :], ps_v[:, e % 2, :], ALU.mult).then_inc(hh_ready, 1)
                if e == 0 and (steady or k >= 1):
                    add_expert(k - 1, (s - 1) % 2, E - 1, steady)
                if here and e >= 1:
                    add_expert(k, s, e - 1, steady)
                if ahead and e == 1:
                    dve.wait_ge(x_loaded[n2], ((k + 1) // 2 + 1) * 16 if not steady else (k + 1 - n2) * 8 + 16)
                    for n in range(BL):
                        link(nc.vector.bn_stats(stats[:, n, :], x[:, n2, n, :]))
                    for n in range(BL):
                        dve.sem_inc(waits_met, 1)
                        link(nc.vector.bn_aggr(mv[:, n, :], stats[:, n, :]))
                    nc.vector.tensor_scalar(v3[:, 0, :], mv[:, :, 1], EPS, None, ALU.add).then_inc(var_ready, 1)
                if ahead and e == 3:
                    dve.wait_ge(rs_ready, k + 2)
                    dve.wait_ge(var_ready, k + 2)
                    link(nc.vector.tensor_tensor(v3[:, 3, :], v3[:, 2, :], v3[:, 2, :], ALU.mult))
                    link(nc.vector.tensor_tensor(v3[:, 3, :], v3[:, 3, :], v3[:, 0, :], ALU.mult))
                    link(nc.vector.tensor_scalar(v3[:, 3, :], v3[:, 3, :], -0.5, 1.5, ALU.mult, ALU.add))
                    link(nc.vector.tensor_tensor(v3[:, 3, :], v3[:, 3, :], v3[:, 2, :], ALU.mult))
                    if steady or k >= 0:
                        dve.wait_ge(xT_done, 2 * k + 2)
                    for n in range(BL):
                        ins = nc.vector.tensor_scalar(xn[:, n, :], x[:, n2, n, :], mv[:, n, 0:1], v3[:, 3, n:n + 1],
                                                      ALU.subtract, ALU.mult)
                        if n < BL - 1:
                            link(ins)
                    ins.then_inc(xn_ready, 1)
                if ahead and e == 6:
                    dve.wait_ge(lg_done, k + 2)
                    link(nc.vector.tensor_copy(lg[:], ps_l[:, 0:BL * E].rearrange("p (n e) -> p n e", n=BL)))
                    for n in range(BL):
                        dve.sem_inc(waits_met, 1)
                        link(nc.vector.max(top[:, n, :], lg[:, n, :]))
                    for n in range(BL):
                        dve.sem_inc(waits_met, 1)
                        link(nc.vector.max_index(idx[:, n, :], top[:, n, :], lg[:, n, :]))
                    nc.vector.tensor_tensor(dl[:, 0, :], top[:, :, 0], top[:, :, 1], ALU.subtract).then_inc(dl_ready, 1)
                    link(nc.vector.tensor_copy(idf[:], idx[:]))
                if ahead and e == 7:
                    dve.wait_ge(tw_ready, 2 * (k + 2))
                    for n in range(BL):
                        for j, dst in ((0, wt[:, n2, n, :]), (1, wtb[:, n, :])):
                            link(nc.vector.tensor_scalar(dst, iota8[:], idf[:, n, j:j + 1], dl[:, 1 + j, n:n + 1],
                                                         ALU.is_equal, ALU.mult))
                    nc.vector.tensor_tensor(wt[:, n2, :, :], wt[:, n2, :, :], wtb[:], ALU.add).then_inc(wt_ready, 1)

        dve.wait_ge(ffn_in, 5 * 16)
        run_steps(dve, step, -1, STEADY, T + 1, 2, link, 2 * (8 * 4 + 8 + 4 + 3 + 1 + 8 + 1 + 8))


def kernel(**inputs):
    import numpy as np
    import concourse.bacc as bacc
    from concourse.bass_utils import run_bass_kernel_spmd

    a = {k: np.asarray(v) for k, v in inputs.items()}
    B, S, D = a["x"].shape
    cst = np.zeros((P, 11), np.float32)
    lane = np.arange(P)
    cst[:, 0] = (lane // 16) % 2 == 0
    cst[:, 1] = (lane // 16) % 2 == 1
    for h in range(8):
        cst[:, 2 + h] = lane // 16 == h
    cst[:, 10] = (lane % S) / S
    arrays = {
        "x": a["x"], "ctx": a["ctx_2048"], "ctxT": a["ctx_2048"].transpose(0, 2, 1),
        "wqT": a["L0_attn_Wq"].T, "wkT": a["L0_attn_Wk"].T, "wvT": a["L0_attn_Wv"].T, "woT": a["L0_attn_Wo"].T,
        "bq": a["L0_attn_bq"], "bk": a["L0_attn_bk"], "bv": a["L0_attn_bv"], "bo": a["L0_attn_bo"],
        "truth": a["L0_attn_truth_gate"], "balance": a["L0_attn_balance_gate"], "order": a["L0_attn_order_gate"],
        "justice": a["L0_attn_justice_gate"], "harmony": a["L0_attn_harmony_gate"],
        "gamma": a["L0_xattn_gamma"].reshape(1), "rwT": a["L0_ffn_router_w"].T,
        "w1": a["L0_ffn_w1"], "w2": a["L0_ffn_w2"], "w3": a["L0_ffn_w3"],
        "ident": np.eye(P, dtype=np.float32), "cst": cst,
        "iota8": np.tile(np.arange(8, dtype=np.float32), (P, 1)),
    }
    nc = bacc.Bacc("TRN2", target_bir_lowering=False, num_devices=1)
    feeds, t = {}, {}
    for name, v in arrays.items():
        v = np.ascontiguousarray(v)
        feeds["in_" + name] = v
        t[name] = nc.dram_tensor("in_" + name, v.shape, mybir.dt.from_np(v.dtype), kind="ExternalInput").ap()
    t["out"] = nc.dram_tensor("out_x", (B, S, D), F32, kind="ExternalOutput").ap()
    decoder_kernel(nc, t)
    r = run_bass_kernel_spmd(nc, [feeds], core_ids=[0])
    return r.results[0]["out_x"]
```

```python
import math
from contextlib import ExitStack

import concourse.bass as bass
from concourse import mybir

F32 = mybir.dt.float32
BF16 = mybir.dt.bfloat16
U32 = mybir.dt.uint32
ALU = mybir.AluOpType
ACT = mybir.ActivationFunctionType
AX_X = mybir.AxisListType.X

P = 128
EPS = 1e-5


class Link:

    def __init__(self, eng, sem):
        self.eng, self.sem, self.base, self.n = eng, sem, 0, 0

    def __call__(self, ins):
        ins.then_inc(self.sem, 1)
        self.n += 1
        self.eng.wait_ge(self.sem, self.base + self.n)

    def mark(self, ins):
        ins.then_inc(self.sem, 1)
        self.n += 1
        return self.n

    def until(self, k):
        self.eng.wait_ge(self.sem, self.base + k)

    def enter_loop(self):
        self.before = self.n
        self.n = 0

    def at(self, i, per):
        self.base = self.before + i * per

    def leave_loop(self, trips, per):
        assert self.n == per, (self.n, per)
        self.base, self.n = 0, self.before + trips * per


def run_steps(eng, step, first, steady, end, unroll, link=None, per=0):
    lo, hi = steady
    for t in range(first, lo):
        step(t, t % unroll, False, lambda n, off=0, t=t: (t + off) // n)
    trips = (hi - lo) // unroll
    assert lo + trips * unroll == hi
    if link:
        link.enter_loop()
    with eng.Fori(0, trips) as i:
        if link:
            link.at(i, per)
        for s in range(unroll):
            step(i * unroll + (lo + s), (lo + s) % unroll, True,
                 lambda n, off=0, s=s: i * (unroll // n) + (lo + s + off) // n)
    if link:
        link.leave_loop(trips, per)
    for t in range(hi, end):
        step(t, t % unroll, False, lambda n, off=0, t=t: (t + off) // n)


def decoder_kernel(nc, t):
    B, S, D = t["x"].shape
    H, HD = 16, D // 16
    TILES = B * S // P
    ctx = ExitStack()

    def sbt(stack, name, shape, dt=F32):
        return stack.enter_context(nc.sbuf_tensor(name, shape, dt))

    def pst(stack, name, shape, dt=F32):
        return stack.enter_context(nc.psum_tensor(name, shape, dt))

    def sem(stack, name):
        return stack.enter_context(nc.semaphore(name))

    x1_dram = nc.dram_tensor("x1_scratch", [B * S, D], F32, kind="Internal").ap()
    x2_dram = nc.dram_tensor("x2_scratch", [B * S, D], F32, kind="Internal").ap()
    qp_dram = nc.dram_tensor("q_parts", [B, 8, 3, 8, D], BF16, kind="Internal").ap()
    o_dram = nc.dram_tensor("o_scratch", [B, 2, P, D], F32, kind="Internal").ap()
    kp_dram = nc.dram_tensor("k_parts", [B, 3, 8, 8, D], BF16, kind="Internal").ap()
    x_in = t["x"].rearrange("b s d -> (b s) d")
    c_in = t["ctx"].rearrange("b s d -> (b s) d")
    out = t["out"].rearrange("b s d -> (b s) d")

    with ctx:
        ident = sbt(ctx, "ident", [P, P])
        ident16 = sbt(ctx, "ident16", [P, P], BF16)
        gamma = sbt(ctx, "gamma", [P, 1])
        w1 = sbt(ctx, "w1", [P, 8, 2, P])
        w2 = sbt(ctx, "w2", [P, 8, 2, P])
        w3 = sbt(ctx, "w3", [P, 8, D])
        rw = sbt(ctx, "rw", [P, 2, 8])
        iota8 = sbt(ctx, "iota8", [P, 8])
        ks = sbt(ctx, "ks", [P, 4, 8, D], BF16)
        qs = sbt(ctx, "qs", [P, 4, 8, D], BF16)
        vaug = sbt(ctx, "vaug", [P, 4, 2, 8, 32])
        consts_done = sem(ctx, "consts_done")
        weights_in = sem(ctx, "weights_in")
        ffn_in = sem(ctx, "ffn_in")

        with ExitStack() as st:
            phase1(nc, t, st, sbt, pst, sem, locals())
        with ExitStack() as st:
            phase2(nc, t, st, sbt, pst, sem, locals())
        with ExitStack() as st:
            phase3(nc, t, st, sbt, pst, sem, locals())


def phase1(nc, t, st, sbt, pst, sem, g):
    TILES, D = g["TILES"], g["D"]
    ident, ident16, gamma = g["ident"], g["ident16"], g["gamma"]
    x_in, c_in, x1_dram, qp_dram, kp_dram = (g[k] for k in ("x_in", "c_in", "x1_dram", "qp_dram", "kp_dram"))
    weights_in, ffn_in, consts_done = g["weights_in"], g["ffn_in"], g["consts_done"]
    ks, qs, vaug = g["ks"], g["qs"], g["vaug"]

    def sb(name, shape, dt=F32):
        return sbt(st, name, shape, dt)

    def sm(name):
        return sem(st, name)

    wq, wk, wv, wo = (sb(n, [P, 2, D]) for n in ("wq", "wk", "wv", "wo"))
    bq, bk = sb("bq", [P, 2]), sb("bk", [P, 2])
    bv, bo = sb("bv", [P, D]), sb("bo", [P, D])
    gates = sb("gates", [P, 5])
    cst = sb("cst", [P, 11])
    sig = sb("sig", [P, 5])
    coef = sb("coef", [P, 6])
    cf = sb("cf", [P, 5, 16])
    bkm = sb("bkm", [P, 2, 2])
    x = sb("x_tile", [P, 4, D])
    c = sb("c_tile", [P, 4, D])
    stats = sb("stats", [P, 2, 8])
    ln_s = sb("ln_s", [P, 2, 4])
    xhat = sb("xhat", [P, 2, D])
    hT = sb("hT", [P, 2, 2, 2, 2, 64])
    qT = sb("qT", [P, 2, 2, P])
    kT = sb("kT", [P, 2, 2, 2, 2, 64])
    ksq = sb("ksq", [P, 2, 2, P])
    vblk = sb("vblk", [P, 2, 2, 8, 2, 17])
    s_sb = sb("s_sb", [P, 16, 64])
    dif = sb("dif", [P, 16, 63])
    dd = sb("dd", [P, 16, 64])
    e1 = sb("e1", [P, 16, 64])
    ed = sb("ed", [P, 16, 64])
    e2 = sb("e2", [P, 8, P])
    pT = sb("pT", [P, 8, P])
    rows = sb("rows", [P, 2, 16, 16])
    KN, ENT, SUM, ABS, MX, Z, RZ, SED, LNZ, KN2, W, T0 = range(12)
    T1, T2, T4 = T0 + 1, T0 + 2, T0 + 4
    att = sb("att", [P, D])
    recw = sb("recw", [P, 2, 16])
    aT = sb("aT", [P, 2, P])
    x1 = sb("x1_tile", [P, 2, D])
    stats2 = sb("stats2", [P, 2, 8])
    ln2 = sb("ln2", [P, 2, 4])
    q = sb("q_tile", [P, D])
    r = sb("q_rest", [P, D])
    qp = sb("q_part", [P, 2, 3, D], BF16)
    cr = sb("c_rest", [P, D])
    cp = sb("c_part", [P, 4, 3, D], BF16)

    ps_x = pst(st, "ps_x", [P, 512])
    ps_qk = pst(st, "ps_qk", [P, 4, P])
    ps_v = pst(st, "ps_v", [P, 2, D])
    ps_s = pst(st, "ps_s", [P, 4, 512])
    ps_o = pst(st, "ps_o", [P, 512])

    x_loaded = [sm(f"x_loaded{i}") for i in range(4)]
    c_loaded = [sm(f"c_loaded{i}") for i in range(4)]
    small_in = sm("small_in")
    setup_done, sig_done = sm("setup_done"), sm("sig_done")
    zeros_done = sm("zeros_done")
    waits_met = sm("waits_met")
    dve_own, act_own = sm("dve_own"), sm("act_own")
    var1_ready, rs1_ready, var2_ready, rs2_ready = sm("var1_ready"), sm("rs1_ready"), sm("var2_ready"), sm("rs2_ready")
    xhat_ready, xT_done, hT_ready = sm("xhat_ready"), sm("xT_done"), sm("hT_ready")
    qk_done, v_done, qk_ready, v_ready = sm("qk_done"), sm("v_done"), sm("qk_ready"), sm("v_ready")
    kn_done, kn_read = sm("kn_done"), sm("kn_read")
    s_done, s_ready, max_ready, sum_done = sm("s_done"), sm("s_ready"), sm("max_ready"), sm("sum_done")
    dif_ready, d_ready, e1_ready, e2_ready, ed_ready = sm("dif_ready"), sm("d_ready"), sm("e1_ready"), sm("e2_ready"), sm("ed_ready")
    abs_done, z_ready, sed_done = sm("abs_done"), sm("z_ready"), sm("sed_done")
    logs_ready, w_arg, w_ready = sm("logs_ready"), sm("w_arg"), sm("w_ready")
    pT_done, pT_ready, o_done, att_ready = sm("pT_done"), sm("pT_ready"), sm("o_done"), sm("att_ready")
    aT_done, aT_ready, y_done, x1_ready = sm("aT_done"), sm("aT_ready"), sm("y_done"), sm("x1_ready")
    qp_ready = sm("qp_ready")
    rz_ready, xb_ready, pool_own = sm("rz_ready"), sm("xb_ready"), sm("pool_own")
    c_copied, c_rest, cp_ready = [sm(f"c_copied{i}") for i in range(2)], sm("c_rest_ready"), sm("cp_ready")
    x1_stored = [sm(f"x1_stored{i}") for i in range(2)]
    qp_stored = [sm(f"qp_stored{i}") for i in range(2)]
    cp_stored = [sm(f"cp_stored{i}") for i in range(4)]
    N_STEADY = (3, TILES - 5)

    block = st.enter_context(nc.Block())

    @block.sync
    def _(sp):
        def load(u, s4):
            row = u * P
            sp.dma_start(x[:, s4, :], x_in[bass.ds(row, P), :]).then_inc(x_loaded[s4], 16)

        sp.dma_start(x[:, 0, :], x_in[0:P, :]).then_inc(x_loaded[0], 16)
        for tile, name in ((ident, "ident"), (cst, "cst")):
            sp.dma_start(tile[:], t[name]).then_inc(small_in, 16)
        for tile, name in ((wq, "wqT"), (wk, "wkT"), (wv, "wvT"), (wo, "woT")):
            sp.dma_start(tile[:], t[name].rearrange("(c p) o -> p c o", p=P)).then_inc(weights_in, 16)
        for tile, name in ((bq, "bq"), (bk, "bk")):
            sp.dma_start(tile[:], t[name].rearrange("(c p) -> p c", p=P), allow_slow_non_contiguous=True).then_inc(small_in, 16)
        for tile, name in ((bv, "bv"), (bo, "bo")):
            a = t[name]
            sp.dma_start(tile[:], bass.AP(a.tensor, a.offset, [[0, P]] + list(a.ap))).then_inc(small_in, 16)
        for i, name in enumerate(("truth", "balance", "order", "justice", "harmony")):
            a = t[name]
            sp.dma_start(gates[:, i:i + 1], bass.AP(a.tensor, a.offset, [[0, P]] + list(a.ap))).then_inc(small_in, 16)
        a = t["gamma"]
        sp.dma_start(gamma[:], bass.AP(a.tensor, a.offset, [[0, P]] + list(a.ap))).then_inc(small_in, 16)
        load(1, 1)
        load(2, 2)
        sp.dma_start(g["iota8"][:], t["iota8"]).then_inc(ffn_in, 16)
        sp.dma_start(g["w1"][:], t["w1"].rearrange("e (c p) f -> p e c f", p=P)).then_inc(ffn_in, 16)
        sp.dma_start(g["w2"][:], t["w2"].rearrange("e (c p) f -> p e c f", p=P)).then_inc(ffn_in, 16)
        sp.dma_start(g["w3"][:], t["w3"].rearrange("e f d -> f e d")).then_inc(ffn_in, 16)
        sp.dma_start(g["rw"][:], t["rwT"].rearrange("(c p) e -> p c e", p=P)).then_inc(ffn_in, 16)

        def step(u, s, steady, over):
            v, sv = u - 1, (s - 1) % 2
            if steady or 0 <= u + 2 < TILES:
                if steady or u >= 2:
                    sp.wait_ge(c_rest, u - 1)
                sp.dma_start(c[:, (s + 2) % 4, :], c_in[bass.ds((u + 2) * P, P), :]).then_inc(c_loaded[(s + 2) % 4], 16)
            w = u - 2
            if steady or 2 <= u <= TILES + 1:
                sp.wait_ge(cp_ready, w + 1)
                for bb in range(2):
                    for i in range(3):
                        sp.dma_start(kp_dram[w * 2 + bb, i].rearrange("d h c -> h d c"),
                                     cp[64 * bb:64 * bb + 64, (s - 2) % 4, i, :]).then_inc(cp_stored[(s - 2) % 4], 16)
            if steady or 1 <= u <= TILES:
                sp.wait_ge(x1_ready, v + 1)
                sp.dma_start(x1_dram[bass.ds(v * P, P), :], x1[:, sv, :]).then_inc(x1_stored[sv], 16)
            if steady or 0 <= u and u + 3 < TILES:
                load(u + 3, (s + 3) % 4)
            if steady or 2 <= u <= TILES + 1:
                sw = s % 2
                sp.wait_ge(qp_ready, w + 1)
                for bb in range(2):
                    for i in range(3):
                        sp.dma_start(qp_dram[w * 2 + bb, :, i].rearrange("d h c -> h d c"),
                                     qp[64 * bb:64 * bb + 64, sw, i, :]).then_inc(qp_stored[sw], 16)

        run_steps(sp, step, -2, (2, TILES - 6), TILES + 2, 4)
        for i in range(2):
            sp.wait_ge(x1_stored[i], 16 * (TILES // 2))
            sp.wait_ge(qp_stored[i], 96 * (TILES // 2))
        for i in range(4):
            sp.wait_ge(cp_stored[i], 96 * (TILES // 4))

    @block.tensor
    def _(pe):
        def transpose_x(u, s2, steady):
            pe.wait_ge(xhat_ready, u + 1)
            if steady or u >= 1:
                pe.wait_ge(hT_ready, u)
            if steady or u >= 2:
                pe.wait_ge(kn_read, u - 1)
            for kc in range(2):
                last = nc.tensor.transpose(ps_x[:, kc * P:(kc + 1) * P], xhat[:, s2, kc * P:(kc + 1) * P], ident[:])
            last.then_inc(xT_done, 1)

        def project_qk(u, s2, steady):
            pe.wait_ge(hT_ready, u + 1)
            if steady or u >= 1:
                pe.wait_ge(qk_ready, u)
            for n, w in enumerate((wq, wk)):
                for m in range(2):
                    for kc in range(2):
                        last = nc.tensor.matmul(ps_qk[:, 2 * n + m, :], w[:, kc, m * P:(m + 1) * P],
                                                hT[:, s2, kc, :, 0, :], start=kc == 0, stop=kc == 1)
            last.then_inc(qk_done, 1)

        def project_v(u, s2, steady):
            if steady or u >= 1:
                pe.wait_ge(v_ready, u)
            for b in range(2):
                for kc in range(2):
                    last = nc.tensor.matmul(ps_v[:, b, :], hT[:, s2, kc, b, :, :], wv[:, kc, :],
                                            start=kc == 0, stop=kc == 1)
            last.then_inc(v_done, 1)

        def weights(u):
            for n in range(8):
                if n % 4 == 0:
                    pe.wait_ge(e2_ready, 2 * u + n // 4 + 1)
                last = nc.tensor.transpose(ps_s[:, n // 4, (n % 4) * P:(n % 4 + 1) * P], e2[:, n, :], ident[:])
                if n % 4 == 3:
                    last.then_inc(pT_done, 1)

        def transpose_att(u):
            pe.wait_ge(att_ready, u + 1)
            for kc in range(2):
                last = nc.tensor.transpose(ps_o[:, kc * P:(kc + 1) * P], att[:, kc * P:(kc + 1) * P], ident[:])
            last.then_inc(aT_done, 1)

        def project_out(u):
            pe.wait_ge(aT_ready, u + 1)
            for kc in range(2):
                last = nc.tensor.matmul(ps_o[:, 0:D], aT[:, kc, :], wo[:, kc, :], start=kc == 0, stop=kc == 1)
            last.then_inc(y_done, 1)

        def scores(u, s2, steady):
            pe.wait_ge(qk_ready, u + 1)
            if steady or u >= 1:
                pe.wait_ge(pT_ready, u)
            for j in range(4):
                for m in range(2):
                    for b in range(2):
                        last = nc.tensor.matmul(ps_s[64 * b:64 * b + 64, j, m * P:(m + 1) * P],
                                                qT[32 * j:32 * j + 32, s2, m, 64 * b:64 * b + 64],
                                                kT[32 * j:32 * j + 32, s2, m, b, :, :], start=True, stop=True)
                if j % 2 == 1:
                    last.then_inc(s_done, 1)

        def norms(u, s2, steady):
            if steady or u + 1 < TILES:
                pe.wait_ge(hT_ready, u + 2)
            if steady or u >= 1:
                pe.wait_ge(kn_read, u)
            for m in range(2):
                last = nc.tensor.matmul(ps_x[:, 256 + 8 * m:264 + 8 * m], ksq[:, s2, m, :], cst[:, 2:10],
                                        start=True, stop=True)
            last.then_inc(kn_done, 1)

        def times_v(u, s2, steady):
            pe.wait_ge(v_ready, u + 1)
            pe.wait_ge(pT_ready, u + 1)
            if steady or u >= 1:
                pe.wait_ge(x1_ready, u)
            for n in range(8):
                for b in range(2):
                    last = nc.tensor.matmul(ps_o[64 * b:64 * b + 64, n * 34:(n + 1) * 34],
                                            pT[:, n, 64 * b:64 * b + 64], vblk[:, s2, b, n, :, :],
                                            start=True, stop=True)
            last.then_inc(o_done, 1)

        def step(u, s, steady, over):
            here, ahead, behind = (steady or 0 <= u < TILES), (steady or -1 <= u < TILES - 1), (steady or 1 <= u <= TILES)
            s2, n2 = s % 2, (s + 1) % 2
            if ahead:
                project_qk(u + 1, n2, steady)
            if behind:
                times_v(u - 1, n2, steady)
            if here:
                weights(u)
            if ahead:
                project_v(u + 1, n2, steady)
            if behind:
                transpose_att(u - 1)
            if steady or u + 2 < TILES:
                transpose_x(u + 2, s2, steady)
            if behind:
                project_out(u - 1)
            if ahead:
                scores(u + 1, n2, steady)
                norms(u + 1, n2, steady)

        pe.wait_ge(small_in, 12 * 16)
        pe.wait_ge(weights_in, 4 * 16)
        run_steps(pe, step, -2, N_STEADY, TILES + 1, 4)

    @block.scalar
    def _(act):
        link = Link(act, act_own)
        act.preload_act_table_set("natural_log_exp_and_others")
        act.wait_ge(small_in, 12 * 16)
        nc.scalar.activation(sig[:], gates[:], ACT.Exp, scale=-1.0).then_inc(sig_done, 1)
        act.wait_ge(setup_done, 1)
        nc.scalar.activation(coef[:, 5:6], coef[:, 5:6], ACT.Exp).then_inc(sig_done, 1)
        act.wait_ge(sig_done, 2)

        def evacuate_qk(m, n2):
            nc.scalar.activation(qT[:, n2, m, :], ps_qk[:, m, :], ACT.Identity, bias=bq[:, m:m + 1])
            for par in range(2):
                nc.scalar.activation(kT[:, n2, m, :, par, :], ps_qk[:, 2 + m, :].rearrange("p (b k) -> p b k", b=2),
                                     ACT.Identity, bias=bkm[:, m, par:par + 1], scale=cst[:, par:par + 1])
            return nc.scalar.activation(ksq[:, n2, m, :], ps_qk[:, 2 + m, :], ACT.Square, bias=bk[:, m:m + 1])

        def rsqrt(v, ready, u, done):
            act.wait_ge(ready, u + 1)
            link(nc.scalar.activation(v[:, 1:2], v[:, 0:1], ACT.Ln))
            nc.scalar.activation(v[:, 2:3], v[:, 1:2], ACT.Exp, scale=-0.5).then_inc(done, 1)

        def step(u, s, steady, over):
            s2, n2 = s % 2, (s + 1) % 2
            here, ahead, behind = (steady or 0 <= u < TILES), (steady or -1 <= u < TILES - 1), (steady or 1 <= u <= TILES)
            if here:
                if steady or u >= 1:
                    act.wait_ge(dif_ready, u)
                    act.wait_ge(d_ready, 2 * u)
                    act.wait_ge(sum_done, u)
                for hf in range(2):
                    act.wait_ge(s_done, 2 * u + hf + 1)
                    nc.scalar.activation(s_sb[:, 8 * hf:8 * hf + 8, :].rearrange("p (j h) k -> p j (h k)", j=2),
                                         ps_s[:, 2 * hf:2 * hf + 2, 0:256], ACT.Copy,
                                         scale=1.0 / math.sqrt(16)).then_inc(s_ready, 1)
            if behind:
                act.wait_ge(z_ready, u)
                link(nc.scalar.activation(rows[:, n2, LNZ, :], rows[:, n2, Z, :], ACT.Ln))
                act.wait_ge(kn_read, u)
                link(nc.scalar.activation(rows[:, n2, KN, :], rows[:, n2, KN2, :], ACT.Ln))
                nc.scalar.activation(rows[:, n2, KN, :], rows[:, n2, KN, :], ACT.Exp, scale=0.5).then_inc(logs_ready, 1)
            if steady or 2 <= u <= TILES + 1:
                rsqrt(ln2[:, s2, :], var2_ready, u - 2, rs2_ready)
            if behind:
                act.wait_ge(c_rest, u)
                nc.scalar.activation(cp[:, (s - 1) % 4, 1, :], cr[:], ACT.Copy).then_inc(c_copied[1], 1)
            if here:
                act.wait_ge(c_loaded[s], over(4) * 16 + 16)
                if steady or u >= 4:
                    act.wait_ge(cp_stored[s], over(4) * 96)
                nc.scalar.activation(cp[:, s, 0, :], c[:, s, :], ACT.Copy).then_inc(c_copied[0], 1)
            if ahead:
                act.wait_ge(qk_done, u + 2)
                if steady or u >= 1:
                    act.wait_ge(kn_done, u)
                evacuate_qk(0, n2)
            if here:
                if steady or u >= 1:
                    act.wait_ge(pT_done, 2 * u)
                    act.wait_ge(ed_ready, u)
                    act.wait_ge(z_ready, u)
                for hf in range(2):
                    act.wait_ge(d_ready, 2 * u + hf + 1)
                    nc.scalar.activation(e2[:, 4 * hf:4 * hf + 4, :].rearrange("p n k -> p (n k)"),
                                         dd[:, 8 * hf:8 * hf + 8, :].rearrange("p h k -> p (h k)"), ACT.Exp,
                                         scale=coef[:, 4:5]).then_inc(e2_ready, 1)
                nc.scalar.activation(e1[:], dd[:], ACT.Exp).then_inc(e1_ready, 1)
            if steady or u + 2 < TILES:
                rsqrt(ln_s[:, s2, :], var1_ready, u + 2, rs1_ready)
            if behind:
                act.wait_ge(w_arg, u)
                nc.scalar.activation(rows[:, n2, W, :], rows[:, n2, T4, :], ACT.Exp).then_inc(w_ready, 1)
            if here:
                if steady or u >= 1:
                    act.wait_ge(o_done, u)
                for hf in range(2):
                    act.wait_ge(pT_done, 2 * u + hf + 1)
                    ins = nc.scalar.activation(pT[:, 4 * hf:4 * hf + 4, :],
                                               ps_s[:, hf, :].rearrange("p (n k) -> p n k", k=P), ACT.Copy,
                                               scale=coef[:, 5:6])
                ins.then_inc(pT_ready, 1)
            if ahead:
                evacuate_qk(1, n2).then_inc(qk_ready, 1)
            if behind:
                act.wait_ge(aT_done, u)
                if steady or u >= 2:
                    act.wait_ge(y_done, u - 1)
                nc.scalar.activation(aT[:], ps_o[:, 0:256].rearrange("p (c t) -> p c t", c=2), ACT.Copy).then_inc(aT_ready, 1)
            if steady or u + 2 < TILES:
                act.wait_ge(xT_done, u + 3)
                if steady or u >= 0:
                    act.wait_ge(v_done, u + 1)
                for i in range(2):
                    ins = nc.scalar.activation(hT[:, s2, :, :, i, :],
                                               ps_x[:, 0:256].rearrange("p (c b t) -> p c b t", c=2, b=2), ACT.Copy)
                ins.then_inc(hT_ready, 1)

        run_steps(act, step, -2, N_STEADY, TILES + 2, 4, link, 4 * 4)

    @block.gpsimd
    def _(pool):
        link = Link(pool, pool_own)
        tt = nc.gpsimd.tensor_tensor

        def step(u, s, steady, over):
            s2, s4 = s % 2, s % 4
            here, behind = (steady or 0 <= u < TILES), (steady or 1 <= u <= TILES)
            R = rows[:, s2]
            if here:
                if steady or u >= 1:
                    pool.wait_ge(e1_ready, u)
                    pool.wait_ge(ed_ready, u)
                for hf in range(2):
                    hs = slice(8 * hf, 8 * hf + 8)
                    pool.wait_ge(s_ready, 2 * u + hf + 1)
                    pool.wait_ge(max_ready, 2 * u + hf + 1)
                    if hf == 1:
                        pool.wait_ge(d_ready, 2 * u + 1)
                    tt(dd[:, hs, :], s_sb[:, hs, :], R[:, MX, hs].unsqueeze(2).to_broadcast([P, 8, 64]), ALU.subtract)\
                        .then_inc(d_ready, 1)
            if behind:
                Rb = rows[:, (s - 1) % 2]
                pool.wait_ge(rz_ready, u)
                pool.wait_ge(sed_done, u)
                pool.wait_ge(logs_ready, u)
                link(tt(Rb[:, ENT, :], Rb[:, RZ, :], Rb[:, SED, :], ALU.mult))
                link(tt(Rb[:, ENT, :], Rb[:, LNZ, :], Rb[:, ENT, :], ALU.subtract))
                link(tt(Rb[:, T0:T0 + 5, :], Rb[:, 0:5, :], cf[:], ALU.mult))
                link(tt(Rb[:, T0:T2, :], Rb[:, T0:T2, :], Rb[:, T2:T4, :], ALU.add))
                link(tt(Rb[:, T0, :], Rb[:, T0, :], Rb[:, T1, :], ALU.add))
                link(tt(Rb[:, T1, :], Rb[:, T4, :], Rb[:, T0, :], ALU.add))
                link(tt(Rb[:, T0, :], Rb[:, T0, :], Rb[:, T1, :], ALU.subtract))
                tt(Rb[:, T4, :], Rb[:, T0, :], Rb[:, T4, :], ALU.add).then_inc(w_arg, 1)
            if here:
                if steady or u >= 1:
                    pool.wait_ge(abs_done, u)
                tt(dif[:], s_sb[:, :, 1:64], s_sb[:, :, 0:63], ALU.subtract).then_inc(dif_ready, 1)
                pool.wait_ge(e1_ready, u + 1)
                pool.wait_ge(d_ready, 2 * u + 2)
                if steady or u >= 1:
                    pool.wait_ge(sed_done, u)
                tt(ed[:], e1[:], dd[:], ALU.mult).then_inc(ed_ready, 1)
            if behind:
                pool.wait_ge(c_copied[1], u)
                pool.wait_ge(c_rest, u)
                tt(cp[:, (s - 1) % 4, 2, :], cr[:], cp[:, (s - 1) % 4, 1, :], ALU.subtract).then_inc(cp_ready, 1)
            if here:
                pool.wait_ge(c_copied[0], u + 1)
                if steady or u >= 1:
                    pool.wait_ge(cp_ready, u)
                tt(cr[:], c[:, s, :], cp[:, s, 0, :], ALU.subtract).then_inc(c_rest, 1)
                pool.wait_ge(xhat_ready, u + 1)
                tt(x[:, s4, :], x[:, s4, :], bo[:], ALU.add).then_inc(xb_ready, 1)

        for tile in (ks, qs, vaug):
            nc.gpsimd.memset(tile[:], 0.0).then_inc(consts_done, 1)
        pool.wait_ge(consts_done, 3)
        nc.gpsimd.memset(ks[96:99, :, :, :], 1.0).then_inc(consts_done, 1)
        pool.wait_ge(consts_done, 4)
        nc.gpsimd.memset(vaug[:, :, :, :, 8:16], 1.0).then_inc(consts_done, 1)
        pool.wait_ge(consts_done, 5)
        pool.wait_ge(small_in, 12 * 16)
        pool.wait_ge(setup_done, 1)
        run_steps(pool, step, 0, (4, TILES - 4), TILES + 1, 4, link, 4 * 7)

    @block.vector
    def _(dve):
        link = Link(dve, dve_own)
        link(nc.vector.memset(vblk[:], 0.0))
        nc.vector.memset(vblk[0:64, :, :, :, 0, 16:17], 1.0).then_inc(zeros_done, 1)
        nc.vector.memset(vblk[64:128, :, :, :, 1, 16:17], 1.0).then_inc(zeros_done, 1)
        dve.wait_ge(zeros_done, 2)
        dve.wait_ge(small_in, 12 * 16)
        link(nc.vector.tensor_copy(ident16[:], ident[:]))
        dve.wait_ge(sig_done, 1)
        link(nc.vector.tensor_scalar(sig[:], sig[:], 1.0, None, ALU.add))
        link(nc.vector.reciprocal(sig[:], sig[:]))
        for i, (gate, f) in enumerate(((0, -0.01), (1, 0.1 / math.log(64)), (3, 0.1 / 64), (4, -0.1 / 63))):
            link(nc.vector.tensor_scalar(coef[:, i:i + 1], sig[:, gate:gate + 1], f, None, ALU.mult))
        link(nc.vector.tensor_scalar(coef[:, 4:5], sig[:, 3:4], -0.1, 1.0, ALU.mult, ALU.add))
        for i in range(5):
            link(nc.vector.tensor_copy(cf[:, i, :], coef[:, i:i + 1].to_broadcast([P, 16])))
        link(nc.vector.tensor_scalar(coef[:, 5:6], cst[:, 10:11], sig[:, 2:3], 0.05, ALU.mult, ALU.mult))
        for par in range(2):
            link(nc.vector.tensor_scalar(bkm[:, :, par], bk[:], cst[:, par:par + 1], None, ALU.mult))
        nc.vector.tensor_scalar(bkm[:, :, 0], bk[:], cst[:, 0:1], None, ALU.mult).then_inc(setup_done, 1)
        dve.wait_ge(setup_done, 1)

        def step(u, s, steady, over):
            s2, n2, s4 = s % 2, (s + 1) % 2, (s + 2) % 4
            here, ahead, behind = (steady or 0 <= u < TILES), (steady or -1 <= u < TILES - 1), (steady or 1 <= u <= TILES)
            ahead2, behind2 = (steady or u + 2 < TILES), (steady or 2 <= u <= TILES + 1)
            R, Rb = rows[:, s2], rows[:, n2]
            L1, S1, L2, S2 = ln_s[:, s2, :], stats[:, s2, :], ln2[:, s2, :], stats2[:, s2, :]
            if here:
                for hf in range(2):
                    hs = slice(8 * hf, 8 * hf + 8)
                    dve.wait_ge(s_ready, 2 * u + hf + 1)
                    nc.vector.tensor_reduce(R[:, MX, hs], s_sb[:, hs, :], AX_X, ALU.max).then_inc(max_ready, 1)
            if ahead2:
                dve.wait_ge(x_loaded[s4], over(4, 2) * 16 + 16)
                k_st = link.mark(nc.vector.bn_stats(S1[:, 0:6], x[:, s4, :]))
            if behind:
                dve.wait_ge(dif_ready, u)
                nc.vector.tensor_reduce(Rb[:, ABS, :], dif[:], AX_X, ALU.add, apply_absolute_value=True)\
                    .then_inc(abs_done, 1)
            if ahead2:
                link.until(k_st)
                dve.sem_inc(waits_met, 1)
                k_st = link.mark(nc.vector.bn_aggr(S1[:, 6:8], S1[:, 0:6]))
            if behind:
                dve.wait_ge(ed_ready, u)
                nc.vector.tensor_reduce(Rb[:, SED, :], ed[:], AX_X, ALU.add).then_inc(sed_done, 1)
            if ahead2:
                if steady or u >= 0:
                    dve.wait_ge(rs1_ready, u + 1)
                link.until(k_st)
                nc.vector.tensor_scalar(L1[:, 0:1], S1[:, 7:8], EPS, None, ALU.add).then_inc(var1_ready, 1)
            if here:
                nc.vector.tensor_reduce(R[:, SUM, :], s_sb[:], AX_X, ALU.add).then_inc(sum_done, 1)
                dve.wait_ge(kn_done, u + 1)
                if steady or u >= 2:
                    dve.wait_ge(logs_ready, u - 1)
                nc.vector.tensor_scalar(R[:, KN2, :].rearrange("p (j m r) -> p m j r", j=4, m=2),
                                        ps_x[:, 256:272].rearrange("p (m j r) -> p m j r", m=2, j=4), 1e-18, None,
                                        ALU.max).then_inc(kn_read, 1)
            if ahead2:
                dve.wait_ge(rs1_ready, u + 3)
                dve.wait_ge(var1_ready, u + 3)
                k1 = link.mark(nc.vector.scalar_tensor_tensor(out=L1[:, 3:4], in0=L1[:, 2:3], scalar=L1[:, 2:3],
                                                              in1=L1[:, 0:1], op0=ALU.mult, op1=ALU.mult))
            if behind2:
                dve.wait_ge(rs2_ready, u - 1)
                dve.wait_ge(var2_ready, u - 1)
                k2 = link.mark(nc.vector.scalar_tensor_tensor(out=L2[:, 3:4], in0=L2[:, 2:3], scalar=L2[:, 2:3],
                                                              in1=L2[:, 0:1], op0=ALU.mult, op1=ALU.mult))
            if ahead2:
                link.until(k1)
                k1 = link.mark(nc.vector.tensor_scalar(L1[:, 3:4], L1[:, 3:4], -0.5, 1.5, ALU.mult, ALU.add))
            if behind2:
                link.until(k2)
                k2 = link.mark(nc.vector.tensor_scalar(L2[:, 3:4], L2[:, 3:4], -0.5, 1.5, ALU.mult, ALU.add))
            if ahead2:
                link.until(k1)
                k1 = link.mark(nc.vector.tensor_tensor(L1[:, 3:4], L1[:, 3:4], L1[:, 2:3], ALU.mult))
            if behind2:
                link.until(k2)
                k2 = link.mark(nc.vector.tensor_tensor(L2[:, 3:4], L2[:, 3:4], L2[:, 2:3], ALU.mult))
            if ahead2:
                link.until(k1)
                if steady or u >= 0:
                    dve.wait_ge(xT_done, u + 1)
                nc.vector.tensor_scalar(xhat[:, s2, :], x[:, s4, :], S1[:, 6:7], L1[:, 3:4],
                                        ALU.subtract, ALU.mult).then_inc(xhat_ready, 1)
            if behind:
                dve.wait_ge(o_done, u)
                dve.wait_ge(w_ready, u)
                o = ps_o[:, 0:272].rearrange("p (h e) -> p h e", e=17)
                k1 = link.mark(nc.vector.tensor_tensor(recw[:, 0, :], o[:, :, 16], Rb[:, W, :], ALU.mult))
            if behind2:
                link.until(k2)
                k2 = link.mark(nc.vector.tensor_scalar(q[:], x1[:, s2, :], S2[:, 6:7], L2[:, 3:4], ALU.subtract, ALU.mult))
            if behind:
                link.until(k1)
                k1 = link.mark(nc.vector.reciprocal(recw[:, 1, :], recw[:, 0, :]))
            if behind2:
                if steady or u >= 4:
                    dve.wait_ge(qp_stored[s2], over(2, -2) * 96)
                link.until(k2)
                k2 = link.mark(nc.vector.tensor_copy(qp[:, s2, 0, :], q[:]))
            if behind:
                link.until(k1)
                k1 = link.mark(nc.vector.tensor_tensor(recw[:, 1, :], recw[:, 1, :], Rb[:, W, :], ALU.mult))
            if behind2:
                link.until(k2)
                k2 = link.mark(nc.vector.tensor_tensor(r[:], q[:], qp[:, s2, 0, :], ALU.subtract))
            if behind:
                link.until(k1)
                for m in range(2):
                    om = o.rearrange("p (j m r) e -> p m j r e", j=4, m=2)[:, m, :, :, 0:16]
                    rm = recw[:, 1, :].rearrange("p (j m r) -> p m j r", j=4, m=2)[:, m].unsqueeze(3).to_broadcast([P, 4, 2, 16])
                    am = att[:, m * P:(m + 1) * P].rearrange("p (j r e) -> p j r e", j=4, r=2)
                    ins = nc.vector.tensor_tensor(am, om, rm, ALU.mult)
                ins.then_inc(att_ready, 1)
            if behind2:
                link.until(k2)
                k2 = link.mark(nc.vector.tensor_copy(qp[:, s2, 1, :], r[:]))
            if here:
                dve.wait_ge(e1_ready, u + 1)
                nc.vector.tensor_reduce(R[:, Z, :], e1[:], AX_X, ALU.add).then_inc(z_ready, 1)
            if behind2:
                link.until(k2)
                nc.vector.tensor_tensor(qp[:, s2, 2, :], r[:], qp[:, s2, 1, :], ALU.subtract).then_inc(qp_ready, 1)
            if here:
                dve.wait_ge(z_ready, u + 1)
                nc.vector.reciprocal(R[:, RZ, :], R[:, Z, :]).then_inc(rz_ready, 1)
            if behind:
                dve.wait_ge(y_done, u)
                dve.wait_ge(xb_ready, u)
                if steady or u >= 3:
                    dve.wait_ge(x1_stored[n2], over(2, -1) * 16)
                k1 = link.mark(nc.vector.tensor_tensor(x1[:, n2, :], ps_o[:, 0:D], x[:, (s - 1) % 4, :], ALU.add))
            if ahead:
                dve.wait_ge(v_done, u + 2)
                if steady or u >= 1:
                    dve.wait_ge(o_done, u)
            for par in range(2):
                for b in range(2):
                    if ahead:
                        rr = slice(64 * par, 64 * par + 64)
                        ov = vblk[rr, n2, b, :, par, 0:16].rearrange("p (j m) e -> p m j e", m=2)
                        i0 = ps_v[rr, b, :].rearrange("p (m j r e) -> p m j r e", m=2, j=4, r=2)[:, :, :, par]
                        i1 = bv[rr, :].rearrange("p (m j r e) -> p m j r e", m=2, j=4, r=2)[:, :, :, par]
                        ins = nc.vector.tensor_tensor(ov, i0, i1, ALU.add)
                        if (par, b) == (1, 1):
                            ins.then_inc(v_ready, 1)
                    if behind and (par, b) == (0, 0):
                        link.until(k1)
                        nc.vector.bn_stats(stats2[:, n2, 0:6], x1[:, n2, :]).then_inc(x1_ready, 1)
                    if behind and (par, b) == (0, 1):
                        dve.wait_ge(x1_ready, u)
                        dve.sem_inc(waits_met, 1)
                        k1 = link.mark(nc.vector.bn_aggr(stats2[:, n2, 6:8], stats2[:, n2, 0:6]))
                    if behind and (par, b) == (1, 1):
                        link.until(k1)
                        nc.vector.tensor_scalar(ln2[:, n2, 0:1], stats2[:, n2, 7:8], EPS, None, ALU.add).then_inc(var2_ready, 1)

        PER = 2 + 3 + 3 + 3 + 4 + 2
        run_steps(dve, step, -2, N_STEADY, TILES + 2, 4, link, 4 * PER)


def phase2(nc, t, st, sbt, pst, sem, g):
    B, S, D = g["B"], g["S"], g["D"]
    HX = 8
    ident16, gamma = g["ident16"], g["gamma"]
    x1_dram, x2_dram, qp_dram, kp_dram, o_dram = (g[k] for k in ("x1_dram", "x2_dram", "qp_dram", "kp_dram", "o_dram"))
    SCALE = 1.0 / math.sqrt(S // HX)
    PAIRS = B // 2

    def sb(name, shape, dt=F32):
        return sbt(st, name, shape, dt)

    def sm(name):
        return sem(st, name)

    ks, qs = g["ks"], g["qs"]
    vT = sb("vT", [P, 4, 2, 64])
    vaug = g["vaug"]
    mx = sb("mx", [P, 2, 16])
    mp = sb("mp", [P, 2, 48], BF16)
    mr = sb("mr", [P, 2, 16])
    mT = sb("mT", [48, 2, P], BF16)
    pr = sb("pr", [P, 2, 4, 2, D])
    o_sb = sb("o_sb", [P, 2, 2, D])
    num = sb("num", [P, 2, D])
    den = sb("den", [P, 2, D])
    r0 = sb("r0", [P, D])
    ra = sb("ra", [P, D])
    lnd = sb("lnd", [P, D])
    ones, twos, gammas = sb("ones", [P, D]), sb("twos", [P, D]), sb("gammas", [P, D])
    x1 = sb("x1_in", [P, 2, D])
    x2 = sb("x2_tile", [P, 2, D])

    ps_s = pst(st, "ps2_s", [P, 2, 2, D])
    ps_t = pst(st, "ps2_t", [P, 2, 2, 2, D])
    ps_o = pst(st, "ps2_o", [P, 2, D])
    ps_m = pst(st, "ps2_m", [P, P * 4], BF16)

    fills_done = sm("fills_done")
    act_own, pool_own, r0_ready = sm("act2_own"), sm("pool2_own"), sm("r0_ready")
    dve_own = sm("dve2_own")
    waits_met, sp_waits_met = sm("waits2_met"), sm("sp_waits_met")
    kq_loaded = [sm(f"kq_loaded{i}") for i in range(4)]
    v_loaded = [sm(f"v_loaded{i}") for i in range(2)]
    m_loaded = [sm(f"m_loaded{i}") for i in range(4)]
    x1_loaded = [sm(f"x1_loaded{i}") for i in range(2)]
    o_moved = [sm(f"o_moved{i}") for i in range(4)]
    o_stored = [sm(f"o_stored{i}") for i in range(2)]
    x2_stored = [sm(f"x2_stored{i}") for i in range(2)]
    s_ready, max_done, mp_ready, mT_done, mT_ready = sm("s2_ready"), sm("max2_done"), sm("mp_ready"), sm("mT_done"), sm("mT_ready")
    st_ready, exp_done, pv_done, o_ready = sm("st_ready"), sm("exp_done"), sm("pv_done"), sm("o_ready")
    vaug_ready, x2_ready = sm("vaug_ready"), sm("x2_ready")
    STEADY = (7, B - 5)

    def slot_value(b, slot, slots, steady, each):
        return (b // slots + 1) * each if not steady else (b - slot) * (each // slots) + each

    block = st.enter_context(nc.Block())

    @block.sync
    def _(sp):
        def load(b, s):
            k, q = kp_dram[b].rearrange("i d h c -> (i d) (h c)"), qp_dram[b].rearrange("d i h c -> (d i) (h c)")
            ki = list(k.ap)
            sp.dma_start(ks[0:72, s, :, :].rearrange("p h c -> p (h c)"),
                         bass.AP(k.tensor, k.offset, [ki[0], [0, 3], ki[1]])).then_inc(kq_loaded[s], 16)
            sp.dma_start(qs[0:72, s, :, :].rearrange("p h c -> p (h c)"),
                         bass.AP(q.tensor, q.offset, [[0, 3]] + list(q.ap))).then_inc(kq_loaded[s], 16)

        def load_v(b, p):
            for i in range(2):
                sp.dma_start(vT[:, 2 * p + i, :, :], t["ctxT"][b + i].rearrange("(c l) r -> l c r", c=2))\
                    .then_inc(v_loaded[p], 16)

        def step(b, s, steady, over):
            if steady or 0 <= b < B - 3:
                if steady or b >= 1:
                    sp.wait_ge(st_ready, b * 4)
                load(b + 3, (s + 3) % 4)
            if s % 2 == 1 and (steady or 1 <= b < B - 4):
                sp.wait_ge(vaug_ready, b + 1)
                load_v(b + 3, ((s + 3) // 2) % 2)
            if s % 2 == 1 and (steady or 0 <= b < B):
                p = (s // 2) % 2
                if steady or b >= 5:
                    sp.wait_ge(x2_ready, over(2, -3))
                sp.dma_start(x1[:, p, :], x1_dram[bass.ds((b - 1) * S, P), :]).then_inc(x1_loaded[p], 16)
            if steady or 2 <= b < B + 2:
                v, sv = b - 2, s % 2
                pp = (((s - 2) % 4) // 2) % 2
                sp.wait_ge(o_stored[sv], over(2) * 16)
                if steady or b >= 6:
                    sp.sem_inc(sp_waits_met, 1)
                    sp.wait_ge(x2_ready, over(2, -4))
                src = o_dram[v].rearrange("f p c -> (f p) c").rearrange("(j w r) c -> w j r c", j=8, w=4)
                sp.dma_start(num[64 * sv:64 * sv + 64, pp, :], src[0]).then_inc(o_moved[2 * pp + sv], 16)
                sp.dma_start(den[64 * sv:64 * sv + 64, pp, :], src[1]).then_inc(o_moved[2 * pp + sv], 16)
            if steady or 0 <= b + 1 < B:
                n = (s + 1) % 4
                sp.wait_ge(mT_ready, b + 2)
                sp.dma_start(qs[96:99, n, :, :].rearrange("p h (c q) -> p (h c) q", c=2),
                             mT[:, n % 2, :]).then_inc(m_loaded[n], 16)
            if s % 2 == 1 and (steady or 3 <= b < B + 2):
                store(b - 2, over(2, -3), (((s - 5) % 4) // 2) % 2) if (steady or b >= 5) else None

        def store(b, count, p):
            sp.wait_ge(x2_ready, count)
            sp.dma_start(x2_dram[bass.ds((b - 3) * S, P), :], x2[:, p, :]).then_inc(x2_stored[p], 16)

        for b in range(3):
            load(b, b)
        load_v(0, 0)
        load_v(2, 1)
        run_steps(sp, step, -1, STEADY, B + 2, 4)
        store(B + 1, PAIRS, (PAIRS - 1) % 2)
        for i in range(2):
            sp.wait_ge(x2_stored[i], 16 * (PAIRS // 2))

    @block.tensor
    def _(pe):
        def weigh(b, s, hf, steady):
            n = 2 * b + hf
            pe.wait_ge(exp_done, 2 * n + 2)
            if hf == 0:
                pe.wait_ge(vaug_ready, b + 1)
                if steady or b >= 1:
                    pe.wait_ge(o_ready, b)
            for lc in range(2):
                for j in range(4):
                    last = nc.tensor.matmul(ps_o[32 * j:32 * j + 32, hf, :], vaug[:, s, lc, 4 * hf + j, :],
                                            pr[:, hf, j, lc, :], start=lc == 0, stop=lc == 1)
            last.then_inc(pv_done, 1)

        def step(b, s, steady, over):
            here, ahead = (steady or 0 <= b < B), (steady or b + 2 < B)
            if here:
                pe.wait_ge(m_loaded[s], slot_value(b, s, 4, steady, 16))
            if ahead:
                sa = (s + 2) % 4
                pe.wait_ge(kq_loaded[sa], slot_value(b + 2, sa, 4, steady, 32))
            for p in range(4):
                if here:
                    u = 4 * b + p
                    if steady or u >= 2:
                        pe.wait_ge(exp_done, u - 1)
                    for h in (2 * p, 2 * p + 1):
                        for lc in range(2):
                            last = nc.tensor.matmul(ps_t[:, p % 2, h % 2, lc, :], ks[:, s, h, lc * P:(lc + 1) * P],
                                                    qs[:, s, h, :], start=True, stop=True)
                    last.then_inc(st_ready, 1)
                if ahead:
                    for h in (2 * p, 2 * p + 1):
                        v = 8 * (b + 2) + h
                        if steady or v >= 2:
                            pe.wait_ge(max_done, v - 1)
                        for c in range(2):
                            last = nc.tensor.matmul(ps_s[:, h % 2, c, :], qs[0:96, sa, h, c * P:(c + 1) * P],
                                                    ks[0:96, sa, h, :], start=True, stop=True)
                        last.then_inc(s_ready, 1)
                if p == 0 and (steady or 1 <= b <= B):
                    weigh(b - 1, (s - 1) % 4, 1, steady)
                if p == 1 and (steady or 0 <= b + 1 < B):
                    n = (s + 1) % 2
                    pe.wait_ge(mp_ready, b + 2)
                    if steady or b >= 0:
                        pe.wait_ge(mT_ready, b + 1)
                    pe.sem_inc(waits_met, 1)
                    nc.tensor.transpose(ps_m[0:48, 0:P], mp[:, n, :], ident16[:]).then_inc(mT_done, 1)
                if p == 3 and here:
                    weigh(b, s, 0, steady)

        run_steps(pe, step, -2, STEADY, B + 1, 4)

    @block.scalar
    def _(act):
        link = Link(act, act_own)
        act.preload_act_table_set("natural_log_exp_and_others")

        def step(b, s, steady, over):
            here = steady or 0 <= b < B
            for p in range(4):
                if here:
                    u = 4 * b + p
                    act.wait_ge(st_ready, u + 1)
                    if steady or 2 * b + p // 2 >= 2:
                        act.wait_ge(pv_done, 2 * b + p // 2 - 1)
                    nc.scalar.activation(pr[:, p // 2, 2 * (p % 2):2 * (p % 2) + 2, :, :], ps_t[:, p % 2, :, :, :],
                                         ACT.Exp, scale=SCALE).then_inc(exp_done, 1)
                if p == 1 and (steady or 0 <= b + 1 < B):
                    n = (s + 1) % 2
                    act.wait_ge(mT_done, b + 2)
                    if steady or b >= 1:
                        m = (s - 1) % 4
                        act.wait_ge(m_loaded[m], slot_value(b - 1, m, 4, steady, 16))
                    nc.scalar.activation(mT[:, n, :], ps_m[0:48, 0:P], ACT.Copy).then_inc(mT_ready, 1)
                if p == 1 and (steady or 1 <= b <= B):
                    v, sv = b - 1, (s - 1) % 2
                    act.wait_ge(pv_done, 2 * v + 2)
                    if steady or v >= 2:
                        act.wait_ge(o_stored[sv], over(2, -1) * 16)
                    nc.scalar.activation(o_sb[:, sv, :, :], ps_o[:], ACT.Copy).then_inc(o_ready, 1)
                    act.wait_ge(o_ready, v + 1)
                    act.dma_start(o_dram[v].rearrange("f p c -> p f c"), o_sb[:, sv, :, :]).then_inc(o_stored[sv], 16)
            if s % 2 == 1 and (steady or 3 <= b < B + 2):
                p = (((s - 3) % 4) // 2) % 2
                for bb in range(2):
                    act.wait_ge(o_moved[2 * p + bb], over(4, 1) * 32)
                link(nc.scalar.activation(lnd[:], den[:, p, :], ACT.Ln))
                if steady or b >= 5:
                    act.wait_ge(x2_ready, over(2, -3))
                nc.scalar.activation(r0[:], lnd[:], ACT.Exp, scale=-1.0).then_inc(r0_ready, 1)
                act.wait_ge(r0_ready, over(2, -1))

        run_steps(act, step, -1, STEADY, B + 2, 4, link, 2)

    @block.gpsimd
    def _(pool):
        for tile, v in ((ones, 1.0), (twos, 2.0)):
            nc.gpsimd.memset(tile[:], v).then_inc(fills_done, 1)
        nc.gpsimd.tensor_copy(gammas[:], gamma[:, 0:1].to_broadcast([P, D])).then_inc(fills_done, 1)
        pool.wait_ge(fills_done, 3)

        link = Link(pool, pool_own)
        tt = nc.gpsimd.tensor_tensor

        def step(b, s, steady, over):
            if steady or 0 <= b + 1 < B:
                a = (s + 1) % 4
                pool.wait_ge(v_loaded[a // 2], over(4, 1) * 32 + 32)
                if steady or b >= 3:
                    pool.wait_ge(pv_done, 2 * (b - 3) + 2)
                tt(vaug[:, a, :, :, 0:8], vT[:, a, :, :].rearrange("p c (h d) -> p c h d", h=HX),
                   ones[:, 0:128].rearrange("p (c h d) -> p c h d", c=2, h=HX), ALU.mult).then_inc(vaug_ready, 1)
            if s % 2 == 1 and (steady or 3 <= b < B + 2):
                p = (((s - 3) % 4) // 2) % 2
                pool.wait_ge(r0_ready, over(2, -1))
                pool.wait_ge(x1_loaded[p], over(4, 1) * 16)
                link(tt(ra[:], den[:, p, :], r0[:], ALU.mult))
                link(tt(ra[:], twos[:], ra[:], ALU.subtract))
                link(tt(ra[:], ra[:], r0[:], ALU.mult))
                link(tt(ra[:], ra[:], num[:, p, :], ALU.mult))
                link(tt(ra[:], ra[:], gammas[:], ALU.mult))
                if steady or b >= 7:
                    pool.wait_ge(x2_stored[p], over(4, -3) * 16)
                tt(x2[:, p, :], ra[:], x1[:, p, :], ALU.add).then_inc(x2_ready, 1)
                pool.wait_ge(x2_ready, over(2, -1))

        run_steps(pool, step, -2, STEADY, B + 2, 4, link, 2 * 5)

    @block.vector
    def _(dve):
        link = Link(dve, dve_own)

        def step(b, s, steady, over):
            if steady or b + 2 < B:
                n = (s + 2) % 2
                for h in range(HX):
                    dve.wait_ge(s_ready, 8 * (b + 2) + h + 1)
                    nc.vector.tensor_reduce(mx[:, n, 2 * h:2 * h + 2], ps_s[:, h % 2, :, :], AX_X, ALU.max).then_inc(max_done, 1)
                dve.wait_ge(max_done, 8 * (b + 2) + 8)
                if steady or b >= 0:
                    dve.wait_ge(mT_done, b + 1)
                part = [mp[:, n, 16 * i:16 * i + 16] for i in range(3)]
                link(nc.vector.tensor_scalar(part[0], mx[:, n, :], -1.0, None, ALU.mult))
                link(nc.vector.scalar_tensor_tensor(out=mr[:, 0, :], in0=mx[:, n, :], scalar=-1.0, in1=part[0],
                                                    op0=ALU.mult, op1=ALU.subtract))
                link(nc.vector.tensor_copy(part[1], mr[:, 0, :]))
                nc.vector.tensor_tensor(part[2], mr[:, 0, :], part[1], ALU.subtract).then_inc(mp_ready, 1)

        run_steps(dve, step, -2, STEADY, B - 2, 4, link, 4 * 3)


def phase3(nc, t, st, sbt, pst, sem, g):
    D = g["D"]
    E, TOK, BL = 8, 512, 4
    T = g["B"] * g["S"] // TOK
    ident, w1, w2, w3, rw, iota8 = (g[k] for k in ("ident", "w1", "w2", "w3", "rw", "iota8"))
    x2_dram, out, ffn_in = g["x2_dram"], g["out"], g["ffn_in"]

    def sb(name, shape, dt=F32):
        return sbt(st, name, shape, dt)

    def sm(name):
        return sem(st, name)

    x = sb("x2_in", [P, 2, BL, D])
    xn = sb("xn", [P, BL, D])
    xnT = sb("xnT", [P, 2, 2, TOK])
    stats = sb("stats3", [P, BL, 6])
    mv = sb("mv3", [P, BL, 2])
    v3 = sb("v3", [P, 4, BL])
    lg = sb("logits", [P, BL, E])
    top = sb("top", [P, BL, 8])
    idx = sb("idx", [P, BL, 8], U32)
    idf = sb("idf", [P, BL, 8])
    dl = sb("dl", [P, 3, BL])
    wt = sb("wt", [P, 2, BL, E])
    wtb = sb("wtb", [P, BL, E])
    sg = sb("sg", [P, 2, TOK])
    hh = sb("hh", [P, 2, TOK])
    acc = sb("acc", [P, 2, BL, D])

    ps_g = pst(st, "ps_g", [P, 2, TOK])
    ps_v = pst(st, "ps3_v", [P, 2, TOK])
    ps_y = pst(st, "ps_y", [P, BL, D])
    ps_x = pst(st, "ps3_x", [P, TOK])
    ps_l = pst(st, "ps_l", [P, 512])

    x_loaded = [sm(f"x2_loaded{i}") for i in range(2)]
    stored = [sm(f"out_stored{i}") for i in range(2)]
    own = sm("dve3_own")
    waits_met = sm("waits3_met")
    act_own = sm("act3_own")
    var_ready, rs_ready, xn_ready = sm("var3_ready"), sm("rs3_ready"), sm("xn_ready")
    xT_done, xT_ready, lg_done, dl_ready, tw_ready, wt_ready = (sm(n) for n in (
        "xT3_done", "xT3_ready", "lg_done", "dl_ready", "tw_ready", "wt_ready"))
    gv_done, sg_ready, hh_ready, y_done, acc_done = (sm(n) for n in ("gv_done", "sg_ready", "hh_ready", "y3_done", "acc_done"))
    STEADY = (1, T - 1)

    block = st.enter_context(nc.Block())

    @block.sync
    def _(sp):
        def rows(ap, k):
            return ap[bass.ds(k * TOK, TOK), :].rearrange("(n p) d -> p n d", p=P)

        def step(k, s, steady, over):
            if steady or k + 1 < T:
                n = (s + 1) % 2
                if steady or k >= 1:
                    sp.wait_ge(acc_done, 8 * (k - 1) + 1)
                sp.dma_start(x[:, n, :, :], rows(x2_dram, k + 1)).then_inc(x_loaded[n], 16)
            if steady or k >= 1:
                sp.wait_ge(acc_done, 8 * k)
                sp.dma_start(rows(out, k - 1), acc[:, (s - 1) % 2, :, :]).then_inc(stored[(s - 1) % 2], 16)

        run_steps(sp, step, -1, STEADY, T + 1, 2)
        for i in range(2):
            sp.wait_ge(stored[i], 16 * (T // 2))

    @block.tensor
    def _(pe):
        def prep(k, s):
            pe.wait_ge(xn_ready, k + 1)
            for kc in range(2):
                if kc == 1:
                    pe.wait_ge(xT_ready, 2 * k + 1)
                for n in range(BL):
                    last = nc.tensor.transpose(ps_x[:, n * P:(n + 1) * P], xn[:, n, kc * P:(kc + 1) * P], ident[:])
                last.then_inc(xT_done, 1)

        def logits(k, s, steady):
            pe.wait_ge(xT_ready, 2 * k + 2)
            for n in range(BL):
                for kc in range(2):
                    last = nc.tensor.matmul(ps_l[:, n * E:(n + 1) * E], xnT[:, s, kc, n * P:(n + 1) * P], rw[:, kc, :],
                                            start=kc == 0, stop=kc == 1)
            last.then_inc(lg_done, 1)

        def expert_out(k, e, steady):
            n = 8 * k + e
            pe.wait_ge(hh_ready, n + 1)
            if steady or n >= 1:
                pe.wait_ge(acc_done, n)
            for bl in range(BL):
                last = nc.tensor.matmul(ps_y[:, bl, :], hh[:, e % 2, bl * P:(bl + 1) * P], w3[:, e, :],
                                        start=True, stop=True)
            last.then_inc(y_done, 1)

        def step(k, s, steady, over):
            here, ahead = (steady or 0 <= k < T), (steady or k + 1 < T)
            for e in range(E):
                if here:
                    n = 8 * k + e
                    if steady or n >= 2:
                        pe.wait_ge(hh_ready, n - 1)
                    if e == 0:
                        pe.wait_ge(xT_ready, 2 * k + 2)
                    for ps, w in ((ps_g, w1), (ps_v, w2)):
                        for kc in range(2):
                            last = nc.tensor.matmul(ps[:, e % 2, :], w[:, e, kc, :], xnT[:, s, kc, :],
                                                    start=kc == 0, stop=kc == 1)
                    last.then_inc(gv_done, 1)
                if e == 0 and (steady or k >= 1):
                    expert_out(k - 1, E - 1, steady)
                if here and e >= 1:
                    expert_out(k, e - 1, steady)
                if ahead and e == 4:
                    prep(k + 1, (s + 1) % 2)
                if ahead and e == 6:
                    logits(k + 1, (s + 1) % 2, steady)

        pe.wait_ge(ffn_in, 5 * 16)
        run_steps(pe, step, -1, STEADY, T + 1, 2)

    @block.scalar
    def _(act):
        link = Link(act, act_own)

        def step(k, s, steady, over):
            here, ahead = (steady or 0 <= k < T), (steady or k + 1 < T)
            n2 = (s + 1) % 2
            for e in range(E):
                if here:
                    n = 8 * k + e
                    act.wait_ge(gv_done, n + 1)
                    if steady or n >= 2:
                        act.wait_ge(hh_ready, n - 1)
                    nc.scalar.activation(sg[:, e % 2, :], ps_g[:, e % 2, :], ACT.Sigmoid).then_inc(sg_ready, 1)
                if ahead and e == 2:
                    act.preload_act_table_set("natural_log_exp_and_others")
                    act.wait_ge(var_ready, k + 2)
                    link(nc.scalar.activation(v3[:, 1, :], v3[:, 0, :], ACT.Ln))
                    nc.scalar.activation(v3[:, 2, :], v3[:, 1, :], ACT.Exp, scale=-0.5).then_inc(rs_ready, 1)
                if ahead and e == 4:
                    for kc in range(2):
                        act.wait_ge(xT_done, 2 * (k + 1) + kc + 1)
                        if kc == 0 and (steady or k >= 1):
                            act.wait_ge(gv_done, 8 * k)
                        nc.scalar.activation(xnT[:, n2, kc, :], ps_x[:], ACT.Copy).then_inc(xT_ready, 1)
                if ahead and e == 6:
                    act.wait_ge(dl_ready, k + 2)
                    nc.scalar.activation(dl[:, 1, :], dl[:, 0, :], ACT.Sigmoid).then_inc(tw_ready, 1)
                    nc.scalar.activation(dl[:, 2, :], dl[:, 0, :], ACT.Sigmoid, scale=-1.0).then_inc(tw_ready, 1)

        run_steps(act, step, -1, STEADY, T, 2, link, 2)

    @block.vector
    def _(dve):
        link = Link(dve, own)

        def add_expert(k, s, e, steady):
            n = 8 * k + e
            dve.wait_ge(y_done, n + 1)
            if e == 0:
                dve.wait_ge(wt_ready, k + 1)
                if steady or k >= 2:
                    dve.wait_ge(stored[s], (k // 2) * 16)
            else:
                dve.wait_ge(acc_done, n)
            for bl in range(BL):
                before = x[:, s, bl, :] if e == 0 else acc[:, s, bl, :]
                ins = nc.vector.scalar_tensor_tensor(out=acc[:, s, bl, :], in0=ps_y[:, bl, :],
                                                     scalar=wt[:, s, bl, e:e + 1], in1=before,
                                                     op0=ALU.mult, op1=ALU.add)
                if bl < BL - 1:
                    link(ins)
            ins.then_inc(acc_done, 1)

        def step(k, s, steady, over):
            here, ahead = (steady or 0 <= k < T), (steady or k + 1 < T)
            n2 = (s + 1) % 2
            for e in range(E):
                if here:
                    n = 8 * k + e
                    dve.wait_ge(sg_ready, n + 1)
                    if steady or n >= 2:
                        dve.wait_ge(y_done, n - 1)
                    link(nc.vector.tensor_tensor(hh[:, e % 2, :], sg[:, e % 2, :], ps_g[:, e % 2, :], ALU.mult))
                    nc.vector.tensor_tensor(hh[:, e % 2, :], hh[:, e % 2, :], ps_v[:, e % 2, :], ALU.mult).then_inc(hh_ready, 1)
                if e == 0 and (steady or k >= 1):
                    add_expert(k - 1, (s - 1) % 2, E - 1, steady)
                if here and e >= 1:
                    add_expert(k, s, e - 1, steady)
                if ahead and e == 1:
                    dve.wait_ge(x_loaded[n2], ((k + 1) // 2 + 1) * 16 if not steady else (k + 1 - n2) * 8 + 16)
                    for n in range(BL):
                        link(nc.vector.bn_stats(stats[:, n, :], x[:, n2, n, :]))
                    for n in range(BL):
                        dve.sem_inc(waits_met, 1)
                        link(nc.vector.bn_aggr(mv[:, n, :], stats[:, n, :]))
                    nc.vector.tensor_scalar(v3[:, 0, :], mv[:, :, 1], EPS, None, ALU.add).then_inc(var_ready, 1)
                if ahead and e == 3:
                    dve.wait_ge(rs_ready, k + 2)
                    dve.wait_ge(var_ready, k + 2)
                    link(nc.vector.tensor_tensor(v3[:, 3, :], v3[:, 2, :], v3[:, 2, :], ALU.mult))
                    link(nc.vector.tensor_tensor(v3[:, 3, :], v3[:, 3, :], v3[:, 0, :], ALU.mult))
                    link(nc.vector.tensor_scalar(v3[:, 3, :], v3[:, 3, :], -0.5, 1.5, ALU.mult, ALU.add))
                    link(nc.vector.tensor_tensor(v3[:, 3, :], v3[:, 3, :], v3[:, 2, :], ALU.mult))
                    if steady or k >= 0:
                        dve.wait_ge(xT_done, 2 * k + 2)
                    for n in range(BL):
                        ins = nc.vector.tensor_scalar(xn[:, n, :], x[:, n2, n, :], mv[:, n, 0:1], v3[:, 3, n:n + 1],
                                                      ALU.subtract, ALU.mult)
                        if n < BL - 1:
                            link(ins)
                    ins.then_inc(xn_ready, 1)
                if ahead and e == 6:
                    dve.wait_ge(lg_done, k + 2)
                    link(nc.vector.tensor_copy(lg[:], ps_l[:, 0:BL * E].rearrange("p (n e) -> p n e", n=BL)))
                    for n in range(BL):
                        dve.sem_inc(waits_met, 1)
                        link(nc.vector.max(top[:, n, :], lg[:, n, :]))
                    for n in range(BL):
                        dve.sem_inc(waits_met, 1)
                        link(nc.vector.max_index(idx[:, n, :], top[:, n, :], lg[:, n, :]))
                    nc.vector.tensor_tensor(dl[:, 0, :], top[:, :, 0], top[:, :, 1], ALU.subtract).then_inc(dl_ready, 1)
                    link(nc.vector.tensor_copy(idf[:], idx[:]))
                if ahead and e == 7:
                    dve.wait_ge(tw_ready, 2 * (k + 2))
                    for n in range(BL):
                        for j, dst in ((0, wt[:, n2, n, :]), (1, wtb[:, n, :])):
                            link(nc.vector.tensor_scalar(dst, iota8[:], idf[:, n, j:j + 1], dl[:, 1 + j, n:n + 1],
                                                         ALU.is_equal, ALU.mult))
                    nc.vector.tensor_tensor(wt[:, n2, :, :], wt[:, n2, :, :], wtb[:], ALU.add).then_inc(wt_ready, 1)

        dve.wait_ge(ffn_in, 5 * 16)
        run_steps(dve, step, -1, STEADY, T + 1, 2, link, 2 * (8 * 4 + 8 + 4 + 3 + 1 + 8 + 1 + 8))


def kernel(**inputs):
    import numpy as np
    import concourse.bacc as bacc
    from concourse.bass_utils import run_bass_kernel_spmd

    a = {k: np.asarray(v) for k, v in inputs.items()}
    B, S, D = a["x"].shape
    cst = np.zeros((P, 11), np.float32)
    lane = np.arange(P)
    cst[:, 0] = (lane // 16) % 2 == 0
    cst[:, 1] = (lane // 16) % 2 == 1
    for h in range(8):
        cst[:, 2 + h] = lane // 16 == h
    cst[:, 10] = (lane % S) / S
    arrays = {
        "x": a["x"], "ctx": a["ctx_2048"], "ctxT": a["ctx_2048"].transpose(0, 2, 1),
        "wqT": a["L0_attn_Wq"].T, "wkT": a["L0_attn_Wk"].T, "wvT": a["L0_attn_Wv"].T, "woT": a["L0_attn_Wo"].T,
        "bq": a["L0_attn_bq"], "bk": a["L0_attn_bk"], "bv": a["L0_attn_bv"], "bo": a["L0_attn_bo"],
        "truth": a["L0_attn_truth_gate"], "balance": a["L0_attn_balance_gate"], "order": a["L0_attn_order_gate"],
        "justice": a["L0_attn_justice_gate"], "harmony": a["L0_attn_harmony_gate"],
        "gamma": a["L0_xattn_gamma"].reshape(1), "rwT": a["L0_ffn_router_w"].T,
        "w1": a["L0_ffn_w1"], "w2": a["L0_ffn_w2"], "w3": a["L0_ffn_w3"],
        "ident": np.eye(P, dtype=np.float32), "cst": cst,
        "iota8": np.tile(np.arange(8, dtype=np.float32), (P, 1)),
    }
    nc = bacc.Bacc("TRN2", target_bir_lowering=False, num_devices=1)
    feeds, t = {}, {}
    for name, v in arrays.items():
        v = np.ascontiguousarray(v)
        feeds["in_" + name] = v
        t[name] = nc.dram_tensor("in_" + name, v.shape, mybir.dt.from_np(v.dtype), kind="ExternalInput").ap()
    t["out"] = nc.dram_tensor("out_x", (B, S, D), F32, kind="ExternalOutput").ap()
    decoder_kernel(nc, t)
    r = run_bass_kernel_spmd(nc, [feeds], core_ids=[0])
    return r.results[0]["out_x"]
```
